# Optimizing a Trainium2 kernel written in Bass

```python
import numpy as np
import jax
import jax.numpy as jnp

def _softmax(x, axis=-1):
    return jax.nn.softmax(x, axis=axis)

def _gelu(x):
    return jax.nn.gelu(x, approximate=True)

def _silu(x):
    return jax.nn.silu(x)

def _sigmoid(x):
    return jax.nn.sigmoid(x)

def _layernorm(x, axis=-1, eps=1e-05):
    m = jnp.mean(x, axis=axis, keepdims=True)
    v = jnp.var(x, axis=axis, keepdims=True)
    return (x - m) / jnp.sqrt(v + eps)

def _scatter_add(tgt, idx, src, axis=0):
    return tgt.at[idx].add(src)

def _segment_sum(src, seg, n):
    return jax.ops.segment_sum(src, seg, n)
kernel_name = 'mk_decoder_preln_d4_seqx_r4_7c845e'

def setup_inputs(seed: int=0):
    np.random.seed(seed)
    _w = jnp.asarray

    def _rec_inputs():
        import jax
        import jax.numpy as jnp
        _rk = jax.random.key(seed)
        x = -0.0002928 + 1 * jax.random.normal(jax.random.fold_in(_rk, 1), (16, 128, 256), jnp.float32)
        _lenS = 128 - jax.random.randint(jax.random.fold_in(_rk, 7), (16,), 0, max(1, 128 // 4) + 1, jnp.int32)
        _lenS2 = 128 - jax.random.randint(jax.random.fold_in(_rk, 8), (16,), 0, max(1, 128 // 4) + 1, jnp.int32)
        _ctx_1024P = jax.random.normal(jax.random.fold_in(_rk, 11), (16, 16, 256), jnp.float32)
        _ctx_1024c = jax.random.dirichlet(jax.random.fold_in(_rk, 511), 0.3 * jnp.ones((16,), jnp.float32), (16, 128))
        _ctx_1024t = jnp.einsum('bsk,bkd->bsd', _ctx_1024c, _ctx_1024P)
        _ctx_1024t = _ctx_1024t * jax.lax.rsqrt(jnp.mean(jnp.square(_ctx_1024t)) + 1e-12) * 0.953939
        ctx_1024 = -1.39393e-06 + 0.999914 * (_ctx_1024t + 0.3 * jax.random.normal(jax.random.fold_in(_rk, 611), (16, 128, 256), jnp.float32))
        _validS = jnp.arange(128)[None, :] < _lenS[:, None]
        _validS2 = jnp.arange(128)[None, :] < _lenS2[:, None]
        _causal = jnp.tril(jnp.ones((128, 128), dtype=bool))
        mask_BxS2_bf1 = jnp.ones((16, 128), dtype=bool)
        mask_BxSxS2_bk0 = jnp.logical_not(jnp.broadcast_to(_validS2[:, None, :], (16, 128, 128)))
        return (x, ctx_1024, mask_BxS2_bf1, mask_BxSxS2_bk0)
    x, ctx_1024, mask_BxS2_bf1, mask_BxSxS2_bk0 = _rec_inputs()

    def _L0_attn_setup():
        import jax, jax.numpy as jnp
        import numpy as np
        NUM_HEADS = 16
        EPS = 1e-06
        CHUNK = 128
        key = jax.random.key(seed)
        ks = jax.random.split(key, 6)
        B, T, E = (4, 512, 256)
        s = 0.02
        x = jax.random.normal(ks[0], (B, T, E), jnp.float32)
        Wq = jax.random.normal(ks[1], (E, E), jnp.float32) * s
        Wk = jax.random.normal(ks[2], (E, E), jnp.float32) * s
        Wv = jax.random.normal(ks[3], (E, E), jnp.float32) * s
        Wp = jax.random.normal(ks[4], (E, E), jnp.float32) * s
        bp = jnp.zeros((E,), jnp.float32)
        return {'x': x, 'Wq': Wq, 'Wk': Wk, 'Wv': Wv, 'Wp': Wp, 'bp': bp}
    _L0_attn_all = _L0_attn_setup()
    _L0_attn_in = {k: v for k, v in _L0_attn_all.items() if k in ('Wq', 'Wk', 'Wv', 'Wp', 'bp')}
    del _L0_attn_all

    def _L0_xattn_setup():
        import jax, jax.numpy as jnp
        import numpy as np
        N_HEADS = 16
        D_MODEL = 256
        HEAD_DIM = D_MODEL // N_HEADS
        MASK_FILL = -100000000.0

        def _split_heads(x):
            B, S, _ = x.shape
            return x.reshape(B, S, N_HEADS, HEAD_DIM).transpose(0, 2, 1, 3)
        key = jax.random.key(seed)
        ks = jax.random.split(key, 12)
        B, L, P = (2, 512, 512)
        s = 1.0 / np.sqrt(D_MODEL).astype(np.float32)
        inp = {'q': jax.random.normal(ks[0], (B, L, D_MODEL), dtype=jnp.float32), 'k': jax.random.normal(ks[1], (B, P, D_MODEL), dtype=jnp.float32), 'v': jax.random.normal(ks[2], (B, P, D_MODEL), dtype=jnp.float32), 'attention_mask': jnp.ones((B, P), dtype=bool), 'Wq': jax.random.normal(ks[3], (D_MODEL, D_MODEL), dtype=jnp.float32) * s, 'bq': jnp.zeros((D_MODEL,), dtype=jnp.float32), 'Wk': jax.random.normal(ks[4], (D_MODEL, D_MODEL), dtype=jnp.float32) * s, 'bk': jnp.zeros((D_MODEL,), dtype=jnp.float32), 'Wv': jax.random.normal(ks[5], (D_MODEL, D_MODEL), dtype=jnp.float32) * s, 'bv': jnp.zeros((D_MODEL,), dtype=jnp.float32), 'Wo': jax.random.normal(ks[6], (D_MODEL, D_MODEL), dtype=jnp.float32) * s, 'bo': jnp.zeros((D_MODEL,), dtype=jnp.float32)}
        return inp
    _L0_xattn_all = _L0_xattn_setup()
    _L0_xattn_in = {k: v for k, v in _L0_xattn_all.items() if k in ('Wq', 'bq', 'Wk', 'bk', 'Wv', 'bv', 'Wo', 'bo')}
    del _L0_xattn_all

    def _L0_ffn_setup():
        import jax, jax.numpy as jnp
        import numpy as np
        from jax import lax
        DIM = 256
        HID = 512
        E = 8
        K = 2
        B, T = (2, 128)
        key = jax.random.key(seed)
        ks = jax.random.split(key, 5)
        scale = 1.0 / np.sqrt(DIM)
        x = jax.random.normal(ks[0], (B, T, DIM), dtype=jnp.float32)
        router_w = jax.random.normal(ks[1], (E, DIM), dtype=jnp.float32) * scale
        w_gate = jax.random.normal(ks[2], (E, HID, DIM), dtype=jnp.float32) * scale
        w_up = jax.random.normal(ks[3], (E, HID, DIM), dtype=jnp.float32) * scale
        w_down = jax.random.normal(ks[4], (E, DIM, HID), dtype=jnp.float32) * (1.0 / np.sqrt(HID))
        return {'x': x, 'router_w': router_w, 'w_gate': w_gate, 'w_up': w_up, 'w_down': w_down}
    _L0_ffn_all = _L0_ffn_setup()
    _L0_ffn_in = {k: v for k, v in _L0_ffn_all.items() if k in ('router_w', 'w_gate', 'w_up', 'w_down')}
    del _L0_ffn_all

    def _L1_attn_setup():
        import jax, jax.numpy as jnp
        import numpy as np
        EPS = 1.1920929e-07

        def rmsnorm(x, w):
            return x * jax.lax.rsqrt(jnp.mean(x * x, axis=-1, keepdims=True) + EPS) * w

        def selective_scan(h, in_w, out_w, A_log, Bp_w, Cp_w, dt_w, dt_b, gate_w):
            B, T, D = h.shape
            SC, ST = A_log.shape
            z = h @ in_w.T
            gate = jax.nn.silu(h @ gate_w.T)
            A = -jnp.exp(A_log)
            Bi = z @ Bp_w.T
            Ci = z @ Cp_w.T
            dt = jax.nn.softplus(z @ dt_w.T + dt_b)
            A_bar = 1.0 + dt[..., None] * A

            def step(state, inp):
                a_bar, dtz_t, b_t, c_t = inp
                state = a_bar * state + dtz_t[:, :, None] * b_t[:, None, :]
                y = jnp.sum(state * c_t[:, None, :], axis=-1)
                return (state, y)
            init = jnp.zeros((B, SC, ST), h.dtype)
            xs = (jnp.swapaxes(A_bar, 0, 1), jnp.swapaxes(dt * z, 0, 1), jnp.swapaxes(Bi, 0, 1), jnp.swapaxes(Ci, 0, 1))
            _, ys = jax.lax.scan(step, init, xs)
            y = jnp.swapaxes(ys, 0, 1) * gate
            return y @ out_w.T
        key = jax.random.key(seed)
        ks = jax.random.split(key, 12)
        D, H, SC, ST = (256, 16, 64, 16)
        B, T = (2, 512)
        s = 0.02
        return {'x': jax.random.normal(ks[0], (B, T, D), jnp.float32), 'qkv_w': jax.random.normal(ks[1], (3 * D, D), jnp.float32) * s, 'o_w': jax.random.normal(ks[2], (D, D), jnp.float32) * s, 'norm1_w': jnp.ones((D,), jnp.float32), 'norm2_w': jnp.ones((D,), jnp.float32), 'in_w': jax.random.normal(ks[3], (SC, D), jnp.float32) * s, 'out_w': jax.random.normal(ks[4], (D, SC), jnp.float32) * s, 'A_log': jax.random.normal(ks[5], (SC, ST), jnp.float32) * 0.1, 'Bp_w': jax.random.normal(ks[6], (ST, SC), jnp.float32) * s, 'Cp_w': jax.random.normal(ks[7], (ST, SC), jnp.float32) * s, 'dt_w': jax.random.normal(ks[8], (SC, SC), jnp.float32) * s, 'dt_b': jnp.full((SC,), -3.0, jnp.float32), 'gate_w': jax.random.normal(ks[9], (SC, D), jnp.float32) * s}
    _L1_attn_all = _L1_attn_setup()
    _L1_attn_in = {k: v for k, v in _L1_attn_all.items() if k in ('qkv_w', 'o_w', 'norm1_w', 'norm2_w', 'in_w', 'out_w', 'A_log', 'Bp_w', 'Cp_w', 'dt_w', 'dt_b', 'gate_w')}
    del _L1_attn_all

    def _L1_xattn_setup():
        import jax, jax.numpy as jnp
        import numpy as np
        from math import sqrt
        B, Q, S, D, H = (2, 512, 512, 256, 16)
        ADIM = D // H
        IEPS = 1e-32

        def sparse_norm(scores, nbias):
            t = jax.nn.relu(scores + nbias[0])
            t = t * t
            return t / (t.sum(-1, keepdims=True) + IEPS)
        key = jax.random.key(seed)
        ks = jax.random.split(key, 7)
        sc = 0.02
        return {'iQ': jax.random.normal(ks[0], (B, Q, D), jnp.float32), 'iK': jax.random.normal(ks[1], (B, S, D), jnp.float32), 'mask': jax.random.randint(ks[2], (B, Q, S), 0, 2) > 0, 'Wq': jax.random.normal(ks[3], (D, D), jnp.float32) * sc, 'Wkv': jax.random.normal(ks[4], (2 * D, D), jnp.float32) * sc, 'Wo': jax.random.normal(ks[5], (D, D), jnp.float32) * sc, 'nbias': jnp.zeros((1,), jnp.float32)}
    _L1_xattn_all = _L1_xattn_setup()
    _L1_xattn_in = {k: v for k, v in _L1_xattn_all.items() if k in ('Wq', 'Wkv', 'Wo', 'nbias')}
    del _L1_xattn_all

    def _L1_ffn_setup():
        import jax, jax.numpy as jnp
        import numpy as np
        B, S, H = (2, 512, 256)
        E_ROUTED = 8
        TOP_K = 2
        I = 512
        key = jax.random.key(seed)
        ks = jax.random.split(key, 9)
        s = 0.02
        return {'x': jax.random.normal(ks[0], (B, S, H), dtype=jnp.float32), 'shared_gate': jax.random.normal(ks[1], (I, H), dtype=jnp.float32) * s, 'shared_up': jax.random.normal(ks[2], (I, H), dtype=jnp.float32) * s, 'shared_down': jax.random.normal(ks[3], (H, I), dtype=jnp.float32) * s, 'gate_w': jax.random.normal(ks[4], (E_ROUTED, H, I), dtype=jnp.float32) * s, 'up_w': jax.random.normal(ks[5], (E_ROUTED, H, I), dtype=jnp.float32) * s, 'down_w': jax.random.normal(ks[6], (E_ROUTED, I, H), dtype=jnp.float32) * s, 'router_w': jax.random.normal(ks[7], (E_ROUTED, H), dtype=jnp.float32) * s, 'routing_bias': jnp.zeros((E_ROUTED,), dtype=jnp.float32)}
    _L1_ffn_all = _L1_ffn_setup()
    _L1_ffn_in = {k: v for k, v in _L1_ffn_all.items() if k in ('shared_gate', 'shared_up', 'shared_down', 'gate_w', 'up_w', 'down_w', 'router_w', 'routing_bias')}
    del _L1_ffn_all

    def _L2_attn_setup():
        import jax, jax.numpy as jnp
        import numpy as np
        HEADS = 16
        DIM_HEAD = 64
        key = jax.random.key(seed)
        ks = jax.random.split(key, 5)
        B, N, D = (4, 512, 256)
        s = 0.02
        return {'x': jax.random.normal(ks[0], (B, N, D), dtype=jnp.float32), 'Wq': jax.random.normal(ks[1], (D, HEADS * DIM_HEAD), dtype=jnp.float32) * s, 'Wk': jax.random.normal(ks[2], (D, HEADS * DIM_HEAD), dtype=jnp.float32) * s, 'Wv': jax.random.normal(ks[3], (D, HEADS * DIM_HEAD), dtype=jnp.float32) * s, 'Wo': jax.random.normal(ks[4], (HEADS * DIM_HEAD, D), dtype=jnp.float32) * s, 'bo': jnp.zeros((D,), dtype=jnp.float32)}
    _L2_attn_all = _L2_attn_setup()
    _L2_attn_in = {k: v for k, v in _L2_attn_all.items() if k in ('Wq', 'Wk', 'Wv', 'Wo', 'bo')}
    del _L2_attn_all

    def _L2_xattn_setup():
        import jax, jax.numpy as jnp
        import numpy as np
        B, S, D = (8, 512, 256)
        key = jax.random.key(seed)
        k1, k2 = jax.random.split(key)
        query = jax.random.normal(k1, (B, S, D), dtype=jnp.float32)
        keys = jax.random.normal(k2, (B, S, D), dtype=jnp.float32)
        return {'query': query, 'keys': keys}
    _L2_xattn_all = _L2_xattn_setup()
    _L2_xattn_in = {k: v for k, v in _L2_xattn_all.items() if k in ()}
    del _L2_xattn_all

    def _L2_ffn_setup():
        import jax, jax.numpy as jnp
        import numpy as np
        B, S, D_MODEL, D_FF = (4, 512, 256, 1024)

        def _quantum_transform(hidden, theta, w_real, w_imag):
            imag = w_imag * jnp.sin(theta + hidden * 0.1)
            quantum_phase = jnp.cos(theta) * w_real + jnp.sin(theta) * w_imag
            return hidden + quantum_phase * imag * 0.1
        key = jax.random.key(seed)
        ks = jax.random.split(key, 8)
        return {'x': jax.random.normal(ks[0], (B, S, D_MODEL), dtype=jnp.float32), 'W1': jax.random.normal(ks[1], (D_MODEL, D_FF), dtype=jnp.float32) * (1.0 / np.sqrt(D_MODEL)), 'b1': jnp.zeros((D_FF,), dtype=jnp.float32), 'quantum_phases': jax.random.normal(ks[2], (D_FF,), dtype=jnp.float32) * (2.0 * np.pi), 'quantum_weights_real': jax.random.normal(ks[3], (D_FF,), dtype=jnp.float32) * 0.1, 'quantum_weights_imag': jax.random.normal(ks[4], (D_FF,), dtype=jnp.float32) * 0.1, 'W2': jax.random.normal(ks[5], (D_FF, D_MODEL), dtype=jnp.float32) * (1.0 / np.sqrt(D_FF)), 'b2': jnp.zeros((D_MODEL,), dtype=jnp.float32)}
    _L2_ffn_all = _L2_ffn_setup()
    _L2_ffn_in = {k: v for k, v in _L2_ffn_all.items() if k in ('W1', 'b1', 'quantum_phases', 'quantum_weights_real', 'quantum_weights_imag', 'W2', 'b2')}
    del _L2_ffn_all

    def _L3_attn_setup():
        import jax, jax.numpy as jnp
        import numpy as np
        B, N, C, H, K = (4, 1024, 256, 16, 2)
        D = C // H

        def _kernel(x):
            return jax.nn.silu(x) + 0.5
        key = jax.random.key(seed)
        ks = jax.random.split(key, 8)
        s = 0.02
        x = jax.random.normal(ks[0], (B, N, C), jnp.float32)
        Wq = jax.random.normal(ks[1], (C, C), jnp.float32) * s
        bq = jnp.zeros((C,), jnp.float32)
        Wk = jax.random.normal(ks[2], (K, C, C), jnp.float32) * s
        bk = jnp.zeros((K, C), jnp.float32)
        Wv = jax.random.normal(ks[3], (K, C, C), jnp.float32) * s
        bv = jnp.zeros((K, C), jnp.float32)
        Wo = jax.random.normal(ks[4], (C, C), jnp.float32) * s
        bo = jnp.zeros((C,), jnp.float32)
        ln_g = jnp.ones((C,), jnp.float32)
        ln_b = jnp.zeros((C,), jnp.float32)
        return dict(x=x, Wq=Wq, bq=bq, Wk=Wk, bk=bk, Wv=Wv, bv=bv, Wo=Wo, bo=bo, ln_g=ln_g, ln_b=ln_b)
    _L3_attn_all = _L3_attn_setup()
    _L3_attn_in = {k: v for k, v in _L3_attn_all.items() if k in ('Wq', 'bq', 'Wk', 'bk', 'Wv', 'bv', 'Wo', 'bo', 'ln_g', 'ln_b')}
    del _L3_attn_all

    def _L3_xattn_setup():
        import jax, jax.numpy as jnp
        import numpy as np
        H = 16
        D = 64
        SCALE = D ** (-0.5)
        TEXT = 77
        IMG = 16
        AUD = 32
        MAXREL = 16
        B, NQ, QD = (32, 256, 256)
        INNER = H * D

        def _heads(t):
            return t.reshape(t.shape[0], t.shape[1], H, D)
        key = jax.random.key(seed)
        ks = jax.random.split(key, 14)
        w = lambda k, s: jax.random.normal(k, s, jnp.float32) * 0.02
        return {'x': jax.random.normal(ks[0], (B, NQ, QD), jnp.float32), 'context': jax.random.normal(ks[1], (B, TEXT + IMG + AUD, QD), jnp.float32), 'Wq': w(ks[2], (QD, INNER)), 'Wk': w(ks[3], (QD, INNER)), 'Wv': w(ks[4], (QD, INNER)), 'Wk_ip': w(ks[5], (QD, INNER)), 'Wv_ip': w(ks[6], (QD, INNER)), 'Wk_ap': w(ks[7], (QD, INNER)), 'Wv_ap': w(ks[8], (QD, INNER)), 'Wo': w(ks[9], (INNER, QD)), 'bo': jnp.zeros((QD,), jnp.float32), 'rel_k': w(ks[10], (2 * MAXREL + 1, D)), 'rel_v': w(ks[11], (2 * MAXREL + 1, D)), 'alpha': jnp.zeros((), jnp.float32), 'beta': jnp.zeros((), jnp.float32)}
    _L3_xattn_all = _L3_xattn_setup()
    _L3_xattn_in = {k: v for k, v in _L3_xattn_all.items() if k in ('Wq', 'Wk', 'Wv', 'Wk_ip', 'Wv_ip', 'Wk_ap', 'Wv_ap', 'Wo', 'bo', 'rel_k', 'rel_v', 'alpha', 'beta')}
    del _L3_xattn_all

    def _L3_ffn_setup():
        import jax, jax.numpy as jnp
        import numpy as np
        QMIN, QMAX = (-128.0, 127.0)

        def _affine_quantize(x):
            amin, amax = (jnp.min(x), jnp.max(x))
            scale = jnp.maximum((amax - amin) / 255.0, 1e-08)
            zp = jnp.clip(jnp.round(-amin / scale) + QMIN, QMIN, QMAX)
            q = jnp.clip(jnp.round(x / scale) + zp, QMIN, QMAX)
            return (q, scale, zp)

        def _sym_quantize(w):
            scale = jnp.maximum(jnp.max(jnp.abs(w)) / 127.0, 1e-08)
            q = jnp.clip(jnp.round(w / scale), -127.0, 127.0)
            return (q, scale)

        def _qlinear(x, W, b):
            xq, sx, zx = _affine_quantize(x)
            wq, sw = _sym_quantize(W)
            acc = jnp.einsum('bsh,oh->bso', xq - zx, wq)
            return acc * (sx * sw) + b
        key = jax.random.key(seed)
        k1, k2, k3, k4, k5 = jax.random.split(key, 5)
        d, h = (256, 1024)
        x = jax.random.normal(k1, (4, 1024, d), dtype=jnp.float32)
        W1 = jax.random.normal(k2, (h, d), dtype=jnp.float32) * (1.0 / np.sqrt(d))
        b1 = jax.random.normal(k3, (h,), dtype=jnp.float32) * 0.02
        W2 = jax.random.normal(k4, (d, h), dtype=jnp.float32) * (1.0 / np.sqrt(h))
        b2 = jax.random.normal(k5, (d,), dtype=jnp.float32) * 0.02
        return {'x': x, 'W1': W1, 'b1': b1, 'W2': W2, 'b2': b2}
    _L3_ffn_all = _L3_ffn_setup()
    _L3_ffn_in = {k: v for k, v in _L3_ffn_all.items() if k in ('W1', 'b1', 'W2', 'b2')}
    del _L3_ffn_all
    return {'x': x, 'ctx_1024': ctx_1024, 'mask_BxS2_bf1': mask_BxS2_bf1, 'mask_BxSxS2_bk0': mask_BxSxS2_bk0, 'L0_attn_Wq': _L0_attn_in['Wq'], 'L0_attn_Wk': _L0_attn_in['Wk'], 'L0_attn_Wv': _L0_attn_in['Wv'], 'L0_attn_Wp': _L0_attn_in['Wp'], 'L0_attn_bp': _L0_attn_in['bp'], 'L0_xattn_Wq': _L0_xattn_in['Wq'], 'L0_xattn_bq': _L0_xattn_in['bq'], 'L0_xattn_Wk': _L0_xattn_in['Wk'], 'L0_xattn_bk': _L0_xattn_in['bk'], 'L0_xattn_Wv': _L0_xattn_in['Wv'], 'L0_xattn_bv': _L0_xattn_in['bv'], 'L0_xattn_Wo': _L0_xattn_in['Wo'], 'L0_xattn_bo': _L0_xattn_in['bo'], 'L0_ffn_router_w': _L0_ffn_in['router_w'], 'L0_ffn_w_gate': _L0_ffn_in['w_gate'], 'L0_ffn_w_up': _L0_ffn_in['w_up'], 'L0_ffn_w_down': _L0_ffn_in['w_down'], 'L1_attn_qkv_w': _L1_attn_in['qkv_w'], 'L1_attn_o_w': _L1_attn_in['o_w'], 'L1_attn_norm1_w': _L1_attn_in['norm1_w'], 'L1_attn_norm2_w': _L1_attn_in['norm2_w'], 'L1_attn_in_w': _L1_attn_in['in_w'], 'L1_attn_out_w': _L1_attn_in['out_w'], 'L1_attn_A_log': _L1_attn_in['A_log'], 'L1_attn_Bp_w': _L1_attn_in['Bp_w'], 'L1_attn_Cp_w': _L1_attn_in['Cp_w'], 'L1_attn_dt_w': _L1_attn_in['dt_w'], 'L1_attn_dt_b': _L1_attn_in['dt_b'], 'L1_attn_gate_w': _L1_attn_in['gate_w'], 'L1_xattn_Wq': _L1_xattn_in['Wq'], 'L1_xattn_Wkv': _L1_xattn_in['Wkv'], 'L1_xattn_Wo': _L1_xattn_in['Wo'], 'L1_xattn_nbias': _L1_xattn_in['nbias'], 'L1_ffn_shared_gate': _L1_ffn_in['shared_gate'], 'L1_ffn_shared_up': _L1_ffn_in['shared_up'], 'L1_ffn_shared_down': _L1_ffn_in['shared_down'], 'L1_ffn_gate_w': _L1_ffn_in['gate_w'], 'L1_ffn_up_w': _L1_ffn_in['up_w'], 'L1_ffn_down_w': _L1_ffn_in['down_w'], 'L1_ffn_router_w': _L1_ffn_in['router_w'], 'L1_ffn_routing_bias': _L1_ffn_in['routing_bias'], 'L2_attn_Wq': _L2_attn_in['Wq'], 'L2_attn_Wk': _L2_attn_in['Wk'], 'L2_attn_Wv': _L2_attn_in['Wv'], 'L2_attn_Wo': _L2_attn_in['Wo'], 'L2_attn_bo': _L2_attn_in['bo'], 'L2_ffn_W1': _L2_ffn_in['W1'], 'L2_ffn_b1': _L2_ffn_in['b1'], 'L2_ffn_quantum_phases': _L2_ffn_in['quantum_phases'], 'L2_ffn_quantum_weights_real': _L2_ffn_in['quantum_weights_real'], 'L2_ffn_quantum_weights_imag': _L2_ffn_in['quantum_weights_imag'], 'L2_ffn_W2': _L2_ffn_in['W2'], 'L2_ffn_b2': _L2_ffn_in['b2'], 'L3_attn_Wq': _L3_attn_in['Wq'], 'L3_attn_bq': _L3_attn_in['bq'], 'L3_attn_Wk': _L3_attn_in['Wk'], 'L3_attn_bk': _L3_attn_in['bk'], 'L3_attn_Wv': _L3_attn_in['Wv'], 'L3_attn_bv': _L3_attn_in['bv'], 'L3_attn_Wo': _L3_attn_in['Wo'], 'L3_attn_bo': _L3_attn_in['bo'], 'L3_attn_ln_g': _L3_attn_in['ln_g'], 'L3_attn_ln_b': _L3_attn_in['ln_b'], 'L3_xattn_Wq': _L3_xattn_in['Wq'], 'L3_xattn_Wk': _L3_xattn_in['Wk'], 'L3_xattn_Wv': _L3_xattn_in['Wv'], 'L3_xattn_Wk_ip': _L3_xattn_in['Wk_ip'], 'L3_xattn_Wv_ip': _L3_xattn_in['Wv_ip'], 'L3_xattn_Wk_ap': _L3_xattn_in['Wk_ap'], 'L3_xattn_Wv_ap': _L3_xattn_in['Wv_ap'], 'L3_xattn_Wo': _L3_xattn_in['Wo'], 'L3_xattn_bo': _L3_xattn_in['bo'], 'L3_xattn_rel_k': _L3_xattn_in['rel_k'], 'L3_xattn_rel_v': _L3_xattn_in['rel_v'], 'L3_xattn_alpha': _L3_xattn_in['alpha'], 'L3_xattn_beta': _L3_xattn_in['beta'], 'L3_ffn_W1': _L3_ffn_in['W1'], 'L3_ffn_b1': _L3_ffn_in['b1'], 'L3_ffn_W2': _L3_ffn_in['W2'], 'L3_ffn_b2': _L3_ffn_in['b2']}

def reference(x, ctx_1024, mask_BxS2_bf1, mask_BxSxS2_bk0, L0_attn_Wq, L0_attn_Wk, L0_attn_Wv, L0_attn_Wp, L0_attn_bp, L0_xattn_Wq, L0_xattn_bq, L0_xattn_Wk, L0_xattn_bk, L0_xattn_Wv, L0_xattn_bv, L0_xattn_Wo, L0_xattn_bo, L0_ffn_router_w, L0_ffn_w_gate, L0_ffn_w_up, L0_ffn_w_down, L1_attn_qkv_w, L1_attn_o_w, L1_attn_norm1_w, L1_attn_norm2_w, L1_attn_in_w, L1_attn_out_w, L1_attn_A_log, L1_attn_Bp_w, L1_attn_Cp_w, L1_attn_dt_w, L1_attn_dt_b, L1_attn_gate_w, L1_xattn_Wq, L1_xattn_Wkv, L1_xattn_Wo, L1_xattn_nbias, L1_ffn_shared_gate, L1_ffn_shared_up, L1_ffn_shared_down, L1_ffn_gate_w, L1_ffn_up_w, L1_ffn_down_w, L1_ffn_router_w, L1_ffn_routing_bias, L2_attn_Wq, L2_attn_Wk, L2_attn_Wv, L2_attn_Wo, L2_attn_bo, L2_ffn_W1, L2_ffn_b1, L2_ffn_quantum_phases, L2_ffn_quantum_weights_real, L2_ffn_quantum_weights_imag, L2_ffn_W2, L2_ffn_b2, L3_attn_Wq, L3_attn_bq, L3_attn_Wk, L3_attn_bk, L3_attn_Wv, L3_attn_bv, L3_attn_Wo, L3_attn_bo, L3_attn_ln_g, L3_attn_ln_b, L3_xattn_Wq, L3_xattn_Wk, L3_xattn_Wv, L3_xattn_Wk_ip, L3_xattn_Wv_ip, L3_xattn_Wk_ap, L3_xattn_Wv_ap, L3_xattn_Wo, L3_xattn_bo, L3_xattn_rel_k, L3_xattn_rel_v, L3_xattn_alpha, L3_xattn_beta, L3_ffn_W1, L3_ffn_b1, L3_ffn_W2, L3_ffn_b2):
    import jax
    import jax.numpy as jnp

    def _L0_attn_ref(x, Wq, Wk, Wv, Wp, bp):
        import jax, jax.numpy as jnp
        import numpy as np
        NUM_HEADS = 16
        EPS = 1e-06
        CHUNK = 128
        B, T, E = x.shape
        H = NUM_HEADS
        D = E // H
        N = T // CHUNK
        q = x @ Wq.T
        k = x @ Wk.T
        v = x @ Wv.T

        def split_heads(t):
            return t.reshape(B, T, H, D).transpose(0, 2, 1, 3).reshape(B, H, N, CHUNK, D)
        phi_q = jax.nn.elu(split_heads(q)) + 1.0
        phi_k = jax.nn.elu(split_heads(k)) + 1.0
        vh = split_heads(v)
        kv = jnp.einsum('bhncd,bhnce->bhnde', phi_k, vh)
        zk = phi_k.sum(axis=3)
        S_prev = jnp.concatenate([jnp.zeros_like(kv[:, :, :1]), jnp.cumsum(kv, axis=2)[:, :, :-1]], axis=2)
        Z_prev = jnp.concatenate([jnp.zeros_like(zk[:, :, :1]), jnp.cumsum(zk, axis=2)[:, :, :-1]], axis=2)
        A = jnp.einsum('bhncd,bhnsd->bhncs', phi_q, phi_k)
        mask = jnp.tril(jnp.ones((CHUNK, CHUNK), bool))
        A = jnp.where(mask, A, 0.0)
        num = jnp.einsum('bhncs,bhnse->bhnce', A, vh) + jnp.einsum('bhncd,bhnde->bhnce', phi_q, S_prev)
        den = A.sum(-1) + jnp.einsum('bhncd,bhnd->bhnc', phi_q, Z_prev) + EPS
        y = num / den[..., None]
        y = y.reshape(B, H, T, D).transpose(0, 2, 1, 3).reshape(B, T, E)
        return y @ Wp.T + bp

    def _L0_xattn_ref(q, k, v, attention_mask, Wq, bq, Wk, bk, Wv, bv, Wo, bo):
        import jax, jax.numpy as jnp
        import numpy as np
        N_HEADS = 16
        D_MODEL = 256
        HEAD_DIM = D_MODEL // N_HEADS
        MASK_FILL = -100000000.0

        def _split_heads(x):
            B, S, _ = x.shape
            return x.reshape(B, S, N_HEADS, HEAD_DIM).transpose(0, 2, 1, 3)
        qm = _split_heads(q @ Wq.T + bq)
        km = _split_heads(k @ Wk.T + bk)
        vm = _split_heads(v @ Wv.T + bv)
        scores = jnp.einsum('bnlh,bnph->bnlp', qm, km) / np.sqrt(HEAD_DIM).astype(np.float32)
        mask = attention_mask[:, None, None, :]
        scores = jnp.where(mask, scores, MASK_FILL)
        attn = jax.nn.softmax(scores, axis=-1)
        out = jnp.einsum('bnlp,bnph->bnlh', attn, vm)
        B, _, L, _ = out.shape
        out = out.transpose(0, 2, 1, 3).reshape(B, L, D_MODEL)
        return out @ Wo.T + bo

    def _L0_ffn_ref(x, router_w, w_gate, w_up, w_down):
        import jax, jax.numpy as jnp
        import numpy as np
        from jax import lax
        DIM = 256
        HID = 512
        E = 8
        K = 2
        B, T = (2, 128)
        Bb, Tt, D = x.shape
        N = Bb * Tt
        xf = x.reshape(N, D)
        logits = xf @ router_w.T
        routing = jax.nn.softmax(logits, axis=-1)
        top_w, top_i = lax.top_k(routing, K)
        top_w = top_w / jnp.sum(top_w, axis=-1, keepdims=True)
        combine = jnp.zeros((N, E), dtype=x.dtype)
        combine = combine.at[jnp.arange(N)[:, None], top_i].add(top_w)
        g = jnp.einsum('nd,ehd->neh', xf, w_gate)
        u = jnp.einsum('nd,ehd->neh', xf, w_up)
        h = jax.nn.silu(g) * u
        y = jnp.einsum('neh,edh->ned', h, w_down)
        out = jnp.einsum('ned,ne->nd', y, combine)
        return out.reshape(Bb, Tt, D)

    def _L1_attn_ref(x, qkv_w, o_w, norm1_w, norm2_w, in_w, out_w, A_log, Bp_w, Cp_w, dt_w, dt_b, gate_w):
        import jax, jax.numpy as jnp
        import numpy as np
        EPS = 1.1920929e-07

        def rmsnorm(x, w):
            return x * jax.lax.rsqrt(jnp.mean(x * x, axis=-1, keepdims=True) + EPS) * w

        def selective_scan(h, in_w, out_w, A_log, Bp_w, Cp_w, dt_w, dt_b, gate_w):
            B, T, D = h.shape
            SC, ST = A_log.shape
            z = h @ in_w.T
            gate = jax.nn.silu(h @ gate_w.T)
            A = -jnp.exp(A_log)
            Bi = z @ Bp_w.T
            Ci = z @ Cp_w.T
            dt = jax.nn.softplus(z @ dt_w.T + dt_b)
            A_bar = 1.0 + dt[..., None] * A

            def step(state, inp):
                a_bar, dtz_t, b_t, c_t = inp
                state = a_bar * state + dtz_t[:, :, None] * b_t[:, None, :]
                y = jnp.sum(state * c_t[:, None, :], axis=-1)
                return (state, y)
            init = jnp.zeros((B, SC, ST), h.dtype)
            xs = (jnp.swapaxes(A_bar, 0, 1), jnp.swapaxes(dt * z, 0, 1), jnp.swapaxes(Bi, 0, 1), jnp.swapaxes(Ci, 0, 1))
            _, ys = jax.lax.scan(step, init, xs)
            y = jnp.swapaxes(ys, 0, 1) * gate
            return y @ out_w.T
        B, T, D = x.shape
        H = 16
        hd = D // H
        h = rmsnorm(x, norm1_w)
        qkv = (h @ qkv_w.T).reshape(B, T, 3, H, hd)
        qkv = jnp.transpose(qkv, (2, 0, 3, 1, 4))
        q, k, v = (qkv[0], qkv[1], qkv[2])
        attn = jnp.einsum('bhqd,bhkd->bhqk', q, k) / np.sqrt(hd).astype(np.float32)
        mask = jnp.tril(jnp.ones((T, T), bool))
        attn = jnp.where(mask, attn, -jnp.inf)
        attn = jax.nn.softmax(attn, axis=-1)
        out = jnp.einsum('bhqk,bhkd->bhqd', attn, v)
        out = jnp.transpose(out, (0, 2, 1, 3)).reshape(B, T, D)
        x = x + out @ o_w.T
        h2 = rmsnorm(x, norm2_w)
        x = x + selective_scan(h2, in_w, out_w, A_log, Bp_w, Cp_w, dt_w, dt_b, gate_w)
        return x

    def _L1_xattn_ref(iQ, iK, mask, Wq, Wkv, Wo, nbias):
        import jax, jax.numpy as jnp
        import numpy as np
        from math import sqrt
        B, Q, S, D, H = (2, 512, 512, 256, 16)
        ADIM = D // H
        IEPS = 1e-32

        def sparse_norm(scores, nbias):
            t = jax.nn.relu(scores + nbias[0])
            t = t * t
            return t / (t.sum(-1, keepdims=True) + IEPS)
        b, q, _ = iQ.shape
        s = iK.shape[1]
        rq = (iQ @ Wq.T).reshape(b, q, H, ADIM)
        kv = (iK @ Wkv.T).reshape(b, s, 2, H, ADIM)
        rk, rv = (kv[:, :, 0], kv[:, :, 1])
        scores = jnp.einsum('bqhd,bshd->bhqs', rq, rk) / sqrt(ADIM)
        scores = jnp.where(mask[:, None, :, :], jnp.float32(-1e+32), scores)
        attn = sparse_norm(scores, nbias)
        o = jnp.einsum('bhqs,bshd->bqhd', attn, rv).reshape(b, q, H * ADIM)
        return o @ Wo.T

    def _L1_ffn_ref(x, shared_gate, shared_up, shared_down, gate_w, up_w, down_w, router_w, routing_bias):
        import jax, jax.numpy as jnp
        import numpy as np
        B, S, H = (2, 512, 256)
        E_ROUTED = 8
        TOP_K = 2
        I = 512
        b, s, h = x.shape
        shared = jnp.einsum('bsi,hi->bsh', jax.nn.silu(jnp.einsum('bsh,ih->bsi', x, shared_gate)) * jnp.einsum('bsh,ih->bsi', x, shared_up), shared_down)
        logits = jnp.einsum('bsh,eh->bse', x, router_w) + routing_bias
        probs = jax.nn.sigmoid(logits)
        scores, indices = jax.lax.top_k(probs, TOP_K)
        scores = scores / jnp.sum(scores, axis=-1, keepdims=True)
        t = b * s
        xf = x.reshape(t, h)
        idx = indices.reshape(t, TOP_K)
        sc = scores.reshape(t, TOP_K)
        w = jnp.zeros((t, E_ROUTED), dtype=x.dtype)
        w = w.at[jnp.arange(t)[:, None], idx].add(sc)
        g = jax.nn.silu(jnp.einsum('th,ehi->tei', xf, gate_w))
        u = jnp.einsum('th,ehi->tei', xf, up_w)
        combined = jnp.einsum('tei,eih,te->th', g * u, down_w, w)
        return shared + combined.reshape(b, s, h)

    def _L2_attn_ref(x, Wq, Wk, Wv, Wo, bo):
        import jax, jax.numpy as jnp
        import numpy as np
        HEADS = 16
        DIM_HEAD = 64
        B, N, D = x.shape
        h, dh = (HEADS, DIM_HEAD)
        scale = dh ** (-0.5)

        def split(t):
            return t.reshape(B, N, h, dh).transpose(0, 2, 1, 3)
        q = split(x @ Wq)
        k = split(x @ Wk)
        v = split(x @ Wv)
        dots = jnp.einsum('bhid,bhjd->bhij', q, k) * scale
        mask_value = -jnp.finfo(dots.dtype).max
        causal = jnp.tril(jnp.ones((N, N), dtype=bool))
        dots = jnp.where(causal, dots, mask_value)
        attn = jax.nn.softmax(dots, axis=-1)
        out = jnp.einsum('bhij,bhjd->bhid', attn, v)
        out = out.transpose(0, 2, 1, 3).reshape(B, N, h * dh)
        return out @ Wo + bo

    def _L2_xattn_ref(query, keys):
        import jax, jax.numpy as jnp
        import numpy as np
        B, S, D = (8, 512, 256)
        query1 = 0.4 * query
        keys1 = 0.6 * keys
        attn = jnp.einsum('bqd,bkd->bqk', query1, keys1)
        attn = jax.nn.softmax(attn, axis=-1)
        fused = jnp.einsum('bqk,bkd->bqd', attn, keys1) + keys
        return fused

    def _L2_ffn_ref(x, W1, b1, quantum_phases, quantum_weights_real, quantum_weights_imag, W2, b2):
        import jax, jax.numpy as jnp
        import numpy as np
        B, S, D_MODEL, D_FF = (4, 512, 256, 1024)

        def _quantum_transform(hidden, theta, w_real, w_imag):
            imag = w_imag * jnp.sin(theta + hidden * 0.1)
            quantum_phase = jnp.cos(theta) * w_real + jnp.sin(theta) * w_imag
            return hidden + quantum_phase * imag * 0.1
        hidden = jnp.einsum('bsd,df->bsf', x, W1) + b1
        q = _quantum_transform(hidden, quantum_phases, quantum_weights_real, quantum_weights_imag)
        act = jax.nn.relu(q)
        return jnp.einsum('bsf,fd->bsd', act, W2) + b2

    def _L3_attn_ref(x, Wq, bq, Wk, bk, Wv, bv, Wo, bo, ln_g, ln_b):
        import jax, jax.numpy as jnp
        import numpy as np
        B, N, C, H, K = (4, 1024, 256, 16, 2)
        D = C // H

        def _kernel(x):
            return jax.nn.silu(x) + 0.5
        dtype = x.dtype
        Bn, Nn, Cn = x.shape
        q = x + x @ Wq.T + bq
        ks = x[None] + jnp.einsum('bnc,kdc->kbnd', x, Wk) + bk[:, None, None, :]
        vs = x[None] + jnp.einsum('bnc,kdc->kbnd', x, Wv) + bv[:, None, None, :]
        q = q.reshape(Bn, Nn, H, D).transpose(0, 2, 1, 3)
        ks = ks.reshape(K, Bn, Nn, H, D).transpose(0, 1, 3, 2, 4)
        vs = vs.reshape(K, Bn, Nn, H, D).transpose(0, 1, 3, 2, 4)
        q = _kernel(q)
        ks = _kernel(ks)
        q = q / (jnp.linalg.norm(q, axis=-1, keepdims=True) + 1e-06)
        ks = ks / (jnp.linalg.norm(ks, axis=-1, keepdims=True) + 1e-06)
        scale = Nn ** (-0.5)
        ks = ks.astype(jnp.float32) * scale
        vs = vs.astype(jnp.float32) * scale
        states = jnp.einsum('kbhnd,kbhne->kbhde', ks, vs)
        state = jnp.prod(states, axis=0)
        out = jnp.einsum('bhnd,bhde->bhne', q.astype(jnp.float32), state)
        out = out.astype(dtype)
        out = out.transpose(0, 2, 1, 3).reshape(Bn, Nn, Cn)
        mu = out.mean(axis=-1, keepdims=True)
        var = out.var(axis=-1, keepdims=True)
        out = (out - mu) * jax.lax.rsqrt(var + 1e-05) * ln_g + ln_b
        out = out @ Wo.T + bo
        return out

    def _L3_xattn_ref(x, context, Wq, Wk, Wv, Wk_ip, Wv_ip, Wk_ap, Wv_ap, Wo, bo, rel_k, rel_v, alpha, beta):
        import jax, jax.numpy as jnp
        import numpy as np
        H = 16
        D = 64
        SCALE = D ** (-0.5)
        TEXT = 77
        IMG = 16
        AUD = 32
        MAXREL = 16
        B, NQ, QD = (32, 256, 256)
        INNER = H * D

        def _heads(t):
            return t.reshape(t.shape[0], t.shape[1], H, D)
        b, nq, _ = x.shape
        q = _heads(x @ Wq)
        ctx_t = context[:, :TEXT]
        ctx_i = context[:, TEXT:TEXT + IMG]
        ctx_a = context[:, TEXT + IMG:]
        k = _heads(ctx_t @ Wk)
        v = _heads(ctx_t @ Wv)
        sim = jnp.einsum('bihd,bjhd->bhij', q, k) * SCALE
        dist = jnp.clip(jnp.arange(TEXT)[None, :] - jnp.arange(nq)[:, None], -MAXREL, MAXREL) + MAXREL
        k2 = rel_k[dist]
        sim = sim + jnp.einsum('bihd,ijd->bhij', q, k2) * SCALE
        attn = jax.nn.softmax(sim, axis=-1)
        out = jnp.einsum('bhij,bjhd->bihd', attn, v)
        out = out + jnp.einsum('bhij,ijd->bihd', attn, rel_v[dist])

        def stream(W_k, W_v, ctx):
            kh = _heads(ctx @ W_k)
            vh = _heads(ctx @ W_v)
            a = jax.nn.softmax(jnp.einsum('bihd,bjhd->bhij', q, kh) * SCALE, axis=-1)
            return jnp.einsum('bhij,bjhd->bihd', a, vh)
        out = out + stream(Wk_ip, Wv_ip, ctx_i) * (jnp.tanh(alpha) + 1.0)
        out = out + stream(Wk_ap, Wv_ap, ctx_a) * (jnp.tanh(beta) + 1.0)
        out = out.reshape(b, nq, INNER)
        return out @ Wo + bo

    def _L3_ffn_ref(x, W1, b1, W2, b2):
        import jax, jax.numpy as jnp
        import numpy as np
        QMIN, QMAX = (-128.0, 127.0)

        def _affine_quantize(x):
            amin, amax = (jnp.min(x), jnp.max(x))
            scale = jnp.maximum((amax - amin) / 255.0, 1e-08)
            zp = jnp.clip(jnp.round(-amin / scale) + QMIN, QMIN, QMAX)
            q = jnp.clip(jnp.round(x / scale) + zp, QMIN, QMAX)
            return (q, scale, zp)

        def _sym_quantize(w):
            scale = jnp.maximum(jnp.max(jnp.abs(w)) / 127.0, 1e-08)
            q = jnp.clip(jnp.round(w / scale), -127.0, 127.0)
            return (q, scale)

        def _qlinear(x, W, b):
            xq, sx, zx = _affine_quantize(x)
            wq, sw = _sym_quantize(W)
            acc = jnp.einsum('bsh,oh->bso', xq - zx, wq)
            return acc * (sx * sw) + b
        h = _qlinear(x, W1, b1)
        h = jax.nn.gelu(h, approximate=False)
        out = _qlinear(h, W2, b2)
        return out
    x = x + _L0_attn_ref(_layernorm(x, axis=-1), L0_attn_Wq, L0_attn_Wk, L0_attn_Wv, L0_attn_Wp, L0_attn_bp)
    x = x + _L0_xattn_ref(_layernorm(x, axis=-1), ctx_1024, ctx_1024, mask_BxS2_bf1, L0_xattn_Wq, L0_xattn_bq, L0_xattn_Wk, L0_xattn_bk, L0_xattn_Wv, L0_xattn_bv, L0_xattn_Wo, L0_xattn_bo)
    x = x + _L0_ffn_ref(_layernorm(x, axis=-1), L0_ffn_router_w, L0_ffn_w_gate, L0_ffn_w_up, L0_ffn_w_down)
    x = x + _L1_attn_ref(_layernorm(x, axis=-1), L1_attn_qkv_w, L1_attn_o_w, L1_attn_norm1_w, L1_attn_norm2_w, L1_attn_in_w, L1_attn_out_w, L1_attn_A_log, L1_attn_Bp_w, L1_attn_Cp_w, L1_attn_dt_w, L1_attn_dt_b, L1_attn_gate_w)
    x = x + _L1_xattn_ref(_layernorm(x, axis=-1), ctx_1024, mask_BxSxS2_bk0, L1_xattn_Wq, L1_xattn_Wkv, L1_xattn_Wo, L1_xattn_nbias)
    x = x + _L1_ffn_ref(_layernorm(x, axis=-1), L1_ffn_shared_gate, L1_ffn_shared_up, L1_ffn_shared_down, L1_ffn_gate_w, L1_ffn_up_w, L1_ffn_down_w, L1_ffn_router_w, L1_ffn_routing_bias)
    x = x + _L2_attn_ref(_layernorm(x, axis=-1), L2_attn_Wq, L2_attn_Wk, L2_attn_Wv, L2_attn_Wo, L2_attn_bo)
    x = x + _L2_xattn_ref(_layernorm(x, axis=-1), ctx_1024)
    x = x + _L2_ffn_ref(_layernorm(x, axis=-1), L2_ffn_W1, L2_ffn_b1, L2_ffn_quantum_phases, L2_ffn_quantum_weights_real, L2_ffn_quantum_weights_imag, L2_ffn_W2, L2_ffn_b2)
    x = x + _L3_attn_ref(_layernorm(x, axis=-1), L3_attn_Wq, L3_attn_bq, L3_attn_Wk, L3_attn_bk, L3_attn_Wv, L3_attn_bv, L3_attn_Wo, L3_attn_bo, L3_attn_ln_g, L3_attn_ln_b)
    x = x + _L3_xattn_ref(_layernorm(x, axis=-1), ctx_1024, L3_xattn_Wq, L3_xattn_Wk, L3_xattn_Wv, L3_xattn_Wk_ip, L3_xattn_Wv_ip, L3_xattn_Wk_ap, L3_xattn_Wv_ap, L3_xattn_Wo, L3_xattn_bo, L3_xattn_rel_k, L3_xattn_rel_v, L3_xattn_alpha, L3_xattn_beta)
    x = x + _L3_ffn_ref(_layernorm(x, axis=-1), L3_ffn_W1, L3_ffn_b1, L3_ffn_W2, L3_ffn_b2)
    return x

_drawn_inputs = setup_inputs


def setup_inputs(seed=0):
    import zlib

    import numpy as np

    out = dict(_drawn_inputs(seed))
    spreads = {'L0_attn_bp': (0.0, 0.1),
     'L0_xattn_bq': (0.0, 0.1),
     'L0_xattn_bk': (0.0, 0.1),
     'L0_xattn_bv': (0.0, 0.1),
     'L0_xattn_bo': (0.0, 0.1),
     'L1_attn_norm1_w': (1.0, 0.2),
     'L1_attn_norm2_w': (1.0, 0.2),
     'L1_attn_dt_b': (-3.0, 0.2),
     'L1_ffn_routing_bias': (0.0, 0.1),
     'L2_attn_bo': (0.0, 0.1),
     'L2_ffn_b1': (0.0, 0.1),
     'L2_ffn_b2': (0.0, 0.1),
     'L3_attn_bq': (0.0, 0.1),
     'L3_attn_bk': (0.0, 0.1),
     'L3_attn_bv': (0.0, 0.1),
     'L3_attn_bo': (0.0, 0.1),
     'L3_attn_ln_g': (1.0, 0.2),
     'L3_attn_ln_b': (0.0, 0.1),
     'L3_xattn_bo': (0.0, 0.1)}
    factors = {}
    for name, (base, spread) in spreads.items():
        noise = np.random.default_rng([zlib.crc32(name.encode()), seed]).standard_normal(out[name].shape)
        drawn = base * np.exp(spread * noise) if base else spread * noise
        out[name] = jnp.asarray(drawn.astype(out[name].dtype))
    for name, factor in factors.items():
        out[name] = (out[name] * factor).astype(out[name].dtype)
    return out
```

```python
from contextlib import ExitStack

import numpy as np

import concourse.bass as bass
from concourse import mybir

ALU = mybir.AluOpType
ACT = mybir.ActivationFunctionType
AX = mybir.AxisListType
F32 = mybir.dt.float32
BF16 = mybir.dt.bfloat16
U8 = mybir.dt.uint8
U32 = mybir.dt.uint32

P = 128
NB = 16
D = 256
DC = D // P
H = 16
HD = D // H
HC = H // DC
GB = 4
NG = NB // GB
GT = GB * P
LN_EPS = 1e-5


class Step:

    def __init__(self, eng, sem):
        self.eng, self.sem, self.n, self.base = eng, sem, 0, None

    def sig(self, ins):
        self.n += 1
        ins.then_inc(self.sem, 1)
        return ins

    def wait(self):
        self.eng.wait_ge(self.sem, self.n if self.base is None else self.base + self.n)

    def do(self, ins):
        self.sig(ins)
        self.wait()

    def enter(self, var, per, start=0):
        self.before, self.per, self.n = self.n, per, 0
        self.base = var * per + (self.before - start * per)

    def leave(self, times):
        assert self.n == self.per, (self.n, self.per)
        self.n, self.base = self.before + times * self.per, None


def past(eng, sem, value):
    if not (isinstance(value, int) and value <= 0):
        eng.wait_ge(sem, value)


class Region:

    def __init__(self, nc, tag):
        self.nc, self.tag, self.ctx, self.sems = nc, tag, ExitStack(), []

    def sb(self, name, shape, dt=F32):
        return self.ctx.enter_context(self.nc.sbuf_tensor(f"{self.tag}_{name}", shape, dt))

    def ps(self, name, shape, dt=F32):
        return self.ctx.enter_context(self.nc.psum_tensor(f"{self.tag}_{name}", shape, dt))

    def sem(self, name):
        self.sems.append(self.nc.alloc_semaphore(name=f"{self.tag}_{name}"))
        return self.sems[-1]

    def block(self):
        return self.ctx.enter_context(self.nc.Block())

    def close(self):
        self.ctx.close()
        self.nc.clear_and_free_semaphores(self.sems)
        self.nc.all_engine_barrier()


class Shared:
    pass


def row_stats(nc, dve, step, G, b, st6, mv, rows=None):
    rows = G.x if rows is None else rows
    nc.vector.memset(G.pad[:, 0:1], 0.0)
    step.do(nc.vector.bn_stats(out=st6[:, :], in_=rows[:, bass.ds(b * D, D)]))
    nc.vector.memset(G.pad[:, 0:1], 0.0)
    step.do(nc.vector.bn_aggr(out=mv[:, :], in_=st6[:, :]))
    step.do(nc.vector.tensor_scalar(G.mv[:, bass.ds(b * 2, 2)], mv[:, :], 1.0, None, ALU.mult))


def all_row_stats(nc, dve, step, G, st6, batches=range(NB)):
    for b in batches:
        ins = nc.vector.bn_stats(out=st6[:, b * 6:(b + 1) * 6], in_=G.x[:, b * D:(b + 1) * D])
    step.do(ins)
    for b in batches:
        ins = nc.vector.bn_aggr(out=G.mv[:, b * 2:b * 2 + 2], in_=st6[:, b * 6:(b + 1) * 6])
    step.do(ins)


def means(G):
    return G.mv[:, :].rearrange("p (b k) -> p k b", k=2)[:, 0, :]


def variances(G):
    return G.mv[:, :].rearrange("p (b k) -> p k b", k=2)[:, 1, :]


def setup(nc, G, A):
    R = Region(nc, "setup")
    s_load, s_ctx, s_step, s_pool = [R.sem(f"x{g}_loaded") for g in range(NG)], R.sem("context_loaded"), R.sem("dve_step"), R.sem("pool_step")
    st6 = R.sb("st6", [P, 6 * NB])
    block = R.block()

    @block.sync
    def _(sp):
        for g in range(NG):
            sp.dma_start(G.x[:, g * GB * D:(g + 1) * GB * D].rearrange("p (b d) -> p b d", b=GB),
                         A["x"][g * GB:(g + 1) * GB].rearrange("b p d -> p b d")).then_inc(s_load[g], 16)
        sp.dma_start(G.ctxT[:, :], A["ctxT"]).then_inc(s_ctx, 16)
        sp.wait_ge(s_ctx, 16)

    @block.gpsimd
    def _(pool):
        step = Step(pool, s_pool)
        step.sig(nc.gpsimd.memset(G.ident[:, :], 0.0))
        step.sig(nc.gpsimd.memset(G.triu[:, :], 1.0))
        step.sig(nc.gpsimd.memset(G.headmask[:, :], 1.0))
        step.sig(nc.gpsimd.memset(G.neg_upper[:, :], 0.0))
        step.sig(nc.gpsimd.memset(G.neg1e5[:, :], LN_EPS))
        step.do(nc.gpsimd.memset(G.ones_row[:, :], 1.0))
        step.sig(nc.gpsimd.affine_select(out=G.ident[:, :], in_=G.ident[:, :], compare_op=ALU.not_equal, fill=1.0,
                                         base=0, pattern=[[-1, P]], channel_multiplier=1))
        step.sig(nc.gpsimd.affine_select(out=G.triu[:, :], in_=G.triu[:, :], compare_op=ALU.is_ge, fill=0.0,
                                         base=0, pattern=[[1, P]], channel_multiplier=-1))
        step.sig(nc.gpsimd.affine_select(out=G.neg_upper[:, :], in_=G.neg_upper[:, :], compare_op=ALU.is_ge,
                                         fill=-1e30, base=0, pattern=[[-1, P]], channel_multiplier=1))
        step.do(nc.gpsimd.affine_select(out=G.headmask[:, :], in_=G.headmask[:, :], compare_op=ALU.is_ge, fill=0.0,
                                        base=0, pattern=[[-HD, HC]], channel_multiplier=1))
        step.do(nc.gpsimd.affine_select(out=G.headmask[:, :], in_=G.headmask[:, :], compare_op=ALU.is_ge, fill=0.0,
                                        base=HD - 1, pattern=[[HD, HC]], channel_multiplier=-1))
        step.do(nc.gpsimd.tensor_copy(G.identb[:, :], G.ident[:, :]))

    @block.vector
    def _(dve):
        step = Step(dve, s_step)
        for g in range(NG):
            dve.wait_ge(s_load[g], 16)
            all_row_stats(nc, dve, step, G, st6, range(g * GB, (g + 1) * GB))

    R.close()


def finish(nc, G, A):
    R = Region(nc, "finish")
    s_out = R.sem("result_stored")
    block = R.block()

    @block.sync
    def _(sp):
        sp.dma_start(A["out"].rearrange("b p d -> p b d"), G.x[:, :].rearrange("p (b d) -> p b d", b=NB)).then_inc(s_out, 16)
        sp.wait_ge(s_out, 16)

    R.close()
def attention16(nc, G, A, tag, kind, w, normed="layer", cross=False, biased=False, out_bias=None):
    natural = kind in ("softmax", "causal")
    R = Region(nc, tag)
    wq, wk, wv, wo = (R.sb(n, [P, DC * D]) for n in ("wq", "wk", "wv", "wo"))
    st6, mv = R.sb("st6", [P, 6]), R.sb("mv", [P, 2])
    rstd, std = R.sb("rstd", [P, NB]), R.sb("std", [P, NB])
    xn = R.sb("xn", [P, D])
    xnT = R.sb("xnT", [P, D])
    qk = R.sb("qk", [P, 2 * D])
    bd = R.sb("bd", [P, H * P])
    PT = R.sb("PT", [P, H * P])
    V = R.sb("V", [P, H * (HD + 1)])
    osb, oT = R.sb("osb", [P, D]), R.sb("oT", [P, D])
    rden, mx = R.sb("rden", [P, H]), R.sb("mx", [P, H])
    if natural:
        Pn = R.sb("Pn", [P, H * P])
    if kind == "linear":
        elu = R.sb("elu", [P, 2 * D])
    if cross:
        srcT = R.sb("srcT", [P, D])
    else:
        srcT = xnT
    if biased:
        bq, bk, bv = R.sb("bq", [P, DC]), R.sb("bk", [P, DC]), R.sb("bv", [1, D])
    if out_bias:
        bo = R.sb("bo", [1, D])
    if kind == "softmax":
        m8, mbc = R.sb("m8", [P, NB * P // 4], U32), R.sb("mbc", [P, NB * P])
        fill = R.sb("fill", [1, NB * P])
    if kind == "relu2":
        m8, keep = R.sb("m8", [P, NB * P // 4], U32), R.sb("keep", [P, NB * P])
        nbias = R.sb("nbias", [P, 1])
    if normed == "rms":
        nw = R.sb("nw", [P, DC])

    psX = R.ps("psX", [P, 512])
    psQK = R.ps("psQK", [P, 512])
    psVY = R.ps("psVY", [P, 512])
    psO = R.ps("psO", [P, 512])
    psS = R.ps("psS", [P, H * P])

    loaded, var_ready, std_ready, rstd_ready = (R.sem(n) for n in ("weights_loaded", "ones_ready", "std_ready", "rstd_ready"))
    mask_ready = R.sem("mask_ready")
    xn_ready, xt_done, xnT_ready, qk_done, qk_ready, bd_ready = (R.sem(n) for n in (
        "xn_ready", "xT_done", "xnT_ready", "qk_done", "qk_ready", "bd_ready"))
    s_done, shifted, p_ready, pt_done, pt_ready, pt_half = (R.sem(n) for n in (
        "scores_done", "shifted", "p_ready", "pT_done", "pT_ready", "pT_half_ready"))
    v_done, v_ready, o_done, osb_ready, ot_done, ot_ready, y_done, x_ready = (R.sem(n) for n in (
        "v_done", "v_ready", "o_done", "o_ready", "oT_done", "oT_ready", "y_done", "x_ready"))
    src_ready, elu_in, elu_out, masked_ready = (R.sem(n) for n in ("src_ready", "elu_in", "elu_out", "masked"))
    s_step = R.sem("dve_step")
    a_step = R.sem("act_step")
    block = R.block()

    loads = [(wq, A[w + "Wq"]), (wk, A[w + "Wk"]), (wv, A[w + "Wv"]), (wo, A[w + "Wo"])]
    if biased:
        loads += [(bq, A[w + "bq"]), (bk, A[w + "bk"]), (bv, A[w + "bv"])]
    if out_bias:
        loads += [(bo, A[w + "bo"])]
    if kind == "softmax":
        loads += [(m8, A["mask_bc"])]
    if kind == "relu2":
        loads += [(m8, A["maskT"]), (nbias, A["nbias_bc"])]
    if normed == "rms":
        loads += [(nw, A[w + "norm"])]
    NL = 16 * len(loads)
    last = NB - 1
    score_scale = 1.0 if kind == "linear" else HD ** -0.5
    den_eps = {"linear": 1e-6, "relu2": 1e-32}.get(kind, 0.0)
    stat, spread = (qk[:, 0:D], qk[:, D:2 * D]) if natural else (qk[:, D:2 * D], qk[:, 0:D])

    @block.sync
    def _(sp):
        for dst, src in loads:
            sp.dma_start(dst[:, :], src).then_inc(loaded, 16)
        sp.wait_ge(loaded, NL)

    @block.gpsimd
    def _(pool):
        def source(b):
            if cross:
                past(pool, v_done, b)
                nc.gpsimd.tensor_copy(srcT[:, :].rearrange("p (c t) -> p c t", c=DC),
                                      G.ctxT[:, :].rearrange("p (c n) -> p c n", c=DC)[:, :, bass.ds(b * P, P)])\
                    .then_inc(src_ready, 1)

        def spread_heads(b):
            pool.wait_ge(qk_ready, b + 1)
            past(pool, s_done, b)
            for c in range(DC):
                nc.gpsimd.tensor_tensor(
                    bd[:, c * HC * P:(c + 1) * HC * P].rearrange("p (h t) -> p h t", h=HC),
                    spread[:, c * P:(c + 1) * P].unsqueeze(1).to_broadcast([P, HC, P]),
                    G.headmask[:, :].unsqueeze(2).to_broadcast([P, HC, P]), ALU.mult).then_inc(bd_ready, 1)

        source(0)
        spread_heads(0)
        with pool.Fori(1, NB) as b:
            source(b)
            spread_heads(b)

    @block.tensor
    def _(pe):
        pe.wait_ge(loaded, NL)
        pe.wait_ge(var_ready, 1)

        def transpose_x(b, first=False):
            pe.wait_ge(xn_ready, b + 1)
            past(pe, xnT_ready, b)
            if not first:
                past(pe, ot_ready, b - 1)
            for c in range(DC):
                last_ = nc.tensor.transpose(psX[:, c * P:(c + 1) * P], xn[:, c * P:(c + 1) * P], G.ident[:, :])
            last_.then_inc(xt_done, 1)

        def project_qk(b):
            pe.wait_ge(xnT_ready, b + 1)
            if cross:
                pe.wait_ge(src_ready, b + 1)
            for i, (wt, act_T) in enumerate(((wq, xnT), (wk, srcT))):
                for j in range(DC):
                    for c in range(DC):
                        last_ = nc.tensor.matmul(psQK[:, (i * DC + j) * P:(i * DC + j + 1) * P],
                                                 wt[:, c * D + j * P:c * D + (j + 1) * P],
                                                 act_T[:, c * P:(c + 1) * P], start=(c == 0), stop=(c == DC - 1))
            last_.then_inc(qk_done, 1)

        def project_v(b, first=False):
            past(pe, v_ready, b)
            if not first:
                past(pe, x_ready, b - 1)
            for c in range(DC):
                last_ = nc.tensor.matmul(psVY[:, 0:D], srcT[:, c * P:(c + 1) * P], wv[:, c * D:(c + 1) * D],
                                         start=(c == 0), stop=(c == DC - 1 and not biased))
            if biased:
                last_ = nc.tensor.matmul(psVY[:, 0:D], G.ones_row[:, :], bv[:, :], start=False, stop=True)
            last_.then_inc(v_done, 1)

        def scores(b):
            pe.wait_ge(bd_ready, DC * b + DC)
            if kind != "relu2":
                past(pe, pt_ready, b)
            if kind != "linear":
                past(pe, pt_half, b)
            if kind == "softmax":
                pe.wait_ge(mask_ready, 1)
            for g in range(4):
                c = g // 2
                last_ = nc.tensor.matmul(psS[:, g * 512:(g + 1) * 512], stat[:, c * P:(c + 1) * P],
                                         bd[:, g * 512:(g + 1) * 512], start=True, stop=not natural)
                if kind == "softmax":
                    last_ = nc.tensor.matmul(psS[:, g * 512:(g + 1) * 512], G.ones_row[:, :],
                                             fill[:, bass.ds(b * P, P)].unsqueeze(1).to_broadcast([1, 4, P]),
                                             start=False, stop=True)
                if kind == "causal":
                    last_ = nc.tensor.matmul(psS[:, g * 512:(g + 1) * 512], G.identb[:, :],
                                             G.neg_upper[:, :].unsqueeze(1).to_broadcast([P, 4, P]),
                                             start=False, stop=True)
            last_.then_inc(s_done, 1)

        def transpose_p(b):
            if natural:
                pe.wait_ge(p_ready, b + 1)
                for h in range(H):
                    last_ = nc.tensor.transpose(psS[:, h * P:(h + 1) * P], Pn[:, h * P:(h + 1) * P], G.ident[:, :])
                last_.then_inc(pt_done, 1)

        def weigh_values(b):
            if kind != "relu2":
                pe.wait_ge(pt_ready, b + 1)
            if kind != "linear":
                pe.wait_ge(pt_half, b + 1)
            pe.wait_ge(v_ready, b + 1)
            past(pe, osb_ready, b)
            for h in range(H):
                last_ = nc.tensor.matmul(psO[:, h * (HD + 1):(h + 1) * (HD + 1)], PT[:, h * P:(h + 1) * P],
                                         V[:, h * (HD + 1):(h + 1) * (HD + 1)], start=True, stop=True)
            last_.then_inc(o_done, 1)

        def transpose_o(b, more):
            if more:
                pe.wait_ge(xnT_ready, b + 2)
            pe.wait_ge(osb_ready, b + 1)
            for c in range(DC):
                last_ = nc.tensor.transpose(psX[:, (DC + c) * P:(DC + c + 1) * P], osb[:, c * P:(c + 1) * P], G.ident[:, :])
            last_.then_inc(ot_done, 1)

        def project_out(b, more):
            if more:
                pe.wait_ge(v_ready, b + 2)
            pe.wait_ge(ot_ready, b + 1)
            past(pe, x_ready, b)
            for c in range(DC):
                last_ = nc.tensor.matmul(psVY[:, D:2 * D], oT[:, c * P:(c + 1) * P], wo[:, c * D:(c + 1) * D],
                                         start=(c == 0), stop=(c == DC - 1 and not out_bias))
            if out_bias:
                last_ = nc.tensor.matmul(psVY[:, D:2 * D], G.ones_row[:, :], bo[:, :], start=False, stop=True)
            last_.then_inc(y_done, 1)

        def body(b, more):
            scores(b)
            if more:
                transpose_x(b + 1)
                project_qk(b + 1)
            transpose_p(b)
            weigh_values(b)
            if more:
                project_v(b + 1)
            transpose_o(b, more)
            project_out(b, more)

        transpose_x(0, first=True)
        project_qk(0)
        project_v(0, first=True)
        body(0, True)
        with pe.Fori(1, last) as b:
            body(b, True)
        body(last, False)

    @block.scalar
    def _(act):
        step = Step(act, a_step)
        if normed == "layer":
            nc.scalar.activation(std[:, :], variances(G), ACT.Sqrt, bias=G.neg1e5[:, 0:1]).then_inc(std_ready, 1)
        act.wait_ge(loaded, NL)

        def take_xT(b):
            act.wait_ge(xt_done, b + 1)
            past(act, v_done, b)
            past(act, qk_done, b)
            for c in range(DC):
                scale = nw[:, c:c + 1] if normed == "rms" else 1.0
                ins = nc.scalar.activation(xnT[:, c * P:(c + 1) * P], psX[:, c * P:(c + 1) * P], ACT.Copy, scale=scale)
            ins.then_inc(xnT_ready, 1)

        def take_qk(b):
            if kind == "linear":
                act.wait_ge(elu_in, b + 1)
                nc.scalar.activation(elu[:, :], elu[:, :], ACT.Exp).then_inc(elu_out, 1)
                return
            act.wait_ge(qk_done, b + 1)
            past(act, s_done, b)
            past(act, bd_ready, DC * b)
            if biased:
                for c in range(DC):
                    ins = nc.scalar.activation(qk[:, c * P:(c + 1) * P], psQK[:, c * P:(c + 1) * P], ACT.Identity,
                                               bias=bq[:, c:c + 1])
                ins.then_inc(masked_ready, 1)
            else:
                nc.scalar.activation(qk[:, :], psQK[:, :], ACT.Copy).then_inc(qk_ready, 1)

        def weights(b):
            if natural:
                act.wait_ge(shifted, b + 1)
                nc.scalar.activation(Pn[:, :], Pn[:, :], ACT.Exp, scale=score_scale).then_inc(p_ready, 1)
            if kind == "relu2":
                act.wait_ge(s_done, b + 1)
                past(act, o_done, b)
                nc.scalar.activation(PT[:, :], psS[:, :], ACT.Relu, scale=score_scale, bias=nbias[:, 0:1])\
                    .then_inc(shifted, 1)

        def take_pT(b):
            if natural:
                act.wait_ge(pt_done, b + 1)
                past(act, o_done, b)
                nc.scalar.activation(PT[:, 0:1024], psS[:, 0:1024], ACT.Copy).then_inc(pt_half, 1)
            if kind == "relu2":
                act.wait_ge(masked_ready, b + 1)
                nc.scalar.activation(PT[:, :], PT[:, :], ACT.Square).then_inc(pt_half, 1)

        def take_oT(b):
            act.wait_ge(ot_done, b + 1)
            past(act, y_done, b)
            nc.scalar.activation(oT[:, :], psX[:, D:2 * D], ACT.Copy).then_inc(ot_ready, 1)

        def body(b, more):
            if kind == "relu2":
                weights(b)
            if more:
                take_xT(b + 1)
                take_qk(b + 1)
            if kind != "relu2":
                weights(b)
            take_pT(b)
            take_oT(b)

        take_xT(0)
        take_qk(0)
        body(0, True)
        with act.Fori(1, last) as b:
            body(b, True)
        body(last, False)

    @block.vector
    def _(dve):
        step = Step(dve, s_step)
        nc.vector.memset(V[:, :], 1.0).then_inc(var_ready, 1)
        if normed == "layer":
            dve.wait_ge(std_ready, 1)
            nc.vector.reciprocal(rstd[:, :], std[:, :]).then_inc(rstd_ready, 1)
            dve.wait_ge(rstd_ready, 1)
        dve.wait_ge(var_ready, 1)
        dve.wait_ge(loaded, NL)
        if kind == "softmax":
            step.do(nc.vector.tensor_copy(mbc[:, :], m8[:, :].bitcast(U8)))
            nc.vector.tensor_scalar(fill[:, :], mbc[0:1, :], -1.0, 1e8 / score_scale, ALU.add, ALU.mult).then_inc(mask_ready, 1)
        if kind == "relu2":
            step.do(nc.vector.tensor_copy(keep[:, :], m8[:, :].bitcast(U8)))
            step.do(nc.vector.tensor_scalar(keep[:, :], keep[:, :], -1.0, 1.0, ALU.mult, ALU.add))

        def normalise(b):
            past(dve, xt_done, b)
            xb = G.x[:, bass.ds(b * D, D)]
            if normed == "layer":
                nc.vector.tensor_scalar(xn[:, :], xb, G.mv[:, bass.ds(b * 2, 1)], rstd[:, bass.ds(b, 1)],
                                        ALU.subtract, ALU.mult).then_inc(xn_ready, 1)
            else:
                nc.vector.tensor_scalar(xn[:, :], xb, G.rrms[:, bass.ds(b, 1)], None, ALU.mult).then_inc(xn_ready, 1)

        def features(b):
            if kind == "linear":
                dve.wait_ge(qk_done, b + 1)
                nc.vector.tensor_scalar(elu[:, :], psQK[:, :], 0.0, None, ALU.min).then_inc(elu_in, 1)
                dve.wait_ge(elu_out, b + 1)
                past(dve, s_done, b)
                past(dve, bd_ready, DC * b)
                nc.vector.scalar_tensor_tensor(qk[:, :], psQK[:, :], 0.0, elu[:, :], ALU.max, ALU.add)\
                    .then_inc(qk_ready, 1)
            if biased:
                dve.wait_ge(masked_ready, b + 1)
                for c in range(DC):
                    ins = nc.vector.scalar_tensor_tensor(
                        qk[:, (DC + c) * P:(DC + c + 1) * P], psQK[:, (DC + c) * P:(DC + c + 1) * P], bk[:, c:c + 1],
                        mbc[:, bass.ds(b * P, P)], ALU.add, ALU.mult)
                ins.then_inc(qk_ready, 1)

        def shift(b):
            S3 = psS[:, :].rearrange("p (h t) -> p h t", h=H)
            P3 = PT[:, :].rearrange("p (h t) -> p h t", h=H)
            if natural:
                dve.wait_ge(s_done, b + 1)
                step.do(nc.vector.tensor_reduce(mx[:, :], S3, AX.X, ALU.max))
                past(dve, pt_done, b)
                nc.vector.tensor_tensor(Pn[:, :].rearrange("p (h t) -> p h t", h=H), S3,
                                        mx[:, :].unsqueeze(2).to_broadcast([P, H, P]), ALU.subtract).then_inc(shifted, 1)
            if kind == "linear":
                dve.wait_ge(s_done, b + 1)
                past(dve, o_done, b)
                nc.vector.tensor_tensor(P3, S3, G.triu[:, :].unsqueeze(1).to_broadcast([P, H, P]), ALU.mult)\
                    .then_inc(pt_ready, 1)
            if kind == "relu2":
                dve.wait_ge(shifted, b + 1)
                nc.vector.tensor_tensor(P3, P3, keep[:, bass.ds(b * P, P)].unsqueeze(1).to_broadcast([P, H, P]),
                                        ALU.mult).then_inc(masked_ready, 1)

        def take_pT(b):
            if natural:
                dve.wait_ge(pt_done, b + 1)
                past(dve, o_done, b)
                nc.vector.tensor_copy(PT[:, 1024:2048], psS[:, 1024:2048]).then_inc(pt_ready, 1)

        def take_v(b):
            dve.wait_ge(v_done, b + 1)
            past(dve, o_done, b)
            nc.vector.tensor_copy(V[:, :].rearrange("p (h e) -> p h e", h=H)[:, :, 0:HD],
                                  psVY[:, 0:D].rearrange("p (h e) -> p h e", h=H)).then_inc(v_ready, 1)

        def normalise_o(b):
            dve.wait_ge(o_done, b + 1)
            O3 = psO[:, 0:H * (HD + 1)].rearrange("p (h e) -> p h e", h=H)
            if den_eps:
                step.do(nc.vector.tensor_scalar(rden[:, :], O3[:, :, HD], den_eps, None, ALU.add))
                step.do(nc.vector.reciprocal(rden[:, :], rden[:, :]))
            else:
                step.do(nc.vector.reciprocal(rden[:, :], O3[:, :, HD]))
            past(dve, ot_done, b)
            nc.vector.tensor_tensor(osb[:, :].rearrange("p (h e) -> p h e", h=H), O3[:, :, 0:HD],
                                    rden[:, :].unsqueeze(2).to_broadcast([P, H, HD]), ALU.mult).then_inc(osb_ready, 1)

        def add_y(b):
            dve.wait_ge(y_done, b + 1)
            xb = G.x[:, bass.ds(b * D, D)]
            nc.vector.tensor_tensor(xb, xb, psVY[:, D:2 * D], ALU.add).then_inc(x_ready, 1)
            dve.wait_ge(x_ready, b + 1)
            row_stats(nc, dve, step, G, b, st6, mv)

        def body(b, more):
            if more:
                normalise(b + 1)
            shift(b)
            if more:
                features(b + 1)
            take_pT(b)
            normalise_o(b)
            if more:
                take_v(b + 1)
            add_y(b)

        normalise(0)
        features(0)
        take_v(0)
        per = 3 + (1 if natural else 0) + (2 if den_eps else 1)
        body(0, True)
        with dve.Fori(1, last) as b:
            step.enter(b, per, start=1)
            body(b, True)
            step.leave(last - 1)
        body(last, False)

    R.close()
def normalised_transpose(nc, G, tag, xT, router=None, logits=None, router_bias=None):
    T, NPAIR, NBUF = NB * P, NB // 2, 4
    R = Region(nc, tag)
    rstd, std = R.sb("rstd", [P, NB]), R.sb("std", [P, NB])
    xn = [R.sb(f"xn{i}", [P, 2 * D]) for i in range(NBUF)]
    psX = [R.ps(f"psX{i}", [P, 512]) for i in range(NBUF)]
    std_ready, rstd_ready = R.sem("std_ready"), R.sem("rstd_ready")
    xn_ready, xt_done, xT_ready = R.sem("xn_ready"), R.sem("xT_done"), R.sem("xT_ready")
    if router is not None:
        rw, rb = R.sb("rw", [P, DC * 8]), R.sb("rb", [1, 8])
        psR = R.ps("psR", [P, 512])
        r_loaded, r_done, r_read = R.sem("router_loaded"), R.sem("router_done"), R.sem("router_read")
    block = R.block()
    NR = 0 if router is None else 16 + (16 if router_bias is not None else 0)

    @block.sync
    def _(sp):
        if router is not None:
            sp.dma_start(rw[:, :], router).then_inc(r_loaded, 16)
            if router_bias is not None:
                sp.dma_start(rb[:, :], router_bias).then_inc(r_loaded, 16)
            sp.wait_ge(r_loaded, NR)

    @block.vector
    def _(dve):
        dve.wait_ge(std_ready, 1)
        nc.vector.reciprocal(rstd[:, :], std[:, :]).then_inc(rstd_ready, 1)
        dve.wait_ge(rstd_ready, 1)
        for n in range(NPAIR):
            if n >= NBUF:
                dve.wait_ge(xt_done, n - NBUF + 1)
            for i in range(2):
                b = 2 * n + i
                ins = nc.vector.tensor_scalar(xn[n % NBUF][:, i * D:(i + 1) * D], G.x[:, b * D:(b + 1) * D], G.mv[:, 2 * b:2 * b + 1],
                                              rstd[:, b:b + 1], ALU.subtract, ALU.mult)
            ins.then_inc(xn_ready, 1)
        if router is not None:
            dve.wait_ge(r_done, 1)
            nc.vector.tensor_copy(logits[:, :], psR[:, 0:8 * NB]).then_inc(r_read, 1)
            dve.wait_ge(r_read, 1)

    @block.tensor
    def _(pe):
        def route(n):
            pe.wait_ge(xT_ready, n + 1)
            for b in (2 * n, 2 * n + 1):
                for c in range(DC):
                    last = nc.tensor.matmul(psR[:, b * 8:(b + 1) * 8], xT[:, c * T + b * P:c * T + (b + 1) * P], rw[:, c * 8:(c + 1) * 8],
                                            start=(c == 0), stop=(c == DC - 1 and router_bias is None))
                if router_bias is not None:
                    last = nc.tensor.matmul(psR[:, b * 8:(b + 1) * 8], G.ones_row[:, :], rb[:, :], start=False, stop=True)
            return last

        if router is not None:
            pe.wait_ge(r_loaded, NR)
        for n in range(NPAIR):
            pe.wait_ge(xn_ready, n + 1)
            if n >= NBUF:
                pe.wait_ge(xT_ready, n - NBUF + 1)
            for i in range(2):
                for c in range(DC):
                    last = nc.tensor.transpose(psX[n % NBUF][:, (c * 2 + i) * P:(c * 2 + i + 1) * P],
                                               xn[n % NBUF][:, i * D + c * P:i * D + (c + 1) * P], G.ident[:, :])
            last.then_inc(xt_done, 1)
            if router is not None and n >= 1:
                route(n - 1)
        if router is not None:
            route(NPAIR - 1).then_inc(r_done, 1)

    @block.scalar
    def _(act):
        nc.scalar.activation(std[:, :], variances(G), ACT.Sqrt, bias=G.neg1e5[:, 0:1]).then_inc(std_ready, 1)
        for n in range(NPAIR):
            act.wait_ge(xt_done, n + 1)
            nc.scalar.activation(xT[:, :].rearrange("p (c n) -> p c n", c=DC)[:, :, n * 2 * P:(n + 1) * 2 * P],
                                 psX[n % NBUF][:, :].rearrange("p (c t) -> p c t", c=DC), ACT.Copy).then_inc(xT_ready, 1)

    R.close()


def experts(nc, G, A, tag, softmax_router, shared):
    E, F = 8, 512
    FC = F // P
    WE = 2 * DC * F + FC * D
    n_experts = E + (1 if shared else 0)
    R = Region(nc, tag)
    xT = R.sb("xT", [P, DC * NB * P])
    prob, comb = R.sb("prob", [P, NB * E]), R.sb("comb", [P, (E + 1) * NB])
    st6 = R.sb("st6", [P, 6 * NB])
    normalised_transpose(nc, G, tag + "_n", xT, A[tag + "_router"], prob, A.get(tag + "_rbias"))

    W = [R.sb(f"W{i}", [P, WE]) for i in range(2)]
    t1, t2, oh1, oh2 = (R.sb(n, [P, NB * E]) for n in ("t1", "t2", "oh1", "oh2"))
    m1, m2, key = (R.sb(n, [P, NB]) for n in ("m1", "m2", "key"))
    order = R.sb("order", [P, E])
    sg = [R.sb(f"sg{i}", [P, GT]) for i in range(2)]
    hT = R.sb("hT", [P, FC * GT])
    psG = [R.ps(f"psG{i}", [P, GT]) for i in range(2)]
    psU = [R.ps(f"psU{i}", [P, GT]) for i in range(2)]
    psY = [R.ps(f"psY{i}", [P, 512]) for i in range(4)]
    w_loaded = [R.sem(f"weights{i}_loaded") for i in range(2)]
    gu_done, sg_ready, h_ready, y_done, y_used = (R.sem(n) for n in ("gate_up_done", "silu_ready", "h_ready", "y_done", "y_used"))
    order_ready, routed, a_ready = R.sem("order_ready"), R.sem("logits_shifted"), R.sem("prob_ready")
    s_step = R.sem("dve_step")
    block = R.block()

    @block.sync
    def _(sp):
        for e in range(n_experts):
            if e >= 2:
                sp.wait_ge(y_done, NG * (e - 1))
            sp.dma_start(W[e % 2][:, :], A[tag + "_w"][e]).then_inc(w_loaded[e % 2], 16)
        for i in range(2):
            sp.wait_ge(w_loaded[i], 16 * ((n_experts + 1 - i) // 2))

    @block.gpsimd
    def _(pool):
        for e in range(E):
            nc.gpsimd.memset(order[:, e:e + 1], float(E - e)).then_inc(order_ready, 1)

    def gate(i, c, j):
        return W[i][:, c * F + j * P:c * F + (j + 1) * P]

    def up(i, c, j):
        return W[i][:, DC * F + c * F + j * P:DC * F + c * F + (j + 1) * P]

    def down(i, j):
        return W[i][:, 2 * DC * F + j * D:2 * DC * F + (j + 1) * D]

    @block.tensor
    def _(pe):
        def group(n, g, i):
            for j in range(FC):
                pe.wait_ge(h_ready, n * FC + j + 1)
                for part, ps in ((gate, psG), (up, psU)):
                    for c in range(DC):
                        last = nc.tensor.matmul(ps[j % 2][:, :], part(i, c, j), xT[:, bass.ds(g * GT + c * NB * P, GT)],
                                                start=(c == 0), stop=(c == DC - 1))
                last.then_inc(gu_done, 1)
            pe.wait_ge(y_used, n + 1)
            for j in range(FC):
                pe.wait_ge(h_ready, n * FC + j + 3)
                for t in range(GB):
                    last = nc.tensor.matmul(psY[t][:, 0:D], hT[:, j * GT + t * P:j * GT + (t + 1) * P], down(i, j),
                                            start=(j == 0), stop=(j == FC - 1))
            last.then_inc(y_done, 1)

        with pe.Fori(0, E // 2) as ep:
            for i in range(2):
                with pe.Fori(0, NG) as g:
                    pe.wait_ge(w_loaded[i], ep * 16 + 16)
                    group(ep * (2 * NG) + (g + i * NG), g, i)
        if shared:
            pe.wait_ge(w_loaded[0], 16 * (E // 2 + 1))
            with pe.Fori(0, NG) as g:
                group(g + E * NG, g, 0)

    @block.scalar
    def _(act):
        act.wait_ge(routed, 1)
        nc.scalar.activation(prob[:, :], prob[:, :], ACT.Exp if softmax_router else ACT.Sigmoid).then_inc(a_ready, 1)

        def group(n):
            for j in range(FC):
                act.wait_ge(gu_done, n * FC + j + 1)
                act.wait_ge(h_ready, n * FC + j + 1)
                nc.scalar.activation(sg[j % 2][:, :], psG[j % 2][:, :], ACT.Silu).then_inc(sg_ready, 1)

        with act.Fori(0, n_experts * NG) as n:
            group(n)

    @block.vector
    def _(dve):
        step = Step(dve, s_step)
        p3, a3, b3 = (t[:, :].rearrange("p (b e) -> p b e", e=E) for t in (prob, t1, t2))
        o1, o2 = (t[:, :].rearrange("p (b e) -> p b e", e=E) for t in (oh1, oh2))
        order3 = order[:, :].unsqueeze(1).to_broadcast([P, NB, E])

        def wide(t):
            return t[:, :].unsqueeze(2).to_broadcast([P, NB, E])

        for i in range(2):
            nc.vector.memset(G.pad[:, 1 + i:2 + i], 0.0).then_inc(h_ready, 1)
        nc.vector.memset(G.pad[:, 3:4], 0.0).then_inc(y_used, 1)
        if softmax_router:
            step.do(nc.vector.tensor_reduce(m1[:, :], p3, AX.X, ALU.max))
            nc.vector.tensor_tensor(p3, p3, wide(m1), ALU.subtract).then_inc(routed, 1)
        else:
            nc.vector.memset(G.pad[:, 4:5], 0.0).then_inc(routed, 1)
        dve.wait_ge(a_ready, 1)
        if softmax_router:
            step.do(nc.vector.tensor_reduce(m1[:, :], p3, AX.X, ALU.add))
            step.do(nc.vector.reciprocal(m2[:, :], m1[:, :]))
            step.do(nc.vector.tensor_tensor(p3, p3, wide(m2), ALU.mult))
        dve.wait_ge(order_ready, E)

        def best(src, mx, tmp, hot):
            step.do(nc.vector.tensor_reduce(mx[:, :], src, AX.X, ALU.max))
            step.do(nc.vector.tensor_tensor(tmp, src, wide(mx), ALU.is_equal))
            step.do(nc.vector.tensor_tensor(tmp, tmp, order3, ALU.mult))
            step.do(nc.vector.tensor_reduce(key[:, :], tmp, AX.X, ALU.max))
            step.do(nc.vector.tensor_tensor(hot, tmp, wide(key), ALU.is_equal))

        best(p3, m1, a3, o1)
        step.do(nc.vector.scalar_tensor_tensor(t2[:, :], oh1[:, :], -2.0, prob[:, :], ALU.mult, ALU.add))
        best(b3, m2, a3, o2)
        step.do(nc.vector.tensor_tensor(m1[:, :], m1[:, :], m2[:, :], ALU.add))
        step.do(nc.vector.reciprocal(m1[:, :], m1[:, :]))
        step.do(nc.vector.tensor_tensor(o1, o1, o2, ALU.add))
        step.do(nc.vector.tensor_tensor(o1, o1, p3, ALU.mult))
        step.sig(nc.vector.tensor_tensor(comb[:, 0:E * NB].rearrange("p (e b) -> p b e", e=E), o1, wide(m1), ALU.mult))
        step.do(nc.vector.memset(comb[:, E * NB:], 1.0))

        def group(n, g, col):
            for j in range(FC):
                dve.wait_ge(sg_ready, n * FC + j + 1)
                nc.vector.tensor_tensor(hT[:, j * GT:(j + 1) * GT], sg[j % 2][:, :], psU[j % 2][:, :], ALU.mult)\
                    .then_inc(h_ready, 1)
            dve.wait_ge(y_done, n + 1)
            for t in range(GB):
                xb = G.x[:, bass.ds(g * (GB * D) + t * D, D)]
                last = nc.vector.scalar_tensor_tensor(xb, psY[t][:, 0:D], comb[:, bass.ds(col + t, 1)], xb, ALU.mult, ALU.add)
            last.then_inc(y_used, 1)

        with dve.Fori(0, E // 2) as ep:
            for i in range(2):
                with dve.Fori(0, NG) as g:
                    group(ep * (2 * NG) + (g + i * NG), g, ep * (2 * NB) + (g * GB + i * NB))
        if shared:
            with dve.Fori(0, NG) as g:
                group(g + E * NG, g, g * GB + E * NB)
        dve.wait_ge(y_used, n_experts * NG + 1)
        all_row_stats(nc, dve, step, G, st6)

    R.close()
RMS_EPS = 1.1920929e-07
SC, ST = 64, 16


def rms_factors(nc, G, tag):
    R = Region(nc, tag)
    ms, rt, eps = R.sb("ms", [P, NB]), R.sb("rt", [P, NB]), R.sb("eps", [P, 1])
    s_step, ms_ready, root_ready = R.sem("dve_step"), R.sem("ms_ready"), R.sem("root_ready")
    block = R.block()

    @block.vector
    def _(dve):
        step = Step(dve, s_step)
        step.do(nc.vector.memset(eps[:, :], RMS_EPS))
        step.do(nc.vector.tensor_tensor(ms[:, :], means(G), means(G), ALU.mult))
        nc.vector.tensor_tensor(ms[:, :], ms[:, :], variances(G), ALU.add).then_inc(ms_ready, 1)
        dve.wait_ge(root_ready, 1)
        step.do(nc.vector.reciprocal(G.rrms[:, :], rt[:, :]))

    @block.scalar
    def _(act):
        act.wait_ge(ms_ready, 1)
        nc.scalar.activation(rt[:, :], ms[:, :], ACT.Sqrt, bias=eps[:, 0:1]).then_inc(root_ready, 1)

    R.close()


def normalise_in_place(nc, G, tag, saved):
    R = Region(nc, tag)
    rstd, std = R.sb("rstd", [P, NB]), R.sb("std", [P, NB])
    s_step, std_ready, saved_ready, x_ready = R.sem("dve_step"), R.sem("std_ready"), R.sem("saved"), R.sem("x_ready")
    block = R.block()

    @block.scalar
    def _(act):
        nc.scalar.activation(std[:, :], variances(G), ACT.Sqrt, bias=G.neg1e5[:, 0:1]).then_inc(std_ready, 1)
        for g in range(NG):
            xg = slice(g * GB * D, (g + 1) * GB * D)
            nc.scalar.activation(saved[:, xg], G.x[:, xg], ACT.Copy).then_inc(saved_ready, 1)

    @block.vector
    def _(dve):
        step = Step(dve, s_step)
        dve.wait_ge(std_ready, 1)
        step.do(nc.vector.reciprocal(rstd[:, :], std[:, :]))
        for b in range(NB):
            if b % GB == 0:
                dve.wait_ge(saved_ready, b // GB + 1)
            xb = G.x[:, b * D:(b + 1) * D]
            nc.vector.tensor_scalar(xb, xb, G.mv[:, b * 2:b * 2 + 1], rstd[:, b:b + 1], ALU.subtract, ALU.mult).then_inc(x_ready, 1)
        dve.wait_ge(x_ready, NB)
        step.do(nc.vector.tensor_tensor(variances(G), variances(G), rstd[:, :], ALU.mult))
        step.do(nc.vector.tensor_tensor(variances(G), variances(G), rstd[:, :], ALU.mult))
        step.do(nc.vector.memset(means(G), 0.0))

    R.close()


def selective_scan(nc, G, A, saved):
    NP2 = NB // 2
    R = Region(nc, "scan")
    inw, gatew = R.sb("inw", [P, DC * SC]), R.sb("gatew", [P, DC * SC])
    dtw, dtb, outw = R.sb("dtw", [P, P]), R.sb("dtb", [P, 1]), R.sb("outw", [P, D])
    bp, cp, alog = R.sb("bp", [P, ST]), R.sb("cp", [P, ST]), R.sb("alog", [P, ST])
    nw, Am = R.sb("nw", [P, DC]), R.sb("Am", [P, ST])
    bdB, bdC = R.sb("bdB", [P, ST * P]), R.sb("bdC", [P, ST * P])
    xn, hT = R.sb("xn", [P, 2 * D]), R.sb("hT", [P, 2 * D])
    zg = R.sb("zg", [P, 2 * P])
    v, av, ev, lv, dt, dtz = (R.sb(n, [P, P]) for n in ("v", "av", "ev", "lv", "dt", "dtz"))
    eg, rg, gg, y, yT = (R.sb(n, [P, P]) for n in ("eg", "rg", "gg", "y", "yT"))
    ab, u, st = R.sb("abar", [P, ST * P]), R.sb("u", [P, ST * P]), R.sb("states", [P, ST * P])
    st6, mv = R.sb("st6", [P, 6]), R.sb("mv", [P, 2])
    psX, psZ, psY0, psY1 = (R.ps(n, [P, 512]) for n in ("psX", "psZ", "psY0", "psY1"))
    psY = (psY0, psY1)
    psB = R.ps("psB", [P, ST * P])
    S = Shared()
    S.dt_sum = R.sem("dt_sum")
    dt0, later = R.sb("dt0", [P, P]), R.sb("later", [P, P])
    S.loaded, S.zeroed, S.dt_loaded, S.aexp_ready = (R.sem(n) for n in ("loaded", "zeroed", "dt_loaded", "aexp_ready",))
    S.consts_ready, S.xn_ready, S.xT_done, S.hT_ready = (R.sem(n) for n in ("consts_ready", "xn_ready", "xT_done", "hT_ready",))
    S.z_done, S.z_ready, S.dt_done, S.b_done = (R.sem(n) for n in ("z_done", "z_ready", "dt_done", "b_done",))
    S.v_ready, S.abs_ready, S.log_ready, S.exp_ready = (R.sem(n) for n in ("v_ready", "abs_ready", "log_ready", "exp_ready",))
    S.dt_ready, S.abar_ready, S.u_ready, S.c_done = (R.sem(n) for n in ("dt_ready", "abar_ready", "u_ready", "c_done",))
    S.yT_ready, S.y_done, S.summed, S.x_ready = (R.sem(n) for n in ("yT_ready", "y_done", "summed", "x_ready",))
    S.state_used, S.gate_exp, S.bias_ready, S.scanned = (R.sem(n) for n in ("state_used", "gate_exp", "bias_ready", "scanned",))
    s_step, a_step, p_step = R.sem("dve_step"), R.sem("act_step"), R.sem("pool_step")
    block = R.block()
    loads = [(inw, A["l1s_in"]), (gatew, A["l1s_gate"]), (dtb, A["l1s_dtb"]), (outw, A["l1s_out"]), (bp, A["l1s_B"]),
             (cp, A["l1s_C"]), (alog, A["l1s_Alog"]), (nw, A["l1s_norm"])]
    NL = 16 * len(loads)

    @block.sync
    def _(sp):
        for dst, src in loads:
            sp.dma_start(dst[:, :], src).then_inc(S.loaded, 16)
        sp.wait_ge(S.zeroed, 3)
        for i in range(2):
            sp.dma_start(dtw[i * SC:(i + 1) * SC, i * SC:(i + 1) * SC], A["l1s_dtw"]).then_inc(S.dt_loaded, 16)
        sp.wait_ge(S.dt_loaded, 32)

    @block.gpsimd
    def _(pool):
        step = Step(pool, p_step)
        for t in (bdB, bdC, dtw):
            nc.gpsimd.memset(t[:, :], 0.0).then_inc(S.zeroed, 1)
        step.do(nc.gpsimd.memset(later[:, :], 1.0))
        nc.gpsimd.memset(later[:, 0:1], 0.0).then_inc(S.zeroed, 1)
        pool.wait_ge(S.zeroed, 4)

        def body(p):
            pool.wait_ge(S.xn_ready, 2 * p + 2)
            xp = G.x[:, bass.ds(p * (2 * D), 2 * D)]
            nc.gpsimd.tensor_tensor(xp, xp, saved[:, bass.ds(p * (2 * D), 2 * D)], ALU.add).then_inc(S.summed, 1)
            pool.wait_ge(S.dt_ready, p + 1)
            past(pool, S.scanned, p)
            ab3 = ab[:, :].rearrange("p (s t) -> p s t", s=ST)
            step.do(nc.gpsimd.tensor_tensor(ab3, dt0[:, :].unsqueeze(1).to_broadcast([P, ST, P]),
                                            Am[:, :].unsqueeze(2).to_broadcast([P, ST, P]), ALU.mult))
            nc.gpsimd.tensor_tensor(ab3, ab3, later[:, :].unsqueeze(1).to_broadcast([P, ST, P]), ALU.add).then_inc(S.abar_ready, 1)

        pool.wait_ge(S.consts_ready, 3)
        body(0)
        with pool.Fori(1, NP2) as p:
            step.enter(p, 1, start=1)
            body(p)
            step.leave(NP2 - 1)

    @block.tensor
    def _(pe):
        pe.wait_ge(S.loaded, NL)
        pe.wait_ge(S.dt_loaded, 32)
        pe.wait_ge(S.consts_ready, 3)

        def body(p):
            pe.wait_ge(S.xn_ready, 2 * p + 2)
            for c in range(DC):
                for i in range(2):
                    last = nc.tensor.transpose(psX[:, (c * 2 + i) * P:(c * 2 + i + 1) * P],
                                               xn[:, i * D + c * P:i * D + (c + 1) * P], G.ident[:, :])
            last.then_inc(S.xT_done, 1)
            pe.wait_ge(S.hT_ready, p + 1)
            for k, w in enumerate((inw, gatew)):
                for i in range(2):
                    for c in range(DC):
                        last = nc.tensor.matmul(psZ[i * SC:(i + 1) * SC, k * P:(k + 1) * P], w[:, c * SC:(c + 1) * SC],
                                                hT[:, (c * 2 + i) * P:(c * 2 + i + 1) * P], start=(c == 0), stop=(c == DC - 1))
            last.then_inc(S.z_done, 1)
            pe.wait_ge(S.z_ready, p + 1)
            nc.tensor.matmul(psZ[:, 2 * P:3 * P], dtw[:, :], zg[:, 0:P], start=True, stop=True).then_inc(S.dt_done, 1)
            past(pe, S.state_used, p)
            for s in range(ST):
                last = nc.tensor.matmul(psB[:, s * P:(s + 1) * P], bdB[:, s * P:(s + 1) * P], zg[:, 0:P], start=True, stop=True)
            last.then_inc(S.b_done, 1)
            pe.wait_ge(S.u_ready, p + 1)
            for s in range(ST):
                last = nc.tensor.matmul(psB[:, s * P:(s + 1) * P], bdC[:, s * P:(s + 1) * P], zg[:, 0:P], start=True, stop=True)
            last.then_inc(S.c_done, 1)
            pe.wait_ge(S.yT_ready, p + 1)
            for i in range(2):
                last = nc.tensor.matmul(psY[i][:, 0:D], yT[i * SC:(i + 1) * SC, :], outw[i * SC:(i + 1) * SC, :],
                                        start=True, stop=True)
            last.then_inc(S.y_done, 1)

        body(0)
        with pe.Fori(1, NP2) as p:
            body(p)

    @block.scalar
    def _(act):
        step = Step(act, a_step)
        act.wait_ge(S.loaded, NL)
        nc.scalar.activation(alog[:, :], alog[:, :], ACT.Exp).then_inc(S.aexp_ready, 1)

        def body(p):
            act.wait_ge(S.xT_done, p + 1)
            for c in range(DC):
                ins = nc.scalar.activation(hT[:, c * D:(c + 1) * D], psX[:, c * D:(c + 1) * D], ACT.Copy, scale=nw[:, c:c + 1])
            ins.then_inc(S.hT_ready, 1)
            act.wait_ge(S.z_done, p + 1)
            past(act, S.yT_ready, p)
            nc.scalar.activation(zg[:, :], psZ[:, 0:2 * P], ACT.Copy).then_inc(S.z_ready, 1)
            act.wait_ge(S.z_ready, p + 1)
            nc.scalar.activation(eg[:, :], zg[:, P:2 * P], ACT.Exp, scale=-1.0).then_inc(S.gate_exp, 1)
            act.wait_ge(S.dt_done, p + 1)
            nc.scalar.activation(v[:, :], psZ[:, 2 * P:3 * P], ACT.Identity, bias=dtb[:, 0:1]).then_inc(S.v_ready, 1)
            act.wait_ge(S.abs_ready, p + 1)
            nc.scalar.activation(ev[:, :], av[:, :], ACT.Exp, scale=-1.0).then_inc(S.exp_ready, 1)
            act.wait_ge(S.exp_ready, p + 1)
            nc.scalar.activation(lv[:, :], ev[:, :], ACT.Ln, bias=1.0).then_inc(S.log_ready, 1)

        body(0)
        with act.Fori(1, NP2) as p:
            body(p)

    @block.vector
    def _(dve):
        step = Step(dve, s_step)
        dve.wait_ge(S.loaded, NL)
        dve.wait_ge(S.zeroed, 4)
        dve.wait_ge(S.aexp_ready, 1)
        for big, small in ((bdB, bp), (bdC, cp)):
            for i in range(2):
                ins = nc.vector.tensor_copy(big[:, :].rearrange("p (s r) -> p s r", s=ST)[i * SC:(i + 1) * SC, :, i * SC:(i + 1) * SC],
                                            small[i * SC:(i + 1) * SC, :].unsqueeze(2).to_broadcast([SC, ST, SC]))
            ins.then_inc(S.consts_ready, 1)
        nc.vector.tensor_scalar(Am[:, :], alog[:, :], -1.0, None, ALU.mult).then_inc(S.consts_ready, 1)

        def body(p):
            past(dve, S.xT_done, p)
            for i in range(2):
                b = p * 2 + i
                nc.vector.tensor_scalar(xn[:, i * D:(i + 1) * D], G.x[:, bass.ds(b * D, D)], G.rrms[:, bass.ds(b, 1)], None,
                                        ALU.mult).then_inc(S.xn_ready, 1)
            dve.wait_ge(S.v_ready, p + 1)
            nc.vector.scalar_tensor_tensor(av[:, :], v[:, :], -1.0, v[:, :], ALU.mult, ALU.max).then_inc(S.abs_ready, 1)
            dve.wait_ge(S.gate_exp, p + 1)
            step.do(nc.vector.tensor_scalar(rg[:, :], eg[:, :], 1.0, None, ALU.add))
            step.do(nc.vector.reciprocal(rg[:, :], rg[:, :]))
            step.sig(nc.vector.tensor_tensor(gg[:, :], zg[:, P:2 * P], rg[:, :], ALU.mult))
            dve.wait_ge(S.log_ready, p + 1)
            past(dve, S.abar_ready, p)
            nc.vector.scalar_tensor_tensor(dt[:, :], v[:, :], 0.0, lv[:, :], ALU.max, ALU.add).then_inc(S.dt_sum, 1)
            dve.wait_ge(S.dt_sum, p + 1)
            nc.vector.tensor_tensor(dt0[:, :], dt[:, :], later[:, :], ALU.mult).then_inc(S.dt_ready, 1)
            step.do(nc.vector.tensor_tensor(dtz[:, :], dt[:, :], zg[:, 0:P], ALU.mult))
            dve.wait_ge(S.b_done, p + 1)
            nc.vector.tensor_tensor(u[:, :].rearrange("p (s t) -> p s t", s=ST), psB[:, :].rearrange("p (s t) -> p s t", s=ST),
                                    dtz[:, :].unsqueeze(1).to_broadcast([P, ST, P]), ALU.mult).then_inc(S.u_ready, 1)
            dve.wait_ge(S.u_ready, p + 1)
            dve.wait_ge(S.abar_ready, p + 1)
            nc.vector.tensor_tensor_scan(st[:, :], ab[:, :], u[:, :], 0.0, ALU.mult, ALU.add).then_inc(S.scanned, 1)
            dve.wait_ge(S.scanned, p + 1)
            dve.wait_ge(S.c_done, p + 1)
            nc.vector.tensor_tensor(u[:, :], st[:, :], psB[:, :], ALU.mult).then_inc(S.state_used, 1)
            dve.wait_ge(S.state_used, p + 1)
            step.do(nc.vector.tensor_reduce(y[:, :], u[:, :].rearrange("p (s t) -> p t s", s=ST), AX.X, ALU.add))
            nc.vector.tensor_tensor(yT[:, :], y[:, :], gg[:, :], ALU.mult).then_inc(S.yT_ready, 1)
            dve.wait_ge(S.y_done, p + 1)
            dve.wait_ge(S.summed, p + 1)
            for i in range(2):
                xb = G.x[:, bass.ds(p * (2 * D) + i * D, D)]
                nc.vector.tensor_tensor(xb, xb, psY[i][:, 0:D], ALU.add).then_inc(S.x_ready, 1)
            dve.wait_ge(S.x_ready, 2 * p + 2)
            for i in range(2):
                row_stats(nc, dve, step, G, p * 2 + i, st6, mv)

        body(0)
        with dve.Fori(1, NP2) as p:
            step.enter(p, 11, start=1)
            body(p)
            step.leave(NP2 - 1)

    R.close()


def l1_attention(nc, G, A):
    R = Region(nc, "l1a")
    saved = R.sb("saved", [P, NB * D])
    normalise_in_place(nc, G, "l1a_ln", saved)
    rms_factors(nc, G, "l1a_rms1")
    attention16(nc, G, A, "l1a_att", "causal", "l1a_", normed="rms")
    rms_factors(nc, G, "l1a_rms2")
    selective_scan(nc, G, A, saved)
    R.close()
def wide_attention(nc, G, A):
    W = 64
    IN = H * W
    IC = IN // P
    VW = W + 1
    R = Region(nc, "l2a")
    xT = R.sb("xT", [P, DC * NB * P])
    normalised_transpose(nc, G, "l2a_n", xT)
    wq, wk, wv = (R.sb(n, [P, DC * IN]) for n in ("wq", "wk", "wv"))
    wo, bo = R.sb("wo", [P, IC * D]), R.sb("bo", [1, D])
    st6, mv = R.sb("st6", [P, 6]), R.sb("mv", [P, 2])
    xs = R.sb("xs", [P, D])
    qk = R.sb("qk", [P, 2 * IN])
    V = R.sb("V", [P, H * VW])
    Pn, PT = R.sb("Pn", [P, H * P]), R.sb("PT", [P, H * P])
    osb, oT = R.sb("osb", [P, IN]), R.sb("oT", [P, IN])
    mx, rden = R.sb("mx", [P, H]), R.sb("rden", [P, H])
    psS, psB = R.ps("psS", [P, 2048]), R.ps("psB", [P, 2048])
    loaded, ones_ready = R.sem("weights_loaded"), R.sem("ones_ready")
    xs_ready, qk_done, qk_ready, s_done, v_done, v_ready = (R.sem(n) for n in (
        "xs_ready", "qk_done", "qk_ready", "scores_done", "v_done", "v_ready"))
    shifted, p_ready, pt_done, pt_half, pt_ready = (R.sem(n) for n in ("shifted", "p_ready", "pT_done", "pT_half", "pT_ready"))
    o_done, osb_ready, ot_done, ot_ready, y_done, x_ready = (R.sem(n) for n in (
        "o_done", "o_ready", "oT_done", "oT_ready", "y_done", "x_ready"))
    s_step = R.sem("dve_step")
    block = R.block()
    loads = [(wq, A["l2a_Wq"]), (wk, A["l2a_Wk"]), (wv, A["l2a_Wv"]), (wo, A["l2a_Wo"]), (bo, A["l2a_bo"])]
    NL = 16 * len(loads)
    last = NB - 1

    def col(h):
        return (h % 2) * 1024 + (h // 2) * P

    @block.sync
    def _(sp):
        for dst, src in loads:
            sp.dma_start(dst[:, :], src).then_inc(loaded, 16)
        sp.wait_ge(loaded, NL)

    @block.gpsimd
    def _(pool):
        def stage(b):
            past(pool, v_done, b)
            nc.gpsimd.tensor_copy(xs[:, :].rearrange("p (c t) -> p c t", c=DC),
                                  xT[:, :].rearrange("p (c n) -> p c n", c=DC)[:, :, bass.ds(b * P, P)]).then_inc(xs_ready, 1)

        stage(0)
        with pool.Fori(1, NB) as b:
            stage(b)

    @block.tensor
    def _(pe):
        pe.wait_ge(loaded, NL)
        pe.wait_ge(ones_ready, 1)

        def project_qk(b):
            past(pe, v_ready, b)
            for i, w in enumerate((wq, wk)):
                for j in range(IC):
                    for c in range(DC):
                        ins = nc.tensor.matmul(psB[:, i * IN + j * P:i * IN + (j + 1) * P], w[:, c * IN + j * P:c * IN + (j + 1) * P],
                                               xT[:, bass.ds(b * P + c * NB * P, P)], start=(c == 0), stop=(c == DC - 1))
            ins.then_inc(qk_done, 1)

        def scores(b):
            pe.wait_ge(qk_ready, b + 1)
            past(pe, x_ready, b)
            for g in range(4):
                nc.tensor.matmul(psS[:, g * 512:(g + 1) * 512], G.identb[:, :],
                                 G.neg_upper[:, :].unsqueeze(1).to_broadcast([P, 4, P]), start=True, stop=False)
            for h in range(H):
                r, j = (h % 2) * W, (h // 2) * P
                ins = nc.tensor.matmul(psS[:, col(h):col(h) + P], qk[r:r + W, j:j + P], qk[r:r + W, IN + j:IN + j + P],
                                       start=False, stop=(h // 2 % 4 == 3))
            ins.then_inc(s_done, 1)

        def project_v(b):
            pe.wait_ge(xs_ready, b + 1)
            for n in range(2):
                for c in range(DC):
                    ins = nc.tensor.matmul(psB[:, n * 512:(n + 1) * 512], xs[:, c * P:(c + 1) * P],
                                           wv[:, c * IN + n * 512:c * IN + (n + 1) * 512], start=(c == 0), stop=(c == DC - 1))
            ins.then_inc(v_done, 1)

        def rest(b, more):
            pe.wait_ge(p_ready, b + 1)
            for h in range(H):
                ins = nc.tensor.transpose(psS[:, col(h):col(h) + P], Pn[:, col(h):col(h) + P], G.ident[:, :])
            ins.then_inc(pt_done, 1)
            pe.wait_ge(v_ready, b + 1)
            if more:
                pe.wait_ge(qk_ready, b + 2)
            pe.wait_ge(pt_half, b + 1)
            pe.wait_ge(pt_ready, b + 1)
            for h in range(H):
                o = (h // 4) * 512 + (h % 4) * VW
                ins = nc.tensor.matmul(psB[:, o:o + VW], PT[:, col(h):col(h) + P], V[:, h * VW:(h + 1) * VW], start=True, stop=True)
            ins.then_inc(o_done, 1)
            pe.wait_ge(osb_ready, b + 1)
            for j in range(IC):
                ins = nc.tensor.transpose(psB[:, j * P:(j + 1) * P], osb[:, j * P:(j + 1) * P], G.ident[:, :])
            ins.then_inc(ot_done, 1)
            pe.wait_ge(ot_ready, b + 1)
            for j in range(IC):
                nc.tensor.matmul(psS[:, 0:D], oT[:, j * P:(j + 1) * P], wo[:, j * D:(j + 1) * D], start=(j == 0), stop=False)
            nc.tensor.matmul(psS[:, 0:D], G.ones_row[:, :], bo[:, :], start=False, stop=True).then_inc(y_done, 1)

        def body(b, more):
            scores(b)
            project_v(b)
            if more:
                project_qk(b + 1)
            rest(b, more)

        project_qk(0)
        body(0, True)
        with pe.Fori(1, last) as b:
            body(b, True)
        body(last, False)

    @block.scalar
    def _(act):
        def take_qk(b):
            act.wait_ge(qk_done, b + 1)
            past(act, s_done, b)
            nc.scalar.activation(qk[:, :], psB[:, :], ACT.Copy).then_inc(qk_ready, 1)

        def body(b, more):
            act.wait_ge(v_done, b + 1)
            past(act, o_done, b)
            nc.scalar.activation(V[:, :].rearrange("p (h e) -> p h e", h=H)[:, :, 0:W],
                                 psB[:, 0:IN].rearrange("p (h e) -> p h e", h=H), ACT.Copy).then_inc(v_ready, 1)
            act.wait_ge(shifted, b + 1)
            nc.scalar.activation(Pn[:, :], Pn[:, :], ACT.Exp, scale=W ** -0.5).then_inc(p_ready, 1)
            if more:
                take_qk(b + 1)
            act.wait_ge(pt_done, b + 1)
            nc.scalar.activation(PT[:, 0:1024], psS[:, 0:1024], ACT.Copy).then_inc(pt_half, 1)
            act.wait_ge(ot_done, b + 1)
            past(act, y_done, b)
            nc.scalar.activation(oT[:, :], psB[:, 0:IN], ACT.Copy).then_inc(ot_ready, 1)

        take_qk(0)
        body(0, True)
        with act.Fori(1, last) as b:
            body(b, True)
        body(last, False)

    @block.vector
    def _(dve):
        step = Step(dve, s_step)
        nc.vector.memset(V[:, :], 1.0).then_inc(ones_ready, 1)
        dve.wait_ge(ones_ready, 1)

        def body(b):
            S3 = psS[:, :].rearrange("p (h t) -> p h t", h=H)
            dve.wait_ge(s_done, b + 1)
            step.do(nc.vector.tensor_reduce(mx[:, :], S3, AX.X, ALU.max))
            past(dve, pt_done, b)
            nc.vector.tensor_tensor(Pn[:, :].rearrange("p (h t) -> p h t", h=H), S3,
                                    mx[:, :].unsqueeze(2).to_broadcast([P, H, P]), ALU.subtract).then_inc(shifted, 1)
            dve.wait_ge(pt_done, b + 1)
            past(dve, o_done, b)
            nc.vector.tensor_copy(PT[:, 1024:2048], psS[:, 1024:2048]).then_inc(pt_ready, 1)
            dve.wait_ge(o_done, b + 1)
            O4 = psB[:, :].rearrange("p (k n) -> p k n", k=4)[:, :, 0:4 * VW].rearrange("p k (h e) -> p k h e", h=4)
            step.do(nc.vector.reciprocal(rden[:, :].rearrange("p (k h) -> p k h", k=4), O4[:, :, :, W]))
            past(dve, ot_done, b)
            for k in range(4):
                ins = nc.vector.tensor_tensor(osb[:, k * 4 * W:(k + 1) * 4 * W].rearrange("p (h e) -> p h e", h=4), O4[:, k, :, 0:W],
                                              rden[:, 4 * k:4 * k + 4].unsqueeze(2).to_broadcast([P, 4, W]), ALU.mult)
            ins.then_inc(osb_ready, 1)
            dve.wait_ge(y_done, b + 1)
            xb = G.x[:, bass.ds(b * D, D)]
            nc.vector.tensor_tensor(xb, xb, psS[:, 0:D], ALU.add).then_inc(x_ready, 1)
            dve.wait_ge(x_ready, b + 1)
            row_stats(nc, dve, step, G, b, st6, mv)

        body(0)
        with dve.Fori(1, NB) as b:
            step.enter(b, 5, start=1)
            body(b)
            step.leave(NB - 1)

    R.close()


def memory_attention(nc, G, A):
    SCALE = 0.4 * 0.6
    R = Region(nc, "l2x")
    xT = R.sb("xT", [P, DC * NB * P])
    normalised_transpose(nc, G, "l2x_n", xT)
    ctx = R.sb("ctx", [P, NB * D])
    st6, mv = R.sb("st6", [P, 6]), R.sb("mv", [P, 2])
    xs = R.sb("xs", [P, 2 * D])
    Pn, PT = R.sb("Pn", [P, 2 * P]), R.sb("PT", [P, 2 * P])
    mx, nmx, den, rden = (R.sb(n, [P, 2]) for n in ("mx", "nmx", "den", "rden"))
    psS, psT, psO = (R.ps(n, [P, 512]) for n in ("psS", "psT", "psO"))
    loaded, xs_ready, s_done, max_ready, p_ready, pt_done, pt_ready, o_done, x_ready = (R.sem(n) for n in (
        "ctx_loaded", "xs_ready", "scores_done", "max_ready", "p_ready", "pT_done", "pT_ready", "o_done", "x_ready"))
    s_step = R.sem("dve_step")
    block = R.block()
    NP2 = NB // 2

    @block.sync
    def _(sp):
        sp.dma_start(ctx[:, :].rearrange("p (b d) -> p b d", b=NB), A["ctx"].rearrange("b p d -> p b d")).then_inc(loaded, 16)
        sp.wait_ge(loaded, 16)

    @block.gpsimd
    def _(pool):
        def stage(p):
            past(pool, s_done, p)
            nc.gpsimd.tensor_copy(xs[:, :].rearrange("p (c t) -> p c t", c=DC),
                                  xT[:, :].rearrange("p (c n) -> p c n", c=DC)[:, :, bass.ds(p * 2 * P, 2 * P)])\
                .then_inc(xs_ready, 1)

        stage(0)
        with pool.Fori(1, NP2) as p:
            stage(p)

    @block.tensor
    def _(pe):
        pe.wait_ge(loaded, 16)

        def body(p):
            pe.wait_ge(xs_ready, p + 1)
            past(pe, p_ready, p)
            for i in range(2):
                for c in range(DC):
                    ins = nc.tensor.matmul(psS[:, i * P:(i + 1) * P], xs[:, c * 2 * P + i * P:c * 2 * P + (i + 1) * P],
                                           G.ctxT[:, bass.ds(p * 2 * P + (c * NB + i) * P, P)], start=(c == 0), stop=(c == DC - 1))
            ins.then_inc(s_done, 1)
            pe.wait_ge(p_ready, p + 1)
            for i in range(2):
                ins = nc.tensor.transpose(psT[:, i * P:(i + 1) * P], Pn[:, i * P:(i + 1) * P], G.ident[:, :])
            ins.then_inc(pt_done, 1)
            pe.wait_ge(pt_ready, p + 1)
            past(pe, x_ready, p)
            for i in range(2):
                ins = nc.tensor.matmul(psO[:, i * D:(i + 1) * D], PT[:, i * P:(i + 1) * P], ctx[:, bass.ds(p * 2 * D + i * D, D)],
                                       start=True, stop=True)
            ins.then_inc(o_done, 1)

        body(0)
        with pe.Fori(1, NP2) as p:
            body(p)

    @block.scalar
    def _(act):
        def body(p):
            act.wait_ge(max_ready, p + 1)
            past(act, pt_done, p)
            for i in range(2):
                ins = nc.scalar.activation(Pn[:, i * P:(i + 1) * P], psS[:, i * P:(i + 1) * P], ACT.Exp, scale=SCALE,
                                           bias=nmx[:, i:i + 1], accum_out=den[:, i:i + 1])
            ins.then_inc(p_ready, 1)
            act.wait_ge(pt_done, p + 1)
            past(act, o_done, p)
            nc.scalar.activation(PT[:, :], psT[:, 0:2 * P], ACT.Copy).then_inc(pt_ready, 1)

        body(0)
        with act.Fori(1, NP2) as p:
            body(p)

    @block.vector
    def _(dve):
        step = Step(dve, s_step)
        dve.wait_ge(loaded, 16)

        def body(p):
            dve.wait_ge(s_done, p + 1)
            step.do(nc.vector.tensor_reduce(mx[:, :], psS[:, 0:2 * P].rearrange("p (i t) -> p i t", i=2), AX.X, ALU.max))
            nc.vector.tensor_scalar(nmx[:, :], mx[:, :], -SCALE, None, ALU.mult).then_inc(max_ready, 1)
            dve.wait_ge(p_ready, p + 1)
            step.do(nc.vector.reciprocal(rden[:, :], den[:, :]))
            step.do(nc.vector.tensor_scalar(rden[:, :], rden[:, :], 0.6, None, ALU.mult))
            xp, cp = G.x[:, bass.ds(p * 2 * D, 2 * D)], ctx[:, bass.ds(p * 2 * D, 2 * D)]
            step.do(nc.vector.tensor_tensor(xp, xp, cp, ALU.add))
            dve.wait_ge(o_done, p + 1)
            for i in range(2):
                xb = G.x[:, bass.ds(p * 2 * D + i * D, D)]
                ins = nc.vector.scalar_tensor_tensor(xb, psO[:, i * D:(i + 1) * D], rden[:, i:i + 1], xb, ALU.mult, ALU.add)
            ins.then_inc(x_ready, 1)
            dve.wait_ge(x_ready, p + 1)
            for i in range(2):
                row_stats(nc, dve, step, G, p * 2 + i, st6, mv)

        body(0)
        with dve.Fori(1, NP2) as p:
            step.enter(p, 10, start=1)
            body(p)
            step.leave(NP2 - 1)

    R.close()


MAGIC = 1.5 * 2.0 ** 23
TWO_PI = float(2.0 * np.pi)


def phase_ffn(nc, G, A):
    F = 1024
    FC = F // P
    INV = 1.0 / TWO_PI
    R = Region(nc, "l2f")
    xT = R.sb("xT", [P, DC * NB * P])
    normalised_transpose(nc, G, "l2f_n", xT)
    w1, w2 = R.sb("w1", [P, DC * F]), R.sb("w2", [P, FC * D])
    b1, theta, wr, wi = (R.sb(n, [P, FC]) for n in ("b1", "theta", "wr", "wi"))
    b2 = R.sb("b2", [1, D])
    turn, tb, ang, rnd, sc, coef = R.sb("turn", [P, FC]), R.sb("tb", [P, FC]), R.sb("ang", [P, 2 * FC]), R.sb("rnd", [P, 2 * FC]), \
        R.sb("sc", [P, 2 * FC]), R.sb("coef", [P, FC])
    hb, yt, kt, ft, sn, q = ([R.sb(f"{n}{i}", [P, GT]) for i in range(2)] for n in ("hb", "yt", "kt", "ft", "sn", "q"))
    aT = R.sb("aT", [P, FC * GT])
    st6 = R.sb("st6", [P, 6 * NB])
    psH = [R.ps(f"psH{i}", [P, GT]) for i in range(4)]
    psY = [R.ps(f"psY{i}", [P, 512]) for i in range(4)]
    loaded, ang_ready, sc_ready, coef_ready = (R.sem(n) for n in (
        "weights_loaded", "angles_ready", "sin_cos_ready", "coef_ready"))
    up_done, y_ready, k_ready, f_ready, sin_ready, q_ready, a_ready, y_done, y_used = (R.sem(n) for n in (
        "up_done", "turns_ready", "rounded", "f_ready", "sin_ready", "q_ready", "act_ready", "y_done", "y_used"))
    s_step = R.sem("dve_step")
    block = R.block()
    loads = [(w1, A["l2f_W1"]), (w2, A["l2f_W2"]), (b1, A["l2f_b1"]), (theta, A["l2f_theta"]), (wr, A["l2f_wr"]),
             (wi, A["l2f_wi"]), (b2, A["l2f_b2"])]
    NL = 16 * len(loads)

    @block.sync
    def _(sp):
        for dst, src in loads:
            sp.dma_start(dst[:, :], src).then_inc(loaded, 16)
        sp.wait_ge(loaded, NL)

    @block.tensor
    def _(pe):
        pe.wait_ge(loaded, NL)

        def group(g):
            for j in range(FC):
                pe.wait_ge(y_ready, g * FC + j + 1)
                for c in range(DC):
                    ins = nc.tensor.matmul(psH[j % 4][:, :], w1[:, c * F + j * P:c * F + (j + 1) * P],
                                           xT[:, bass.ds(g * GT + c * NB * P, GT)], start=(c == 0), stop=(c == DC - 1))
                ins.then_inc(up_done, 1)
            pe.wait_ge(y_used, g + 1)
            for j in range(FC):
                pe.wait_ge(a_ready, g * FC + j + 1)
                for t in range(GB):
                    nc.tensor.matmul(psY[t][:, 0:D], aT[:, j * GT + t * P:j * GT + (t + 1) * P], w2[:, j * D:(j + 1) * D],
                                     start=(j == 0), stop=False)
            for t in range(GB):
                ins = nc.tensor.matmul(psY[t][:, 0:D], G.ones_row[:, :], b2[:, :], start=False, stop=True)
            ins.then_inc(y_done, 1)

        with pe.Fori(0, NG) as g:
            group(g)

    @block.scalar
    def _(act):
        act.wait_ge(ang_ready, 1)
        nc.scalar.activation(sc[:, :], ang[:, :], ACT.Sin, scale=TWO_PI).then_inc(sc_ready, 1)
        act.wait_ge(coef_ready, 1)

        def sine(n, j):
            act.wait_ge(f_ready, n + j + 1)
            nc.scalar.activation(sn[j % 2][:, :], ft[j % 2][:, :], ACT.Sin, scale=TWO_PI).then_inc(sin_ready, 1)

        with act.Fori(0, NG) as g:
            n = g * FC
            for j in range(FC):
                act.wait_ge(up_done, n + j + 1)
                act.wait_ge(q_ready, n + j + 1)
                nc.scalar.activation(hb[j % 2][:, :], psH[j % 4][:, :], ACT.Identity, bias=b1[:, j:j + 1])
                nc.scalar.activation(yt[j % 2][:, :], psH[j % 4][:, :], ACT.Identity, scale=0.1 * INV, bias=tb[:, j:j + 1])\
                    .then_inc(y_ready, 1)
                if j:
                    sine(n, j - 1)
            sine(n, FC - 1)

    @block.gpsimd
    def _(pool):
        with pool.Fori(0, NG) as g:
            for j in range(FC):
                pool.wait_ge(k_ready, g * FC + j + 1)
                nc.gpsimd.tensor_tensor(ft[j % 2][:, :], yt[j % 2][:, :], kt[j % 2][:, :], ALU.subtract).then_inc(f_ready, 1)

    @block.vector
    def _(dve):
        step = Step(dve, s_step)
        for i in range(4):
            nc.vector.memset(G.pad[:, 1 + i:2 + i], 0.0).then_inc(y_ready, 1)
        for i in range(2):
            nc.vector.memset(G.pad[:, 5 + 2 * i:6 + 2 * i], 0.0).then_inc(q_ready, 1)
        nc.vector.memset(G.pad[:, 9:10], 0.0).then_inc(y_used, 1)
        dve.wait_ge(loaded, NL)
        step.do(nc.vector.tensor_scalar(ang[:, 0:FC], theta[:, :], INV, None, ALU.mult))
        step.sig(nc.vector.tensor_scalar(ang[:, FC:], ang[:, 0:FC], 0.25, None, ALU.add))
        step.do(nc.vector.tensor_scalar(tb[:, :], b1[:, :], 0.1 * INV, None, ALU.mult))
        step.sig(nc.vector.tensor_tensor(tb[:, :], tb[:, :], ang[:, 0:FC], ALU.add))
        step.do(nc.vector.tensor_scalar(rnd[:, :], ang[:, :], MAGIC, MAGIC, ALU.add, ALU.subtract))
        nc.vector.tensor_tensor(ang[:, :], ang[:, :], rnd[:, :], ALU.subtract).then_inc(ang_ready, 1)
        dve.wait_ge(sc_ready, 1)
        step.do(nc.vector.tensor_tensor(sc[:, 0:FC], sc[:, 0:FC], wi[:, :], ALU.mult))
        step.do(nc.vector.tensor_tensor(sc[:, FC:], sc[:, FC:], wr[:, :], ALU.mult))
        step.do(nc.vector.tensor_tensor(coef[:, :], sc[:, 0:FC], sc[:, FC:], ALU.add))
        step.do(nc.vector.tensor_tensor(coef[:, :], coef[:, :], wi[:, :], ALU.mult))
        nc.vector.tensor_scalar(coef[:, :], coef[:, :], 0.1, None, ALU.mult).then_inc(coef_ready, 1)
        dve.wait_ge(coef_ready, 1)

        def combine(n, j):
            dve.wait_ge(sin_ready, n + j + 1)
            nc.vector.scalar_tensor_tensor(q[j % 2][:, :], sn[j % 2][:, :], coef[:, j:j + 1], hb[j % 2][:, :], ALU.mult, ALU.add)\
                .then_inc(q_ready, 1)
            dve.wait_ge(q_ready, n + j + 3)
            nc.vector.tensor_scalar(aT[:, j * GT:(j + 1) * GT], q[j % 2][:, :], 0.0, None, ALU.max).then_inc(a_ready, 1)

        with dve.Fori(0, NG) as g:
            n = g * FC
            for j in range(FC):
                dve.wait_ge(y_ready, n + j + 5)
                nc.vector.tensor_scalar(kt[j % 2][:, :], yt[j % 2][:, :], MAGIC, MAGIC, ALU.add, ALU.subtract).then_inc(k_ready, 1)
                if j:
                    combine(n, j - 1)
            combine(n, FC - 1)
            dve.wait_ge(y_done, g + 1)
            for t in range(GB):
                xb = G.x[:, bass.ds(g * (GB * D) + t * D, D)]
                ins = nc.vector.tensor_tensor(xb, xb, psY[t][:, 0:D], ALU.add)
            ins.then_inc(y_used, 1)
        dve.wait_ge(y_used, NG + 1)
        all_row_stats(nc, dve, step, G, st6)

    R.close()
def kernel_attention(nc, G, A):
    FQ = 3 * D
    FV = 2 * D
    NH3 = 3 * H
    STATE_SCALE = 1.0 / P ** 2
    R = Region(nc, "l3a")
    w, bias = R.sb("w", [P, DC * 5 * D]), R.sb("bias", [1, 5 * D])
    xT = R.sb("xT", [P, DC * NB * P])
    normalised_transpose(nc, G, "l3a_n", xT)
    F, VV = R.sb("F", [P, NB * FQ]), R.sb("VV", [P, NB * FV])
    ss = R.sb("ss", [P, NB * NH3])
    wo, bo, g, bt = R.sb("wo", [P, DC * D]), R.sb("bo", [1, D]), R.sb("ln_g", [P, DC]), R.sb("ln_b", [P, DC])
    st6, mv = R.sb("st6", [P, 6]), R.sb("mv", [P, 2])
    std, rstd = R.sb("std", [P, NB]), R.sb("rstd", [P, NB])
    diag = R.sb("diag", [P, P])
    OUT = xT

    B = Region(nc, "l3a_f")
    xs = [B.sb(f"xs{i}", [P, D]) for i in range(2)]
    sq = B.sb("sq", [P, FQ])
    ps = [B.ps(f"ps{i}", [P, 3 * 512]) for i in range(2)]
    loaded, w_ready, xs_ready, done, silu_ready, v_taken, half_ready, sq_ready, ss_ready = (B.sem(n) for n in (
        "loaded", "w_ready", "xs_ready", "proj_done", "silu_ready", "v_taken", "half_ready", "sq_ready", "ss_ready"))
    block = B.block()
    loads = [(w, A["l3a_w"]), (bias, A["l3a_bias"]), (wo, A["l3a_Wo"]), (bo, A["l3a_bo"]), (g, A["l3a_g"]), (bt, A["l3a_b"])]
    NL = 16 * len(loads)

    @block.sync
    def _(sp):
        for dst, src in loads:
            sp.dma_start(dst[:, :], src).then_inc(loaded, 16)
        sp.wait_ge(loaded, NL)

    @block.gpsimd
    def _(pool):
        def stage(b, i):
            past(pool, done, b - 1)
            nc.gpsimd.tensor_copy(xs[i][:, :].rearrange("p (c t) -> p c t", c=DC),
                                  xT[:, :].rearrange("p (c n) -> p c n", c=DC)[:, :, bass.ds(b * P, P)]).then_inc(xs_ready, 1)

        stage(0, 0)
        stage(1, 1)
        with pool.Fori(2, NB - 1, 2) as b:
            stage(b, 0)
            stage(b + 1, 1)

    @block.tensor
    def _(pe):
        pe.wait_ge(loaded, NL)
        pe.wait_ge(w_ready, 5 * DC)

        def project(b, i):
            pe.wait_ge(xs_ready, b + 1)
            past(pe, v_taken, b - 1)
            past(pe, silu_ready, b - 1)
            for o, n, col in ((0, D, 0), (512, 2 * D, D), (1024, 2 * D, 3 * D)):
                for c in range(DC):
                    nc.tensor.matmul(ps[i][:, o:o + n], xs[i][:, c * P:(c + 1) * P], w[:, c * 5 * D + col:c * 5 * D + col + n],
                                     start=(c == 0), stop=False)
                ins = nc.tensor.matmul(ps[i][:, o:o + n], G.ones_row[:, :], bias[:, col:col + n], start=False, stop=True)
            ins.then_inc(done, 1)

        project(0, 0)
        project(1, 1)
        with pe.Fori(2, NB - 1, 2) as b:
            project(b, 0)
            project(b + 1, 1)

    @block.scalar
    def _(act):
        def take(b, i):
            act.wait_ge(done, b + 1)
            nc.scalar.activation(F[:, bass.ds(b * FQ, D)], ps[i][:, 0:D], ACT.Silu)
            nc.scalar.activation(F[:, bass.ds(b * FQ + D, 2 * D)], ps[i][:, 512:1024], ACT.Silu).then_inc(silu_ready, 1)
            nc.scalar.activation(VV[:, bass.ds(b * FV, FV)], ps[i][:, 1024:1536], ACT.Copy).then_inc(v_taken, 1)

        with act.Fori(0, NB - 1, 2) as b:
            take(b, 0)
            take(b + 1, 1)

    @block.vector
    def _(dve):
        dve.wait_ge(loaded, NL)
        for c in range(DC):
            for k in range(5):
                wd = w[:, c * 5 * D + k * D + c * P:c * 5 * D + k * D + (c + 1) * P]
                nc.vector.tensor_tensor(wd, wd, G.ident[:, :], ALU.add).then_inc(w_ready, 1)
        nc.vector.tensor_copy(diag[:, :].rearrange("p (h e) -> p h e", h=HC), G.headmask[:, :].unsqueeze(2).to_broadcast([P, HC, HD]))
        with dve.Fori(0, NB) as b:
            dve.wait_ge(silu_ready, b + 1)
            Fb = F[:, bass.ds(b * FQ, FQ)]
            nc.vector.tensor_scalar(Fb, Fb, 0.5, None, ALU.add).then_inc(half_ready, 1)
            dve.wait_ge(half_ready, b + 1)
            nc.vector.tensor_tensor(sq[:, :], Fb, Fb, ALU.mult).then_inc(sq_ready, 1)
            dve.wait_ge(sq_ready, b + 1)
            nc.vector.tensor_reduce(ss[:, bass.ds(b * NH3, NH3)], sq[:, :].rearrange("p (h e) -> p h e", h=NH3), AX.X, ALU.add)\
                .then_inc(ss_ready, 1)
        dve.wait_ge(ss_ready, NB)

    B.close()

    B = Region(nc, "l3a_s")
    fn = B.sb("fn", [P, FQ])
    qT = B.sb("qT", [P, D])
    s0, s1 = B.sb("s0", [P, D]), B.sb("s1", [P, D])
    psQ, psS, psO = (B.ps(n, [P, 512]) for n in ("psQ", "psS", "psO"))
    root_ready, fn_ready, qt_done, qt_ready, s_done, s_ready, o_done, out_ready = (B.sem(n) for n in (
        "root_ready", "fn_ready", "qT_done", "qT_ready", "states_done", "states_ready", "o_done", "out_ready"))
    s_step = B.sem("dve_step")
    block = B.block()

    @block.tensor
    def _(pe):
        def body(b):
            pe.wait_ge(fn_ready, b + 1)
            past(pe, qt_ready, b)
            for c in range(DC):
                ins = nc.tensor.transpose(psQ[:, c * P:(c + 1) * P], fn[:, c * P:(c + 1) * P], G.ident[:, :])
            ins.then_inc(qt_done, 1)
            past(pe, s_ready, b)
            for k in range(2):
                for c in range(DC):
                    o = k * D + c * P
                    ins = nc.tensor.matmul(psS[:, o:o + P], fn[:, D + o:D + o + P], VV[:, bass.ds(b * FV + o, P)], start=True, stop=True)
            ins.then_inc(s_done, 1)
            pe.wait_ge(qt_ready, b + 1)
            pe.wait_ge(s_ready, b + 1)
            past(pe, out_ready, b)
            for c in range(DC):
                ins = nc.tensor.matmul(psO[:, c * P:(c + 1) * P], qT[:, c * P:(c + 1) * P], s1[:, c * P:(c + 1) * P], start=True, stop=True)
            ins.then_inc(o_done, 1)

        body(0)
        with pe.Fori(1, NB) as b:
            body(b)

    @block.scalar
    def _(act):
        nc.scalar.activation(ss[:, :], ss[:, :], ACT.Sqrt).then_inc(root_ready, 1)

        def body(b):
            act.wait_ge(qt_done, b + 1)
            past(act, o_done, b)
            nc.scalar.activation(qT[:, :], psQ[:, 0:D], ACT.Copy).then_inc(qt_ready, 1)
            act.wait_ge(o_done, b + 1)
            nc.scalar.activation(OUT[:, bass.ds(b * D, D)], psO[:, 0:D], ACT.Copy).then_inc(out_ready, 1)

        body(0)
        with act.Fori(1, NB) as b:
            body(b)

    @block.vector
    def _(dve):
        step = Step(dve, s_step)
        dve.wait_ge(root_ready, 1)
        step.do(nc.vector.tensor_scalar(ss[:, :], ss[:, :], 1e-6, None, ALU.add))
        step.do(nc.vector.reciprocal(ss[:, :], ss[:, :]))

        def features(b):
            past(dve, s_done, b)
            past(dve, qt_done, b)
            nc.vector.tensor_tensor(fn[:, :].rearrange("p (h e) -> p h e", h=NH3),
                                    F[:, bass.ds(b * FQ, FQ)].rearrange("p (h e) -> p h e", h=NH3),
                                    ss[:, bass.ds(b * NH3, NH3)].unsqueeze(2).to_broadcast([P, NH3, HD]), ALU.mult).then_inc(fn_ready, 1)

        def states(b):
            dve.wait_ge(s_done, b + 1)
            step.do(nc.vector.scalar_tensor_tensor(s0[:, :].rearrange("p (c n) -> p c n", c=DC),
                                                   psS[:, 0:D].rearrange("p (c n) -> p c n", c=DC), STATE_SCALE,
                                                   diag[:, :].unsqueeze(1).to_broadcast([P, DC, P]), ALU.mult, ALU.mult))
            past(dve, o_done, b)
            nc.vector.tensor_tensor(s1[:, :], s0[:, :], psS[:, D:2 * D], ALU.mult).then_inc(s_ready, 1)

        def rows(b):
            dve.wait_ge(out_ready, b + 1)
            row_stats(nc, dve, step, G, b, st6, mv, OUT)

        features(0)
        states(0)
        features(1)
        rows(0)
        with dve.Fori(1, NB - 1) as b:
            step.enter(b, 4, start=1)
            states(b)
            features(b + 1)
            rows(b)
            step.leave(NB - 2)
        states(NB - 1)
        rows(NB - 1)

    B.close()

    B = Region(nc, "l3a_o")
    on, oT = B.sb("on", [P, D]), B.sb("oT", [P, D])
    psX, psY = B.ps("psX", [P, 512]), B.ps("psY", [P, 512])
    std_ready, on_ready, t_done, oT_ready, y_done, x_ready = (B.sem(n) for n in (
        "std_ready", "on_ready", "t_done", "oT_ready", "y_done", "x_ready"))
    s_step = B.sem("dve_step")
    block = B.block()

    @block.tensor
    def _(pe):
        def body(b):
            pe.wait_ge(on_ready, b + 1)
            past(pe, oT_ready, b)
            for c in range(DC):
                ins = nc.tensor.transpose(psX[:, c * P:(c + 1) * P], on[:, c * P:(c + 1) * P], G.ident[:, :])
            ins.then_inc(t_done, 1)
            pe.wait_ge(oT_ready, b + 1)
            past(pe, x_ready, b)
            for c in range(DC):
                nc.tensor.matmul(psY[:, 0:D], oT[:, c * P:(c + 1) * P], wo[:, c * D:(c + 1) * D], start=(c == 0), stop=False)
            nc.tensor.matmul(psY[:, 0:D], G.ones_row[:, :], bo[:, :], start=False, stop=True).then_inc(y_done, 1)

        body(0)
        with pe.Fori(1, NB) as b:
            body(b)

    @block.scalar
    def _(act):
        nc.scalar.activation(std[:, :], variances(G), ACT.Sqrt, bias=G.neg1e5[:, 0:1]).then_inc(std_ready, 1)

        def body(b):
            act.wait_ge(t_done, b + 1)
            past(act, y_done, b)
            for c in range(DC):
                ins = nc.scalar.activation(oT[:, c * P:(c + 1) * P], psX[:, c * P:(c + 1) * P], ACT.Identity,
                                           scale=g[:, c:c + 1], bias=bt[:, c:c + 1])
            ins.then_inc(oT_ready, 1)

        body(0)
        with act.Fori(1, NB) as b:
            body(b)

    @block.vector
    def _(dve):
        step = Step(dve, s_step)
        dve.wait_ge(std_ready, 1)
        step.do(nc.vector.reciprocal(rstd[:, :], std[:, :]))

        def normalise(b):
            past(dve, t_done, b)
            nc.vector.tensor_scalar(on[:, :], OUT[:, bass.ds(b * D, D)], G.mv[:, bass.ds(b * 2, 1)], rstd[:, bass.ds(b, 1)],
                                    ALU.subtract, ALU.mult).then_inc(on_ready, 1)

        def add(b):
            dve.wait_ge(y_done, b + 1)
            xb = G.x[:, bass.ds(b * D, D)]
            nc.vector.tensor_tensor(xb, xb, psY[:, 0:D], ALU.add).then_inc(x_ready, 1)
            dve.wait_ge(x_ready, b + 1)
            row_stats(nc, dve, step, G, b, st6, mv)

        normalise(0)
        normalise(1)
        add(0)
        with dve.Fori(1, NB - 1) as b:
            step.enter(b, 3, start=1)
            normalise(b + 1)
            add(b)
            step.leave(NB - 2)
        add(NB - 1)

    B.close()
    R.close()


def quantised_ffn(nc, G, A):
    F = 1024
    FC = F // P
    T = NB * P
    RMAX = bass.bass_isa.ReduceOp.max
    R = Region(nc, "l3f")
    xT = R.sb("xT", [P, DC * T])
    normalised_transpose(nc, G, "l3f_n", xT)
    w1, w2 = R.sb("w1", [P, DC * F]), R.sb("w2", [P, FC * D])
    b1, b2 = R.sb("b1", [P, FC]), R.sb("b2", [P, D])
    w1q, w2q = R.sb("w1q", [P, DC * F], BF16), R.sb("w2q", [P, FC * D], BF16)
    xq = R.sb("xq", [P, DC * T], BF16)
    tmp = R.sb("tmp", [P, DC * F])
    ext, top = R.sb("ext", [P, 4]), R.sb("top", [P, 4])
    hext, htop = R.sb("hext", [P, 2]), R.sb("htop", [P, 2])
    part = R.sb("part", [P, 2 * NG * FC])
    sc = R.sb("sc", [P, 24])
    hT = R.sb("hT", [P, NG * FC * GT])
    ra, rb = ([R.sb(f"{n}{i}", [P, GT]) for i in range(2)] for n in ("ra", "rb"))
    hq = R.sb("hq", [P, FC * GT], BF16)
    yb = R.sb("yb", [P, D])
    psH = [R.ps(f"psH{i}", [P, GT]) for i in range(4)]
    psY = [R.ps(f"psY{i}", [P, 512]) for i in range(4)]
    loaded, ext_ready, top_ready, q_ready, h_done, h_ready, h_taken, hext_ready, htop_ready, s2_ready = (R.sem(n) for n in (
        "weights_loaded", "ext_ready", "top_ready", "quantised", "up_done", "gelu_ready", "range_taken", "hext_ready",
        "htop_ready", "scales_ready"))
    ra_ready, rb_ready, hq_ready, y_done, y_used = (R.sem(n) for n in ("scaled", "clipped", "hq_ready", "y_done", "y_used"))
    s_step = R.sem("dve_step")
    block = R.block()
    loads = [(w1, A["l3f_W1"]), (w2, A["l3f_W2"]), (b1, A["l3f_b1"]), (b2, A["l3f_b2"])]
    NL = 16 * len(loads)

    def s(i):
        return sc[:, i:i + 1]

    SX, ISX, LO, HI, SW1, SW2, ISW1, ISW2, S1, T0, SH, ISH, HLO, HHI, S2 = range(15)

    @block.sync
    def _(sp):
        for dst, src in loads:
            sp.dma_start(dst[:, :], src).then_inc(loaded, 16)
        sp.wait_ge(loaded, NL)

    @block.gpsimd
    def _(pool):
        pool.wait_ge(ext_ready, 4)
        nc.gpsimd.partition_all_reduce(top[:, :], ext[:, :], P, RMAX).then_inc(top_ready, 1)
        pool.wait_ge(hext_ready, 2)
        nc.gpsimd.partition_all_reduce(htop[:, :], hext[:, :], P, RMAX).then_inc(htop_ready, 1)

    @block.tensor
    def _(pe):
        pe.wait_ge(q_ready, 3)
        with pe.Fori(0, NG) as g:
            for j in range(FC):
                pe.wait_ge(h_ready, g * FC + j + 1)
                for c in range(DC):
                    ins = nc.tensor.matmul(psH[j % 4][:, :], w1q[:, c * F + j * P:c * F + (j + 1) * P],
                                           xq[:, bass.ds(g * GT + c * T, GT)], start=(c == 0), stop=(c == DC - 1))
                ins.then_inc(h_done, 1)
        with pe.Fori(0, NG) as g:
            pe.wait_ge(y_used, g + 1)
            for j in range(FC):
                pe.wait_ge(hq_ready, g * FC + j + 1)
                for t in range(GB):
                    ins = nc.tensor.matmul(psY[t][:, 0:D], hq[:, j * GT + t * P:j * GT + (t + 1) * P], w2q[:, j * D:(j + 1) * D],
                                           start=(j == 0), stop=(j == FC - 1))
            ins.then_inc(y_done, 1)

    @block.scalar
    def _(act):
        act.wait_ge(q_ready, 3)
        with act.Fori(0, NG) as g:
            for j in range(FC):
                act.wait_ge(h_done, g * FC + j + 1)
                nc.scalar.activation(hT[:, bass.ds(g * (FC * GT) + j * GT, GT)], psH[j % 4][:, :], ACT.Gelu,
                                     scale=s(S1), bias=b1[:, j:j + 1]).then_inc(h_ready, 1)
        act.wait_ge(s2_ready, 1)

        def to_bf16(n, j):
            act.wait_ge(rb_ready, n + j + 1)
            nc.scalar.activation(hq[:, j * GT:(j + 1) * GT], rb[j % 2][:, :], ACT.Copy, bias=-MAGIC).then_inc(hq_ready, 1)

        with act.Fori(0, NG) as g:
            n = g * FC
            for j in range(FC):
                nc.scalar.activation(ra[j % 2][:, :], hT[:, bass.ds(g * (FC * GT) + j * GT, GT)], ACT.Identity,
                                     scale=s(ISH), bias=s(S2 + 1)).then_inc(ra_ready, 1)
                if j == 1:
                    act.wait_ge(y_done, g + 1)
                if j:
                    to_bf16(n, j - 1)
            to_bf16(n, FC - 1)

    @block.vector
    def _(dve):
        step = Step(dve, s_step)
        for i in range(4):
            nc.vector.memset(G.pad[:, 1 + i:2 + i], 0.0).then_inc(h_ready, 1)
        nc.vector.memset(G.pad[:, 5:6], 0.0).then_inc(y_used, 1)
        nc.vector.memset(G.pad[:, 6:7], 0.0).then_inc(y_done, 1)
        step.sig(nc.vector.memset(s(S2 + 1), MAGIC))
        nc.vector.tensor_reduce(ext[:, 0:1], xT[:, :], AX.X, ALU.max).then_inc(ext_ready, 1)
        nc.vector.tensor_reduce(ext[:, 1:2], xT[:, :], AX.X, ALU.min, negate=True).then_inc(ext_ready, 1)
        dve.wait_ge(loaded, NL)
        for k, w in enumerate((w1, w2)):
            nc.vector.tensor_reduce(ext[:, 2 + k:3 + k], w[:, :], AX.X, ALU.max, apply_absolute_value=True).then_inc(ext_ready, 1)
        dve.wait_ge(top_ready, 1)

        def affine(up, down, sx, isx, lo, hi):
            step.do(nc.vector.tensor_tensor(s(T0), up, down, ALU.add))
            step.do(nc.vector.tensor_scalar(s(sx), s(T0), 1.0 / 255.0, 1e-8, ALU.mult, ALU.max))
            step.do(nc.vector.reciprocal(s(isx), s(sx)))
            step.do(nc.vector.tensor_tensor(s(T0), down, s(isx), ALU.mult))
            step.do(nc.vector.tensor_scalar(s(T0), s(T0), MAGIC, MAGIC, ALU.add, ALU.subtract))
            step.do(nc.vector.tensor_scalar(s(T0), s(T0), -128.0, -128.0, ALU.add, ALU.max))
            step.do(nc.vector.tensor_scalar(s(T0), s(T0), 127.0, None, ALU.min))
            step.do(nc.vector.tensor_scalar(s(lo), s(T0), -1.0, -128.0, ALU.mult, ALU.add))
            step.do(nc.vector.tensor_scalar(s(hi), s(lo), MAGIC + 255.0, None, ALU.add))
            step.do(nc.vector.tensor_scalar(s(lo), s(lo), MAGIC, None, ALU.add))

        affine(top[:, 0:1], top[:, 1:2], SX, ISX, LO, HI)
        step.do(nc.vector.tensor_scalar(sc[:, SW1:SW1 + 2], top[:, 2:4], 1.0 / 127.0, 1e-8, ALU.mult, ALU.max))
        step.do(nc.vector.reciprocal(sc[:, ISW1:ISW1 + 2], sc[:, SW1:SW1 + 2]))
        step.do(nc.vector.tensor_tensor(s(S1), s(SX), s(SW1), ALU.mult))
        for w, wq_, isw in ((w1, w1q, ISW1), (w2, w2q, ISW2)):
            step.do(nc.vector.tensor_scalar(tmp[:, :], w[:, :], s(isw), MAGIC, ALU.mult, ALU.add))
            step.do(nc.vector.tensor_scalar(tmp[:, :], tmp[:, :], MAGIC + 127.0, MAGIC - 127.0, ALU.min, ALU.max))
            nc.vector.tensor_scalar(wq_[:, :], tmp[:, :], MAGIC, None, ALU.subtract).then_inc(q_ready, 1)
            dve.wait_ge(q_ready, 1)
        step.do(nc.vector.tensor_scalar(xT[:, :], xT[:, :], s(ISX), MAGIC, ALU.mult, ALU.add))
        step.do(nc.vector.tensor_scalar(xT[:, :], xT[:, :], s(LO), s(HI), ALU.max, ALU.min))
        nc.vector.tensor_scalar(xq[:, :], xT[:, :], MAGIC, None, ALU.subtract).then_inc(q_ready, 1)
        with dve.Fori(0, NG) as g:
            for j in range(FC):
                dve.wait_ge(h_ready, g * FC + j + 5)
                hc = hT[:, bass.ds(g * (FC * GT) + j * GT, GT)]
                nc.vector.tensor_reduce(part[:, bass.ds(g * FC + j, 1)], hc, AX.X, ALU.max)
                nc.vector.tensor_reduce(part[:, bass.ds(g * FC + (NG * FC + j), 1)], hc, AX.X, ALU.min).then_inc(h_taken, 1)
        dve.wait_ge(h_taken, NG * FC)
        nc.vector.tensor_reduce(hext[:, 0:1], part[:, 0:NG * FC], AX.X, ALU.max).then_inc(hext_ready, 1)
        nc.vector.tensor_reduce(hext[:, 1:2], part[:, NG * FC:], AX.X, ALU.min, negate=True).then_inc(hext_ready, 1)
        dve.wait_ge(htop_ready, 1)
        affine(htop[:, 0:1], htop[:, 1:2], SH, ISH, HLO, HHI)
        nc.vector.tensor_tensor(s(S2), s(SH), s(SW2), ALU.mult).then_inc(s2_ready, 1)
        dve.wait_ge(s2_ready, 1)

        with dve.Fori(0, NG) as g:
            n = g * FC
            for j in range(FC):
                dve.wait_ge(ra_ready, n + j + 1)
                nc.vector.tensor_scalar(rb[j % 2][:, :], ra[j % 2][:, :], s(HLO), s(HHI), ALU.max, ALU.min).then_inc(rb_ready, 1)
            dve.wait_ge(y_done, g + 2)
            step.enter(g, 2 * GB)
            for t in range(GB):
                xb = G.x[:, bass.ds(g * (GB * D) + t * D, D)]
                step.do(nc.vector.scalar_tensor_tensor(yb[:, :], psY[t][:, 0:D], s(S2), b2[:, :], ALU.mult, ALU.add))
                step.do(nc.vector.tensor_tensor(xb, xb, yb[:, :], ALU.add))
            step.leave(NG)
            nc.vector.memset(G.pad[:, 7:8], 0.0).then_inc(y_used, 1)

    R.close()
SEG = (77, 16, 35)
SEG0 = (0, 77, 93)
MAXREL = 16
NREL = SEG[0] - 1 + MAXREL


def stream_keys(nc, G, A, KD, VD):
    IN, T = 1024, NB * P
    IC = IN // P
    seg_rows = [sum(SEG[:s]) * NB for s in range(3)]

    R = Region(nc, "l3x_kv")
    ck = R.sb("ck", [P, DC * T])
    wk = [R.sb(f"wk{s}", [P, DC * IN]) for s in range(3)]
    wv = [R.sb(f"wv{s}", [P, DC * IN]) for s in range(3)]
    KT = [R.sb(f"KT{i}", [P, GB * IN]) for i in range(2)]
    Vs = [R.sb(f"Vs{i}", [P, IN]) for i in range(2)]
    psK = [R.ps(f"psK{i}", [P, 512]) for i in range(4)]
    psV = [R.ps(f"psV{i}", [P, 512]) for i in range(4)]
    loaded, k_done, ka_taken, kd_taken, v_done, va_taken, vd_taken = (R.sem(n) for n in (
        "loaded", "k_done", "k_taken_act", "k_taken_dve", "v_done", "v_taken_act", "v_taken_dve"))
    k_stored, v_stored = [R.sem(f"k{i}_stored") for i in range(2)], [R.sem(f"v{i}_stored") for i in range(2)]
    block = R.block()
    NL = 16 * 7
    units = [(s, j) for s in range(3) for j in range(IC)]
    tiles = [(s, r0, min(P, NB * SEG[s] - r0)) for s in range(3) for r0 in range(0, NB * SEG[s], P)]

    def kt_view(g, s):
        return KT[g % 2][:, :].rearrange("p (b j k) -> p j b k", b=GB, j=IC)[:, :, :, SEG0[s]:SEG0[s] + SEG[s]]

    @block.sync
    def _(sp):
        sp.dma_start(ck[:, :], A["ctx_packed"]).then_inc(loaded, 16)
        for s, n in enumerate(("", "_ip", "_ap")):
            sp.dma_start(wk[s][:, :], A["l3x_Wk" + n]).then_inc(loaded, 16)
        for s, n in enumerate(("", "_ip", "_ap")):
            sp.dma_start(wv[s][:, :], A["l3x_Wv" + n]).then_inc(loaded, 16)
        for g in range(NG):
            sp.wait_ge(ka_taken, (g + 1) * len(units) // 2)
            sp.wait_ge(kd_taken, (g + 1) * len(units) // 2)
            sp.dma_start(KD[g], KT[g % 2][:, :]).then_inc(k_stored[g % 2], 16)
        for n, (s, r0, m) in enumerate(tiles):
            sp.wait_ge(va_taken, n + 1)
            sp.wait_ge(vd_taken, n + 1)
            sp.dma_start(VD[seg_rows[s] + r0:seg_rows[s] + r0 + m, :], Vs[n % 2][0:m, :]).then_inc(v_stored[n % 2], 16)
        for i in range(2):
            sp.wait_ge(k_stored[i], 16 * (NG // 2))
            sp.wait_ge(v_stored[i], 16 * ((len(tiles) + 1 - i) // 2))

    @block.tensor
    def _(pe):
        pe.wait_ge(loaded, NL)
        for g in range(NG):
            for n, (s, j) in enumerate(units):
                taken = ka_taken if n % 2 == 0 else kd_taken
                past(pe, taken, g * len(units) // 2 + n // 2 - 1)
                for c in range(DC):
                    o = c * T + seg_rows[s] + g * GB * SEG[s]
                    ins = nc.tensor.matmul(psK[n % 4][:, 0:GB * SEG[s]], wk[s][:, c * IN + j * P:c * IN + (j + 1) * P],
                                           ck[:, o:o + GB * SEG[s]], start=(c == 0), stop=(c == DC - 1))
                ins.then_inc(k_done, 1)
        for n, (s, r0, m) in enumerate(tiles):
            past(pe, va_taken, n - 1)
            past(pe, vd_taken, n - 1)
            for q in range(2):
                for c in range(DC):
                    o = c * T + seg_rows[s] + r0
                    ins = nc.tensor.matmul(psV[2 * (n % 2) + q][0:m, :], ck[:, o:o + m], wv[s][:, c * IN + q * 512:c * IN + (q + 1) * 512],
                                           start=(c == 0), stop=(c == DC - 1))
            ins.then_inc(v_done, 1)

    def take_keys(eng, copy, odd, taken):
        for g in range(NG):
            if g >= 2:
                eng.wait_ge(k_stored[g % 2], 16 * (g // 2))
            for n, (s, j) in enumerate(units):
                if n % 2 == odd:
                    eng.wait_ge(k_done, g * len(units) + n + 1)
                    copy(kt_view(g, s)[:, j], psK[n % 4][:, 0:GB * SEG[s]].rearrange("p (b k) -> p b k", b=GB)).then_inc(taken, 1)

    def take_values(eng, copy, q, taken):
        for n, (s, r0, m) in enumerate(tiles):
            if n >= 2:
                eng.wait_ge(v_stored[n % 2], 16 * (n // 2))
            eng.wait_ge(v_done, n + 1)
            copy(Vs[n % 2][0:m, q * 512:(q + 1) * 512], psV[2 * (n % 2) + q][0:m, :]).then_inc(taken, 1)

    @block.scalar
    def _(act):
        def copy(dst, src):
            return nc.scalar.activation(dst, src, ACT.Copy)
        take_keys(act, copy, 0, ka_taken)
        take_values(act, copy, 0, va_taken)

    @block.vector
    def _(dve):
        take_keys(dve, nc.vector.tensor_copy, 1, kd_taken)
        take_values(dve, nc.vector.tensor_copy, 1, vd_taken)

    R.close()


def stream_attention(nc, G, A):
    W, IN, T = 64, 1024, NB * P
    IC, HH = IN // P, H // 2
    GB, NG, GT = 8, NB // 8, 8 * P
    KD = nc.dram_tensor("keys", (4, P, 4 * IN), F32, kind="Internal").ap()
    VD = nc.dram_tensor("values", (T, IN), F32, kind="Internal").ap()
    stream_keys(nc, G, A, KD, VD)
    seg_rows = [sum(SEG[:s]) * NB for s in range(3)]
    xT = G.ctxT
    normalised_transpose(nc, G, "l3x_n", xT)
    R = Region(nc, "l3x")
    wq, wo, bo = R.sb("wq", [P, DC * IN]), R.sb("wo", [P, IC * D]), R.sb("bo", [1, D])
    rk, rv = R.sb("rel_k", [P, P - 1 + SEG[0]]), R.sb("rel_v", [SEG[0], (NREL + 1) * W])
    gates, gate3 = R.sb("gates", [P, 2]), R.sb("gate3", [P, 3])
    K, V = [R.sb(f"K{i}", [P, IN]) for i in range(2)], [R.sb(f"V{i}", [P, IN]) for i in range(2)]
    qT = R.sb("qT", [P, IC * GT])
    RP = R.sb("rel_or_weights", [P, GB * H * P])
    Pn = [R.sb(f"Pn{i}", [P, HH * P]) for i in range(3)]
    mx = [R.sb(f"mx{i}", [P, 3 * HH]) for i in range(2)]
    den = [R.sb(f"den{i}", [P, 3 * HH]) for i in range(2)]
    fac = [R.sb(f"fac{i}", [P, 3 * HH]) for i in range(3)]
    st6 = R.sb("st6", [P, 6 * NB])
    psS, psB = R.ps("psS", [P, 2048]), R.ps("psB", [P, 2048])
    loaded, gate_ready = R.sem("weights_loaded"), R.sem("gates_ready")
    kv_loaded = [R.sem(f"kv{i}_loaded") for i in range(2)]
    q_done, q_taken, r_done, r0_taken, r1_taken, s_done, shifted, e_ready, f_ready, p_ready = (R.sem(n) for n in (
        "q_done", "q_taken", "rel_done", "rel0_taken", "rel1_taken", "scores_done", "shifted", "exp_ready", "factors_ready", "p_ready"))
    t_done, pt_taken, pv_done, ot_taken, w_done, w_taken, y_done, x_ready = (R.sem(n) for n in (
        "pT_done", "pT_taken", "pv_done", "o_taken", "relv_done", "relv_taken", "y_done", "x_ready"))
    s_step = R.sem("dve_step")
    block = R.block()
    loads = [(wq, "l3x_Wq"), (wo, "l3x_Wo"), (bo, "l3x_bo"), (rk, "l3x_relk"), (rv, "l3x_relv"), (gates, "l3x_gates")]
    NL = 16 * len(loads)
    RPv = RP[:, :].rearrange("p (b h i) -> p b h i", b=GB, h=H)
    qTv = qT[:, :].rearrange("p (j b i) -> p b j i", j=IC, b=GB)
    OTv = qTv
    QN = 512 // (GB * HH)
    runs = [(i0, min(QN, NREL - i0)) for i0 in range(0, NREL, QN)]
    NU = len(runs) + GB
    UN = 2 * GB
    TAIL = P - NREL

    def bank(i, n=512):
        return psB[:, i * 512:i * 512 + n]

    @block.sync
    def _(sp):
        for dst, src in loads:
            sp.dma_start(dst[:, :], A[src]).then_inc(loaded, 16)
        with sp.Fori(0, NG) as g:
            for b in range(GB):
                i = b % 2
                sp.wait_ge(pv_done, g * UN + 2 * b + 2)
                sp.dma_start(K[i][:, :], KD[bass.ds(g * 2 + b // 4, 1), :, (b % 4) * IN:(b % 4 + 1) * IN].rearrange("g p n -> (g p) n"))\
                    .then_inc(kv_loaded[i], 16)
                for s in range(3):
                    sp.dma_start(V[i][SEG0[s]:SEG0[s] + SEG[s], :],
                                 VD[bass.ds(g * (GB * SEG[s]) + (seg_rows[s] + b * SEG[s]), SEG[s]), :]).then_inc(kv_loaded[i], 16)
        sp.wait_ge(loaded, NL)

    @block.tensor
    def _(pe):
        pe.wait_ge(loaded, NL)

        def rows(half):
            return slice(half * W, (half + 1) * W)

        def scores(g, u):
            b, half = u // 2, u % 2
            if half == 0:
                pe.wait_ge(kv_loaded[b % 2], g * (32 * GB) + 64 * (b // 2 + 1))
            if u >= 2:
                pe.wait_ge(shifted, g * (3 * UN) + 3 * (u - 1))
            for j in range(HH):
                o = half * 1024 + j * P
                nc.tensor.matmul(psS[:, o:o + P], qTv[rows(half), b, j, :], K[b % 2][rows(half), j * P:(j + 1) * P],
                                 start=True, stop=False)
                ins = nc.tensor.matmul(psS[:, o:o + SEG[0]], RPv[0:SEG[0], b, half * HH + j, :], G.ident[0:SEG[0], 0:SEG[0]],
                                       start=False, stop=True)
            ins.then_inc(s_done, 1)

        def weigh(g, u):
            b, half = u // 2, u % 2
            if u >= 1:
                pe.wait_ge(pt_taken, g * UN + u)
            pe.wait_ge(p_ready, g * (3 * UN) + 3 * (u + 1))
            for j in range(HH):
                ins = nc.tensor.transpose(psB[:, 1024 + j * P:1024 + (j + 1) * P], Pn[u % 3][:, j * P:(j + 1) * P], G.ident[:, :])
            ins.then_inc(t_done, 1)
            pe.wait_ge(pt_taken, g * UN + u + 1)
            if u >= 2:
                pe.wait_ge(ot_taken, g * UN + u - 1)
            for j in range(HH):
                h = 2 * j + half
                ins = nc.tensor.matmul(psB[rows(half), j * P:(j + 1) * P], V[b % 2][:, h * W:(h + 1) * W], RPv[:, b, half * HH + j, :],
                                       start=True, stop=True)
            ins.then_inc(pv_done, 1)

        with pe.Fori(0, NG) as g:
            for n in range(2 * IC):
                j, t = n // 2, n % 2
                if n >= 4:
                    pe.wait_ge(q_taken, g * (2 * IC) + n - 3)
                for c in range(DC):
                    ins = nc.tensor.matmul(bank(n % 4), wq[:, c * IN + j * P:c * IN + (j + 1) * P],
                                           xT[:, bass.ds(g * GT + (c * T + t * 512), 512)], start=(c == 0), stop=(c == DC - 1))
                ins.then_inc(q_done, 1)
            pe.wait_ge(q_taken, g * (2 * IC) + 2 * IC)
            for u in range(NU):
                if u >= 2:
                    pe.wait_ge(r0_taken, g * NU + u - 1)
                    pe.wait_ge(r1_taken, g * NU + u - 1)
                if u < len(runs):
                    i0, n = runs[u]
                    for i in range(i0, i0 + n):
                        for half in range(2):
                            ins = nc.tensor.matmul(bank(2 * (u % 2) + half)[0:SEG[0], (i - i0) * (GB * HH):(i - i0 + 1) * (GB * HH)],
                                                   rk[rows(half), P - 1 - i:P - 1 - i + SEG[0]], qTv[rows(half), :, :, i],
                                                   start=True, stop=True)
                else:
                    for half in range(2):
                        ins = nc.tensor.matmul(bank(2 * (u % 2) + half)[0:SEG[0], 0:HH * TAIL], rk[rows(half), 0:SEG[0]],
                                               qTv[rows(half), u - len(runs), :, NREL:], start=True, stop=True)
                ins.then_inc(r_done, 1)
            pe.wait_ge(r0_taken, g * NU + NU)
            pe.wait_ge(r1_taken, g * NU + NU)
            scores(g, 0)
            scores(g, 1)
            for u in range(UN):
                if u + 2 < UN:
                    scores(g, u + 2)
                weigh(g, u)
            pe.wait_ge(ot_taken, g * UN + UN)
            for u in range(NU):
                if u >= 4:
                    pe.wait_ge(w_taken, g * NU + u - 3)
                for i in (range(runs[u][0], sum(runs[u])) if u < len(runs) else (NREL,)):
                    for half in range(2):
                        if u < len(runs):
                            dst = bank(u % 4)[rows(half), (i - runs[u][0]) * (GB * HH):(i - runs[u][0] + 1) * (GB * HH)]
                            src = RPv[0:SEG[0], :, half * HH:(half + 1) * HH, i]
                        else:
                            dst = bank(u % 4)[rows(half), 0:HH * TAIL]
                            src = RPv[0:SEG[0], u - len(runs), half * HH:(half + 1) * HH, NREL:]
                        ins = nc.tensor.matmul(dst, rv[:, i * W:(i + 1) * W], src, start=True, stop=True)
                ins.then_inc(w_done, 1)
            pe.wait_ge(w_taken, g * NU + NU)
            for b in range(GB):
                if b >= 4:
                    pe.wait_ge(x_ready, g * GB + b - 3)
                for j in range(IC):
                    nc.tensor.matmul(bank(b % 4, D), OTv[:, b, j, :], wo[:, j * D:(j + 1) * D], start=(j == 0), stop=False)
                nc.tensor.matmul(bank(b % 4, D), G.ones_row[:, :], bo[:, :], start=False, stop=True).then_inc(y_done, 1)
            pe.wait_ge(x_ready, g * GB + GB)

    def take_rel(eng, copy, g, half, taken):
        for u in range(NU):
            eng.wait_ge(r_done, g * NU + u + 1)
            ps = bank(2 * (u % 2) + half)
            if u < len(runs):
                i0, n = runs[u]
                copy(RPv[0:SEG[0], :, half * HH:(half + 1) * HH, i0:i0 + n],
                     ps[0:SEG[0], 0:n * GB * HH].rearrange("p (i b j) -> p b j i", b=GB, j=HH)).then_inc(taken, 1)
            else:
                copy(RPv[0:SEG[0], u - len(runs), half * HH:(half + 1) * HH, NREL:],
                     ps[0:SEG[0], 0:HH * TAIL].rearrange("p (j i) -> p j i", j=HH)).then_inc(taken, 1)

    @block.scalar
    def _(act):
        act.wait_ge(loaded, NL)
        nc.scalar.activation(gates[:, :], gates[:, :], ACT.Tanh).then_inc(gate_ready, 1)

        def exps(g, u):
            act.wait_ge(shifted, g * (3 * UN) + 3 * (u + 1))
            nc.scalar.activation(Pn[u % 3][:, :], Pn[u % 3][:, :], ACT.Exp, scale=W ** -0.5).then_inc(e_ready, 1)

        def take(g, u):
            b, half = u // 2, u % 2
            act.wait_ge(t_done, g * UN + u + 1)
            nc.scalar.activation(RP[:, (b * H + half * HH) * P:(b * H + (half + 1) * HH) * P], psB[:, 1024:2048],
                                 ACT.Copy).then_inc(pt_taken, 1)
            act.wait_ge(pv_done, g * UN + u + 1 + 4)
            nc.scalar.activation(OTv[half * W:(half + 1) * W, b], psB[half * W:(half + 1) * W, 0:1024].rearrange("p (j i) -> p j i", j=IC),
                                 ACT.Copy).then_inc(ot_taken, 1)

        with act.Fori(0, NG) as g:
            for n in range(2 * IC):
                act.wait_ge(q_done, g * (2 * IC) + n + 1)
                nc.scalar.activation(qT[:, n * 512:(n + 1) * 512], bank(n % 4), ACT.Copy).then_inc(q_taken, 1)
            take_rel(act, lambda o, i: nc.scalar.activation(o, i, ACT.Copy), g, 0, r0_taken)
            exps(g, 0)
            for u in range(UN):
                if u + 1 < UN:
                    exps(g, u + 1)
                take(g, u)

    @block.gpsimd
    def _(pool):
        with pool.Fori(0, NG) as g:
            for u in range(UN):
                pool.wait_ge(f_ready, g * UN + u + 1)
                for s in range(3):
                    v = Pn[u % 3][:, :].rearrange("p (h k) -> p h k", h=HH)[:, :, SEG0[s]:SEG0[s] + SEG[s]]
                    nc.gpsimd.tensor_tensor(v, v, fac[u % 3][:, s * HH:(s + 1) * HH].unsqueeze(2).to_broadcast([P, HH, SEG[s]]), ALU.mult)\
                        .then_inc(p_ready, 1)

    @block.vector
    def _(dve):
        step = Step(dve, s_step)
        for i in range(4):
            nc.vector.memset(G.pad[:, 1 + i:2 + i], 0.0).then_inc(pv_done, 1)
        step.sig(nc.vector.memset(gate3[:, 0:1], 1.0))
        dve.wait_ge(gate_ready, 1)
        step.do(nc.vector.tensor_scalar(gate3[:, 1:3], gates[:, :], 1.0, None, ALU.add))

        def shift(g, u):
            half = u % 2
            dve.wait_ge(s_done, g * UN + u + 1)
            S3 = psS[:, half * 1024:(half + 1) * 1024].rearrange("p (h k) -> p h k", h=HH)
            P3 = Pn[u % 3][:, :].rearrange("p (h k) -> p h k", h=HH)
            for s in range(3):
                step.sig(nc.vector.tensor_reduce(mx[half][:, s * HH:(s + 1) * HH], S3[:, :, SEG0[s]:SEG0[s] + SEG[s]], AX.X, ALU.max))
            step.wait()
            for s in range(3):
                nc.vector.tensor_tensor(P3[:, :, SEG0[s]:SEG0[s] + SEG[s]], S3[:, :, SEG0[s]:SEG0[s] + SEG[s]],
                                        mx[half][:, s * HH:(s + 1) * HH].unsqueeze(2).to_broadcast([P, HH, SEG[s]]), ALU.subtract)\
                    .then_inc(shifted, 1)

        def factors(g, u):
            half = u % 2
            dve.wait_ge(e_ready, g * UN + u + 1)
            P3 = Pn[u % 3][:, :].rearrange("p (h k) -> p h k", h=HH)
            for s in range(3):
                step.sig(nc.vector.tensor_reduce(den[half][:, s * HH:(s + 1) * HH], P3[:, :, SEG0[s]:SEG0[s] + SEG[s]], AX.X, ALU.add))
            step.wait()
            step.do(nc.vector.reciprocal(den[half][:, :], den[half][:, :]))
            nc.vector.tensor_tensor(fac[u % 3][:, :].rearrange("p (s h) -> p s h", s=3), den[half][:, :].rearrange("p (s h) -> p s h", s=3),
                                    gate3[:, :].unsqueeze(2).to_broadcast([P, 3, HH]), ALU.mult).then_inc(f_ready, 1)

        with dve.Fori(0, NG) as g:
            step.enter(g, 7 * UN)
            take_rel(dve, nc.vector.tensor_copy, g, 1, r1_taken)
            shift(g, 0)
            for u in range(UN):
                if u + 1 < UN:
                    if u >= 2:
                        dve.wait_ge(t_done, g * UN + u - 1)
                    shift(g, u + 1)
                factors(g, u)
            dve.wait_ge(ot_taken, g * UN + UN)
            for u in range(NU):
                dve.wait_ge(w_done, g * NU + u + 1)
                if u < len(runs):
                    i0, n = runs[u]
                    o = OTv[:, :, :, i0:i0 + n]
                    i = bank(u % 4)[:, 0:n * GB * HH].rearrange("p (i b j) -> p b j i", b=GB, j=HH)
                else:
                    o = OTv[:, u - len(runs), :, NREL:]
                    i = bank(u % 4)[:, 0:HH * TAIL].rearrange("p (j i) -> p j i", j=HH)
                nc.vector.tensor_tensor(o, o, i, ALU.add).then_inc(w_taken, 1)
            for b in range(GB):
                dve.wait_ge(y_done, g * GB + b + 1)
                xb = G.x[:, bass.ds(g * (GB * D) + b * D, D)]
                nc.vector.tensor_tensor(xb, xb, bank(b % 4, D), ALU.add).then_inc(x_ready, 1)
            step.leave(NG)
        dve.wait_ge(x_ready, NB)
        all_row_stats(nc, dve, step, G, st6)

    R.close()
STAGES = ("l0a", "l0x", "l0f", "l1a", "l1x", "l1f", "l2a", "l2x", "l2f", "l3a", "l3x", "l3f")
SUBLAYERS = {
    "l0a": lambda nc, G, A: attention16(nc, G, A, "l0a", "linear", "l0a_", out_bias=True),
    "l0x": lambda nc, G, A: attention16(nc, G, A, "l0x", "softmax", "l0x_", cross=True, biased=True, out_bias=True),
    "l0f": lambda nc, G, A: experts(nc, G, A, "l0f", True, False),
    "l1a": l1_attention,
    "l1x": lambda nc, G, A: attention16(nc, G, A, "l1x", "relu2", "l1x_", cross=True),
    "l1f": lambda nc, G, A: experts(nc, G, A, "l1f", False, True),
}


SUBLAYERS["l2a"], SUBLAYERS["l2x"], SUBLAYERS["l2f"] = wide_attention, memory_attention, phase_ffn


SUBLAYERS["l3a"], SUBLAYERS["l3f"] = kernel_attention, quantised_ffn


SUBLAYERS["l3x"] = stream_attention


def expert(gate, up, down):
    return np.concatenate([chunks(gate), chunks(up), chunks(down)], axis=1)


def more_layout(I, A):
    I = {n: np.asarray(a) for n, a in I.items()}
    A["l0f_router"] = chunks(I["L0_ffn_router_w"].T)
    A["l0f_w"] = np.stack([expert(I["L0_ffn_w_gate"][e].T, I["L0_ffn_w_up"][e].T, I["L0_ffn_w_down"][e].T) for e in range(8)])
    twice = lambda a: np.concatenate([a, a], axis=0)
    A["l1s_in"], A["l1s_gate"] = chunks(I["L1_attn_in_w"].T), chunks(I["L1_attn_gate_w"].T)
    A["l1s_dtw"], A["l1s_dtb"] = np.ascontiguousarray(I["L1_attn_dt_w"].T), twice(I["L1_attn_dt_b"].reshape(-1, 1))
    A["l1s_out"], A["l1s_Alog"] = twice(I["L1_attn_out_w"].T), twice(I["L1_attn_A_log"])
    A["l1s_B"], A["l1s_C"] = twice(I["L1_attn_Bp_w"].T), twice(I["L1_attn_Cp_w"].T)
    A["l1s_norm"] = cols(I["L1_attn_norm2_w"])
    for n in ("Wq", "Wk", "Wv", "Wo"):
        A["l2a_" + n] = chunks(I["L2_attn_" + n])
    A["l2a_bo"] = row(I["L2_attn_bo"])
    A["ctx"] = np.ascontiguousarray(I["ctx_1024"])
    A["l2f_W1"], A["l2f_W2"] = chunks(I["L2_ffn_W1"]), chunks(I["L2_ffn_W2"])
    A["l2f_b1"], A["l2f_b2"], A["l2f_theta"] = cols(I["L2_ffn_b1"]), row(I["L2_ffn_b2"]), cols(I["L2_ffn_quantum_phases"])
    A["l2f_wr"], A["l2f_wi"] = cols(I["L2_ffn_quantum_weights_real"]), cols(I["L2_ffn_quantum_weights_imag"])
    A["l3a_w"] = chunks(np.concatenate([I["L3_attn_Wq"].T, I["L3_attn_Wk"][0].T, I["L3_attn_Wk"][1].T,
                                       I["L3_attn_Wv"][0].T, I["L3_attn_Wv"][1].T], axis=1))
    A["l3a_bias"] = row(np.concatenate([I["L3_attn_bq"], I["L3_attn_bk"].reshape(-1), I["L3_attn_bv"].reshape(-1)]))
    A["l3a_Wo"], A["l3a_bo"] = chunks(I["L3_attn_Wo"].T), row(I["L3_attn_bo"])
    A["l3a_g"], A["l3a_b"] = cols(I["L3_attn_ln_g"]), cols(I["L3_attn_ln_b"])
    A["l3f_W1"], A["l3f_W2"], A["l3f_b1"] = chunks(I["L3_ffn_W1"].T), chunks(I["L3_ffn_W2"].T), cols(I["L3_ffn_b1"])
    A["l3f_b2"] = np.ascontiguousarray(np.broadcast_to(I["L3_ffn_b2"].reshape(1, D), (P, D)))
    for n in ("Wq", "Wk", "Wv", "Wk_ip", "Wv_ip", "Wk_ap", "Wv_ap", "Wo"):
        A["l3x_" + n] = chunks(I["L3_xattn_" + n])
    A["l3x_bo"] = row(I["L3_xattn_bo"])
    ctx = I["ctx_1024"]
    A["ctx_packed"] = chunks(np.concatenate([ctx[:, a:a + n].reshape(-1, D) for a, n in zip(SEG0, SEG)]).T)
    at = np.clip(np.arange(P - 1 + SEG[0]) - (P - 1), -MAXREL, MAXREL) + MAXREL
    A["l3x_relk"] = twice(np.ascontiguousarray(I["L3_xattn_rel_k"][at].T))
    at = np.clip(np.arange(SEG[0])[:, None] - np.arange(NREL + 1)[None, :], -MAXREL, MAXREL) + MAXREL
    A["l3x_relv"] = np.ascontiguousarray(I["L3_xattn_rel_v"][at].reshape(SEG[0], -1))
    both = np.stack([I["L3_xattn_alpha"], I["L3_xattn_beta"]]).reshape(1, 2)
    A["l3x_gates"] = np.ascontiguousarray(np.broadcast_to(both, (P, 2)))
    A["l1f_router"] = chunks(I["L1_ffn_router_w"].T)
    A["l1f_rbias"] = row(I["L1_ffn_routing_bias"])
    A["l1f_w"] = np.stack([expert(I["L1_ffn_gate_w"][e], I["L1_ffn_up_w"][e], I["L1_ffn_down_w"][e]) for e in range(8)]
                          + [expert(I["L1_ffn_shared_gate"].T, I["L1_ffn_shared_up"].T, I["L1_ffn_shared_down"].T)])


def used_inputs():
    t = set(STAGES)
    names = {"x", "ctxT"}
    names |= {f"{k}_{w}" for k in t for w in ("Wq", "Wk", "Wv", "Wo", "bq", "bk", "bv", "bo", "norm", "router", "rbias", "w", "W1", "W2", "b1", "b2",
                                          "theta", "wr", "wi", "bias", "g", "b")}
    if "l0x" in t:
        names |= {"mask_bc"}
    if "l1a" in t:
        names |= {"l1s_" + n for n in ("in", "gate", "dtw", "dtb", "out", "Alog", "B", "C", "norm")}
    if "l2x" in t:
        names |= {"ctx"}
    if "l3x" in t:
        names |= {"ctx_packed"} | {"l3x_" + n for n in ("Wk_ip", "Wk_ap", "Wv_ip", "Wv_ap", "relk", "relv", "gates")}
    if "l1x" in t:
        names |= {"maskT", "nbias_bc"}
    return names
def chunks(a):
    a = np.asarray(a)
    return np.ascontiguousarray(a.reshape(-1, P, a.shape[-1]).transpose(1, 0, 2).reshape(P, -1))


def cols(a):
    return np.ascontiguousarray(np.asarray(a).reshape(-1, P).T)


def row(a):
    return np.ascontiguousarray(np.asarray(a).reshape(1, -1))


def layout(I):
    A = {"x": np.ascontiguousarray(I["x"])}
    ctx = np.asarray(I["ctx_1024"])
    A["ctxT"] = chunks(ctx.reshape(NB * P, D).T)
    m = np.ascontiguousarray(I["mask_BxS2_bf1"]).view(np.uint8).reshape(1, NB * P)
    A["mask_bc"] = np.ascontiguousarray(np.broadcast_to(m, (P, NB * P))).view(np.uint32)
    m = np.ascontiguousarray(I["mask_BxSxS2_bk0"]).view(np.uint8)
    A["maskT"] = np.ascontiguousarray(m.transpose(2, 0, 1).reshape(P, NB * P)).view(np.uint32)
    A["nbias_bc"] = np.ascontiguousarray(np.broadcast_to(np.asarray(I["L1_xattn_nbias"]).reshape(1, 1), (P, 1)))
    for n, o in (("Wq", "Wq"), ("Wk", "Wk"), ("Wv", "Wv"), ("Wp", "Wo")):
        A["l0a_" + o] = chunks(np.asarray(I["L0_attn_" + n]).T)
    A["l0a_bo"] = row(I["L0_attn_bp"])
    for n in ("Wq", "Wk", "Wv", "Wo"):
        A["l0x_" + n] = chunks(np.asarray(I["L0_xattn_" + n]).T)
    A["l0x_bq"], A["l0x_bk"] = cols(I["L0_xattn_bq"]), cols(I["L0_xattn_bk"])
    A["l0x_bv"], A["l0x_bo"] = row(I["L0_xattn_bv"]), row(I["L0_xattn_bo"])
    qkv = np.asarray(I["L1_attn_qkv_w"])
    for i, n in enumerate(("Wq", "Wk", "Wv")):
        A["l1a_" + n] = chunks(qkv[i * D:(i + 1) * D].T)
    A["l1a_Wo"] = chunks(np.asarray(I["L1_attn_o_w"]).T)
    A["l1a_norm"] = cols(I["L1_attn_norm1_w"])
    A["l1x_Wq"] = chunks(np.asarray(I["L1_xattn_Wq"]).T)
    kv = np.asarray(I["L1_xattn_Wkv"])
    A["l1x_Wk"], A["l1x_Wv"] = chunks(kv[:D].T), chunks(kv[D:].T)
    A["l1x_Wo"] = chunks(np.asarray(I["L1_xattn_Wo"]).T)
    more_layout(I, A)
    return {n: a for n, a in A.items() if n in used_inputs()}


def program(nc, A):
    G = Shared()
    with ExitStack() as ctx:
        def sb(name, shape, dt=F32):
            return ctx.enter_context(nc.sbuf_tensor(name, shape, dt))
        G.x = sb("x", [P, NB * D])
        G.mv, G.rrms = sb("mean_var", [P, 2 * NB]), sb("rrms", [P, NB])
        G.ctxT = sb("ctxT", [P, DC * NB * P])
        G.ident, G.identb = sb("ident", [P, P]), sb("identb", [P, P], BF16)
        G.triu, G.neg_upper = sb("triu", [P, P]), sb("neg_upper", [P, P], BF16)
        G.headmask = sb("headmask", [P, HC])
        G.neg1e5 = sb("ln_eps", [P, 1])
        G.pad = sb("pad", [1, 16])
        G.ones_row = sb("ones_row", [1, P])
        setup(nc, G, A)
        for sublayer in STAGES:
            SUBLAYERS[sublayer](nc, G, A)
        finish(nc, G, A)


def kernel(**inputs):
    import concourse.bacc as bacc
    from concourse.bass_utils import run_bass_kernel_spmd

    nc = bacc.Bacc("TRN2", target_bir_lowering=False, num_devices=1)
    arrays = layout(inputs)
    A = {n: nc.dram_tensor(f"in_{n}", a.shape, mybir.dt.from_np(a.dtype), kind="ExternalInput").ap()
         for n, a in arrays.items()}
    A["out"] = nc.dram_tensor("out_x", (NB, P, D), F32, kind="ExternalOutput").ap()
    program(nc, A)
    r = run_bass_kernel_spmd(nc, [{f"in_{n}": a for n, a in arrays.items()}], core_ids=[0])
    return r.results[0]["out_x"]
```

```python
from contextlib import ExitStack

import numpy as np

import concourse.bass as bass
from concourse import mybir

ALU = mybir.AluOpType
ACT = mybir.ActivationFunctionType
AX = mybir.AxisListType
F32 = mybir.dt.float32
BF16 = mybir.dt.bfloat16
F32R = mybir.dt.float32r
U8 = mybir.dt.uint8
U32 = mybir.dt.uint32

P = 128
NB = 16
D = 256
DC = D // P
H = 16
HD = D // H
HC = H // DC
GB = 4
NG = NB // GB
GT = GB * P
LN_EPS = 1e-5


class Step:

    def __init__(self, eng, sem):
        self.eng, self.sem, self.n, self.base = eng, sem, 0, None

    def sig(self, ins):
        self.n += 1
        ins.then_inc(self.sem, 1)
        return ins

    def wait(self):
        self.eng.wait_ge(self.sem, self.n if self.base is None else self.base + self.n)

    def do(self, ins):
        self.sig(ins)
        self.wait()

    def enter(self, var, per, start=0):
        self.before, self.per, self.n = self.n, per, 0
        self.base = var * per + (self.before - start * per)

    def leave(self, times):
        assert self.n == self.per, (self.n, self.per)
        self.n, self.base = self.before + times * self.per, None


def past(eng, sem, value):
    if not (isinstance(value, int) and value <= 0):
        eng.wait_ge(sem, value)


class Region:

    def __init__(self, nc, tag):
        self.nc, self.tag, self.ctx, self.sems = nc, tag, ExitStack(), []

    def sb(self, name, shape, dt=F32):
        return self.ctx.enter_context(self.nc.sbuf_tensor(f"{self.tag}_{name}", shape, dt))

    def ps(self, name, shape, dt=F32):
        return self.ctx.enter_context(self.nc.psum_tensor(f"{self.tag}_{name}", shape, dt))

    def sem(self, name):
        self.sems.append(self.nc.alloc_semaphore(name=f"{self.tag}_{name}"))
        return self.sems[-1]

    def block(self):
        return self.ctx.enter_context(self.nc.Block())

    def close(self):
        self.ctx.close()
        self.nc.clear_and_free_semaphores(self.sems)
        self.nc.all_engine_barrier()


class Shared:
    pass


def all_row_stats(nc, dve, step, G, st6, batches=range(NB), rows=None):
    rows = G.x if rows is None else rows
    for b in batches:
        ins = nc.vector.bn_stats(out=st6[:, b * 6:(b + 1) * 6], in_=rows[:, b * D:(b + 1) * D])
    step.do(ins)
    for b in batches:
        ins = nc.vector.bn_aggr(out=G.mv[:, b * 2:b * 2 + 2], in_=st6[:, b * 6:(b + 1) * 6])
    step.do(ins)


def means(G):
    return G.mv[:, :].rearrange("p (b k) -> p k b", k=2)[:, 0, :]


def variances(G):
    return G.mv[:, :].rearrange("p (b k) -> p k b", k=2)[:, 1, :]


def setup(nc, G, A):
    R = Region(nc, "setup")
    s_load, s_ctx, s_step, s_pool = [R.sem(f"x{g}_loaded") for g in range(NG)], R.sem("context_loaded"), R.sem("dve_step"), R.sem("pool_step")
    st6 = R.sb("st6", [P, 6 * NB])
    block = R.block()

    @block.sync
    def _(sp):
        for g in range(NG):
            sp.dma_start(G.x[:, g * GB * D:(g + 1) * GB * D].rearrange("p (b d) -> p b d", b=GB),
                         A["x"][g * GB:(g + 1) * GB].rearrange("b p d -> p b d")).then_inc(s_load[g], 16)
        sp.dma_start(G.ctxT[:, :], A["ctxT"]).then_inc(s_ctx, 16)
        sp.wait_ge(s_ctx, 16)

    @block.gpsimd
    def _(pool):
        step = Step(pool, s_pool)
        step.sig(nc.gpsimd.memset(G.ident[:, :], 0.0))
        step.sig(nc.gpsimd.memset(G.triu[:, :], 1.0))
        step.sig(nc.gpsimd.memset(G.headmask[:, :], 1.0))
        step.sig(nc.gpsimd.memset(G.neg_upper[:, :], 0.0))
        step.sig(nc.gpsimd.memset(G.neg1e5[:, :], LN_EPS))
        step.do(nc.gpsimd.memset(G.ones_row[:, :], 1.0))
        step.sig(nc.gpsimd.affine_select(out=G.ident[:, :], in_=G.ident[:, :], compare_op=ALU.not_equal, fill=1.0,
                                         base=0, pattern=[[-1, P]], channel_multiplier=1))
        step.sig(nc.gpsimd.affine_select(out=G.triu[:, :], in_=G.triu[:, :], compare_op=ALU.is_ge, fill=0.0,
                                         base=0, pattern=[[1, P]], channel_multiplier=-1))
        step.sig(nc.gpsimd.affine_select(out=G.neg_upper[:, :], in_=G.neg_upper[:, :], compare_op=ALU.is_ge,
                                         fill=-1e30, base=0, pattern=[[-1, P]], channel_multiplier=1))
        step.do(nc.gpsimd.affine_select(out=G.headmask[:, :], in_=G.headmask[:, :], compare_op=ALU.is_ge, fill=0.0,
                                        base=0, pattern=[[-HD, HC]], channel_multiplier=1))
        step.do(nc.gpsimd.affine_select(out=G.headmask[:, :], in_=G.headmask[:, :], compare_op=ALU.is_ge, fill=0.0,
                                        base=HD - 1, pattern=[[HD, HC]], channel_multiplier=-1))
        step.do(nc.gpsimd.tensor_copy(G.identb[:, :], G.ident[:, :]))

    @block.vector
    def _(dve):
        step = Step(dve, s_step)
        for g in range(NG):
            dve.wait_ge(s_load[g], 16)
            all_row_stats(nc, dve, step, G, st6, range(g * GB, (g + 1) * GB))

    R.close()


def finish(nc, G, A):
    R = Region(nc, "finish")
    s_out = R.sem("result_stored")
    block = R.block()

    @block.sync
    def _(sp):
        sp.dma_start(A["out"].rearrange("b p d -> p b d"), G.x[:, :].rearrange("p (b d) -> p b d", b=NB)).then_inc(s_out, 16)
        sp.wait_ge(s_out, 16)

    R.close()
def attention16(nc, G, A, tag, kind, w, normed="layer", cross=False, biased=False, out_bias=None):
    natural = kind in ("softmax", "causal")
    HHP = H // 2 * P
    R = Region(nc, tag)
    wq, wk, wv, wo = (R.sb(n, [P, DC * D]) for n in ("wq", "wk", "wv", "wo"))
    st6 = R.sb("st6", [P, 6 * NB])
    rstd, std = R.sb("rstd", [P, NB]), R.sb("std", [P, NB])
    xn = R.sb("xn", [P, D])
    xnT = R.sb("xnT", [P, D])
    qk = R.sb("qk", [P, 2 * D])
    bd = R.sb("bd", [P, H * P])
    PT = R.sb("PT", [P, H * P])
    V = R.sb("V", [P, H * (HD + 1)])
    osb, oT = R.sb("osb", [P, D]), R.sb("oT", [P, D])
    rden, mx = R.sb("rden", [P, H]), R.sb("mx", [P, H])
    if natural:
        Pn = R.sb("Pn", [P, H * P])
    if kind == "linear":
        elu = R.sb("elu", [P, 2 * D])
    if cross:
        srcT = R.sb("srcT", [P, D])
    else:
        srcT = xnT
    if biased:
        bq, bk, bv = R.sb("bq", [P, DC]), R.sb("bk", [P, DC]), R.sb("bv", [1, D])
    if out_bias:
        bo = R.sb("bo", [1, D])
    if kind == "softmax":
        m8, mbc = R.sb("m8", [P, NB * P // 4], U32), R.sb("mbc", [P, NB * P])
        fill, ones = R.sb("fill", [P, NB * P], BF16), R.sb("ones", [P, P], BF16)
        piece = R.sb("piece", [P, 1])
    if kind == "relu2":
        m8, keep = R.sb("m8", [P, NB * P // 4], U32), R.sb("keep", [P, NB * P])
        nbias = R.sb("nbias", [P, 1])
    if normed == "rms":
        nw = R.sb("nw", [P, DC])

    psX = R.ps("psX", [P, 512])
    psQK = R.ps("psQK", [P, 512])
    psVY = R.ps("psVY", [P, 512])
    psO = R.ps("psO", [P, 512])
    psS = R.ps("psS", [P, H * P])

    loaded, var_ready, std_ready, rstd_ready = (R.sem(n) for n in ("weights_loaded", "ones_ready", "std_ready", "rstd_ready"))
    mask_ready = R.sem("mask_ready")
    xn_ready, xt_done, xnT_ready, qk_done, qk_ready, bd_ready = (R.sem(n) for n in (
        "xn_ready", "xT_done", "xnT_ready", "qk_done", "qk_ready", "bd_ready"))
    s_done, shifted, p_ready, pt_done, pt_ready, pt_half = (R.sem(n) for n in (
        "scores_done", "shifted", "p_ready", "pT_done", "pT_ready", "pT_half_ready"))
    v_done, v_ready, o_done, osb_ready, ot_done, ot_ready, y_done, x_ready = (R.sem(n) for n in (
        "v_done", "v_ready", "o_done", "o_ready", "oT_done", "oT_ready", "y_done", "x_ready"))
    src_ready, elu_in, elu_out, masked_ready = (R.sem(n) for n in ("src_ready", "elu_in", "elu_out", "masked"))
    s_step = R.sem("dve_step")
    a_step = R.sem("act_step")
    block = R.block()

    loads = [(wq, A[w + "Wq"]), (wk, A[w + "Wk"]), (wv, A[w + "Wv"]), (wo, A[w + "Wo"])]
    if biased:
        loads += [(bq, A[w + "bq"]), (bk, A[w + "bk"]), (bv, A[w + "bv"])]
    if out_bias:
        loads += [(bo, A[w + "bo"])]
    if kind == "softmax":
        loads += [(m8, A["mask_bc"])]
    if kind == "relu2":
        loads += [(m8, A["maskT"]), (nbias, A["nbias_bc"])]
    if normed == "rms":
        loads += [(nw, A[w + "norm"])]
    NL = 16 * len(loads)
    last = NB - 1
    score_scale = 1.0 if kind == "linear" else HD ** -0.5
    den_eps = {"linear": 1e-6, "relu2": 1e-32}.get(kind, 0.0)
    stat, spread = (qk[:, 0:D], qk[:, D:2 * D]) if natural else (qk[:, D:2 * D], qk[:, 0:D])

    @block.sync
    def _(sp):
        for dst, src in loads:
            sp.dma_start(dst[:, :], src).then_inc(loaded, 16)
        sp.wait_ge(loaded, NL)

    @block.gpsimd
    def _(pool):
        def source(b):
            if cross:
                past(pool, v_done, b)
                nc.gpsimd.tensor_copy(srcT[:, :].rearrange("p (c t) -> p c t", c=DC),
                                      G.ctxT[:, :].rearrange("p (c n) -> p c n", c=DC)[:, :, bass.ds(b * P, P)])\
                    .then_inc(src_ready, 1)

        def spread_heads(b):
            pool.wait_ge(qk_ready, b + 1)
            past(pool, s_done, 2 * b)
            for c in range(DC):
                nc.gpsimd.tensor_tensor(
                    bd[:, c * HC * P:(c + 1) * HC * P].rearrange("p (h t) -> p h t", h=HC),
                    spread[:, c * P:(c + 1) * P].unsqueeze(1).to_broadcast([P, HC, P]),
                    G.headmask[:, :].unsqueeze(2).to_broadcast([P, HC, P]), ALU.mult).then_inc(bd_ready, 1)

        source(0)
        spread_heads(0)
        with pool.Fori(1, NB) as b:
            source(b)
            spread_heads(b)

    @block.tensor
    def _(pe):
        pe.wait_ge(loaded, NL)
        pe.wait_ge(var_ready, 1)

        def transpose_x(b):
            pe.wait_ge(xn_ready, b + 1)
            past(pe, xnT_ready, b)
            for c in range(DC):
                last_ = nc.tensor.transpose(psX[:, c * P:(c + 1) * P], xn[:, c * P:(c + 1) * P], G.ident[:, :])
            last_.then_inc(xt_done, 1)

        def project_qk(b):
            pe.wait_ge(xnT_ready, b + 1)
            if cross:
                pe.wait_ge(src_ready, b + 1)
            for i, (wt, act_T) in enumerate(((wq, xnT), (wk, srcT))):
                for j in range(DC):
                    for c in range(DC):
                        last_ = nc.tensor.matmul(psQK[:, (i * DC + j) * P:(i * DC + j + 1) * P],
                                                 wt[:, c * D + j * P:c * D + (j + 1) * P],
                                                 act_T[:, c * P:(c + 1) * P], start=(c == 0), stop=(c == DC - 1))
            last_.then_inc(qk_done, 1)

        def project_v(b, first=False):
            past(pe, v_ready, b)
            if not first:
                past(pe, x_ready, b - 1)
            for c in range(DC):
                last_ = nc.tensor.matmul(psVY[:, 0:D], srcT[:, c * P:(c + 1) * P], wv[:, c * D:(c + 1) * D],
                                         start=(c == 0), stop=(c == DC - 1 and not biased))
            if biased:
                last_ = nc.tensor.matmul(psVY[:, 0:D], G.ones_row[:, :], bv[:, :], start=False, stop=True)
            last_.then_inc(v_done, 1)

        def scores(b):
            if kind == "softmax":
                pe.wait_ge(mask_ready, 1)
            for g in range(4):
                c = u = g // 2
                if g % 2 == 0:
                    pe.wait_ge(bd_ready, DC * b + c + 1)
                    if natural:
                        past(pe, (pt_half, pt_ready)[u], b)
                    else:
                        past(pe, pt_ready if kind == "linear" else shifted, 2 * b + u - 1)
                last_ = nc.tensor.matmul(psS[:, g * 512:(g + 1) * 512], stat[:, c * P:(c + 1) * P],
                                         bd[:, g * 512:(g + 1) * 512], start=True, stop=not natural)
                if kind == "softmax":
                    last_ = nc.tensor.matmul(psS[:, g * 512:(g + 1) * 512], ones[:, :],
                                             fill[:, bass.ds(b * P, P)].unsqueeze(1).to_broadcast([P, 4, P]),
                                             start=False, stop=True)
                if kind == "causal":
                    last_ = nc.tensor.matmul(psS[:, g * 512:(g + 1) * 512], G.identb[:, :],
                                             G.neg_upper[:, :].unsqueeze(1).to_broadcast([P, 4, P]),
                                             start=False, stop=True)
                if g % 2 == 1:
                    last_.then_inc(s_done, 1)

        def transpose_p(b):
            if natural:
                for u in range(2):
                    pe.wait_ge(p_ready, 2 * b + u + 1)
                    for h in range(u * H // 2, (u + 1) * H // 2):
                        last_ = nc.tensor.transpose(psS[:, h * P:(h + 1) * P], Pn[:, h * P:(h + 1) * P], G.ident[:, :])
                    last_.then_inc(pt_done, 1)

        def weigh_values(b):
            pe.wait_ge(v_ready, b + 1)
            past(pe, ot_ready, b)
            for h in range(H):
                if h % (H // 2) == 0:
                    u = h // (H // 2)
                    if natural:
                        pe.wait_ge((pt_half, pt_ready)[u], b + 1)
                    else:
                        pe.wait_ge(pt_ready if kind == "linear" else pt_half, 2 * b + u + 1)
                last_ = nc.tensor.matmul(psO[:, h * (HD + 1):(h + 1) * (HD + 1)], PT[:, h * P:(h + 1) * P],
                                         V[:, h * (HD + 1):(h + 1) * (HD + 1)], start=True, stop=True)
            last_.then_inc(o_done, 1)

        def transpose_o(b):
            pe.wait_ge(osb_ready, b + 1)
            for c in range(DC):
                last_ = nc.tensor.transpose(psO[:, c * P:(c + 1) * P], osb[:, c * P:(c + 1) * P], G.ident[:, :])
            last_.then_inc(ot_done, 1)

        def project_out(b, more):
            if more:
                pe.wait_ge(v_ready, b + 2)
            pe.wait_ge(ot_ready, b + 1)
            past(pe, x_ready, b)
            for c in range(DC):
                last_ = nc.tensor.matmul(psVY[:, D:2 * D], oT[:, c * P:(c + 1) * P], wo[:, c * D:(c + 1) * D],
                                         start=(c == 0), stop=(c == DC - 1 and not out_bias))
            if out_bias:
                last_ = nc.tensor.matmul(psVY[:, D:2 * D], G.ones_row[:, :], bo[:, :], start=False, stop=True)
            last_.then_inc(y_done, 1)

        def body(b, more, first=False):
            scores(b)
            if not first:
                transpose_o(b - 1)
            if more:
                transpose_x(b + 1)
            if not first:
                project_out(b - 1, True)
            if more:
                project_qk(b + 1)
            transpose_p(b)
            weigh_values(b)
            if more:
                project_v(b + 1)

        transpose_x(0)
        project_qk(0)
        project_v(0, first=True)
        body(0, True, first=True)
        with pe.Fori(1, last) as b:
            body(b, True)
        body(last, False)
        transpose_o(last)
        project_out(last, False)

    @block.scalar
    def _(act):
        step = Step(act, a_step)
        if normed == "layer":
            nc.scalar.activation(std[:, :], variances(G), ACT.Sqrt, bias=G.neg1e5[:, 0:1]).then_inc(std_ready, 1)
        act.wait_ge(loaded, NL)

        def take_xT(b):
            act.wait_ge(xt_done, b + 1)
            past(act, v_done, b)
            past(act, qk_done, b)
            for c in range(DC):
                scale = nw[:, c:c + 1] if normed == "rms" else 1.0
                ins = nc.scalar.activation(xnT[:, c * P:(c + 1) * P], psX[:, c * P:(c + 1) * P], ACT.Copy, scale=scale)
            ins.then_inc(xnT_ready, 1)

        def take_qk(b):
            if kind == "relu2":
                return
            if kind == "linear":
                act.wait_ge(elu_in, b + 1)
                nc.scalar.activation(elu[:, :], elu[:, :], ACT.Exp).then_inc(elu_out, 1)
                return
            act.wait_ge(qk_done, b + 1)
            past(act, s_done, 2 * b)
            past(act, bd_ready, DC * b)
            if biased:
                for c in range(DC):
                    ins = nc.scalar.activation(qk[:, c * P:(c + 1) * P], psQK[:, c * P:(c + 1) * P], ACT.Identity,
                                               bias=bq[:, c:c + 1])
                ins.then_inc(masked_ready, 1)
            else:
                nc.scalar.activation(qk[:, :], psQK[:, :], ACT.Copy).then_inc(qk_ready, 1)

        def exponentials(b, u):
            if natural:
                act.wait_ge(shifted, 2 * b + u + 1)
                half = Pn[:, u * HHP:(u + 1) * HHP]
                nc.scalar.activation(half, half, ACT.Exp, scale=score_scale).then_inc(p_ready, 1)

        def weights(b):
            if kind == "relu2":
                for u in range(2):
                    act.wait_ge(s_done, 2 * b + u + 1)
                    past(act, o_done, b)
                    nc.scalar.activation(PT[:, u * HHP:(u + 1) * HHP], psS[:, u * HHP:(u + 1) * HHP], ACT.Relu,
                                         scale=score_scale, bias=nbias[:, 0:1]).then_inc(shifted, 1)

        def take_pT(b):
            if natural:
                act.wait_ge(pt_done, 2 * b + 1)
                past(act, o_done, b)
                nc.scalar.activation(PT[:, 0:1024], psS[:, 0:1024], ACT.Copy).then_inc(pt_half, 1)
            if kind == "relu2":
                for u in range(2):
                    act.wait_ge(masked_ready, 2 * b + u + 1)
                    half = PT[:, u * HHP:(u + 1) * HHP]
                    nc.scalar.activation(half, half, ACT.Square).then_inc(pt_half, 1)

        def take_oT(b):
            act.wait_ge(ot_done, b + 1)
            past(act, y_done, b)
            nc.scalar.activation(oT[:, :], psO[:, 0:D], ACT.Copy).then_inc(ot_ready, 1)

        def body(b, more, first=False):
            weights(b)
            if not first:
                take_oT(b - 1)
            if more:
                take_xT(b + 1)
            exponentials(b, 0)
            exponentials(b, 1)
            if more:
                take_qk(b + 1)
            take_pT(b)

        take_xT(0)
        take_qk(0)
        body(0, True, first=True)
        with act.Fori(1, last) as b:
            body(b, True)
        body(last, False)
        take_oT(last)

    @block.vector
    def _(dve):
        step = Step(dve, s_step)
        nc.vector.memset(V[:, :], 1.0).then_inc(var_ready, 1)
        if normed == "layer":
            dve.wait_ge(std_ready, 1)
            nc.vector.reciprocal(rstd[:, :], std[:, :]).then_inc(rstd_ready, 1)
            dve.wait_ge(rstd_ready, 1)
        dve.wait_ge(var_ready, 1)
        dve.wait_ge(loaded, NL)
        if kind == "softmax":
            step.do(nc.vector.tensor_copy(mbc[:, :], m8[:, :].bitcast(U8)))
            step.sig(nc.vector.memset(ones[:, :], 1.0))
            step.do(nc.vector.memset(piece[:, :], 0.0))
            rest = np.float32(1e8 / score_scale)
            for r in (0, 32, 64):
                part = (rest.view(np.uint32) & np.uint32(0xFFFF0000)).view(np.float32)
                rest = np.float32(rest - part)
                step.do(nc.vector.memset(piece[r:r + 1, :], float(part)))
            assert rest == 0
            nc.vector.tensor_scalar(fill[:, :], mbc[:, :], -1.0, piece[:, 0:1], ALU.add, ALU.mult).then_inc(mask_ready, 1)
        if kind == "relu2":
            step.do(nc.vector.tensor_copy(keep[:, :], m8[:, :].bitcast(U8)))
            step.do(nc.vector.tensor_scalar(keep[:, :], keep[:, :], -1.0, 1.0, ALU.mult, ALU.add))

        def normalise(b):
            past(dve, xt_done, b)
            xb = G.x[:, bass.ds(b * D, D)]
            if normed == "layer":
                nc.vector.tensor_scalar(xn[:, :], xb, G.mv[:, bass.ds(b * 2, 1)], rstd[:, bass.ds(b, 1)],
                                        ALU.subtract, ALU.mult).then_inc(xn_ready, 1)
            else:
                nc.vector.tensor_scalar(xn[:, :], xb, G.rrms[:, bass.ds(b, 1)], None, ALU.mult).then_inc(xn_ready, 1)

        def features(b):
            if kind == "linear":
                dve.wait_ge(qk_done, b + 1)
                nc.vector.tensor_scalar(elu[:, :], psQK[:, :], 0.0, None, ALU.min).then_inc(elu_in, 1)
                dve.wait_ge(elu_out, b + 1)
                past(dve, s_done, 2 * b)
                past(dve, bd_ready, DC * b)
                nc.vector.scalar_tensor_tensor(qk[:, :], psQK[:, :], 0.0, elu[:, :], ALU.max, ALU.add)\
                    .then_inc(qk_ready, 1)
            if kind == "relu2":
                dve.wait_ge(qk_done, b + 1)
                past(dve, s_done, 2 * b)
                past(dve, bd_ready, DC * b)
                nc.vector.tensor_copy(qk[:, :], psQK[:, :]).then_inc(qk_ready, 1)
            if biased:
                dve.wait_ge(masked_ready, b + 1)
                for c in range(DC):
                    ins = nc.vector.scalar_tensor_tensor(
                        qk[:, (DC + c) * P:(DC + c + 1) * P], psQK[:, (DC + c) * P:(DC + c + 1) * P], bk[:, c:c + 1],
                        mbc[:, bass.ds(b * P, P)], ALU.add, ALU.mult)
                ins.then_inc(qk_ready, 1)

        def shift(b):
            S3 = psS[:, :].rearrange("p (h t) -> p h t", h=H)
            P3 = PT[:, :].rearrange("p (h t) -> p h t", h=H)
            if natural:
                for u in range(2):
                    hs = slice(u * H // 2, (u + 1) * H // 2)
                    dve.wait_ge(s_done, 2 * b + u + 1)
                    step.do(nc.vector.tensor_reduce(mx[:, hs], S3[:, hs, :], AX.X, ALU.max))
                    past(dve, pt_done, 2 * b)
                    nc.vector.tensor_tensor(Pn[:, :].rearrange("p (h t) -> p h t", h=H)[:, hs, :], S3[:, hs, :],
                                            mx[:, hs].unsqueeze(2).to_broadcast([P, H // 2, P]), ALU.subtract).then_inc(shifted, 1)
            for u in range(2):
                hs = slice(u * H // 2, (u + 1) * H // 2)
                if kind == "linear":
                    dve.wait_ge(s_done, 2 * b + u + 1)
                    past(dve, o_done, b)
                    nc.vector.tensor_tensor(P3[:, hs, :], S3[:, hs, :], G.triu[:, :].unsqueeze(1).to_broadcast([P, H // 2, P]),
                                            ALU.mult).then_inc(pt_ready, 1)
                if kind == "relu2":
                    dve.wait_ge(shifted, 2 * b + u + 1)
                    nc.vector.tensor_tensor(P3[:, hs, :], P3[:, hs, :],
                                            keep[:, bass.ds(b * P, P)].unsqueeze(1).to_broadcast([P, H // 2, P]),
                                            ALU.mult).then_inc(masked_ready, 1)

        def take_pT(b):
            if natural:
                dve.wait_ge(pt_done, 2 * b + 2)
                past(dve, o_done, b)
                nc.vector.tensor_copy(PT[:, 1024:2048], psS[:, 1024:2048]).then_inc(pt_ready, 1)

        def take_v(b):
            dve.wait_ge(v_done, b + 1)
            past(dve, o_done, b)
            nc.vector.tensor_copy(V[:, :].rearrange("p (h e) -> p h e", h=H)[:, :, 0:HD],
                                  psVY[:, 0:D].rearrange("p (h e) -> p h e", h=H)).then_inc(v_ready, 1)

        def normalise_o(b):
            dve.wait_ge(o_done, b + 1)
            O3 = psO[:, 0:H * (HD + 1)].rearrange("p (h e) -> p h e", h=H)
            if den_eps:
                step.do(nc.vector.tensor_scalar(rden[:, :], O3[:, :, HD], den_eps, None, ALU.add))
                step.do(nc.vector.reciprocal(rden[:, :], rden[:, :]))
            else:
                step.do(nc.vector.reciprocal(rden[:, :], O3[:, :, HD]))
            past(dve, ot_done, b)
            nc.vector.tensor_tensor(osb[:, :].rearrange("p (h e) -> p h e", h=H), O3[:, :, 0:HD],
                                    rden[:, :].unsqueeze(2).to_broadcast([P, H, HD]), ALU.mult).then_inc(osb_ready, 1)

        def add_y(b):
            dve.wait_ge(y_done, b + 1)
            xb = G.x[:, bass.ds(b * D, D)]
            nc.vector.tensor_tensor(xb, xb, psVY[:, D:2 * D], ALU.add).then_inc(x_ready, 1)

        def body(b, more, first=False):
            if more:
                normalise(b + 1)
            shift(b)
            if not first:
                add_y(b - 1)
            if more:
                features(b + 1)
            take_pT(b)
            normalise_o(b)
            if more:
                take_v(b + 1)

        normalise(0)
        features(0)
        take_v(0)
        per = (2 if natural else 0) + (2 if den_eps else 1)
        body(0, True, first=True)
        with dve.Fori(1, last) as b:
            step.enter(b, per, start=1)
            body(b, True)
            step.leave(last - 1)
        body(last, False)
        add_y(last)
        dve.wait_ge(x_ready, NB)
        all_row_stats(nc, dve, step, G, st6)

    R.close()
def normalised_transpose(nc, G, tag, xT, router=None, logits=None, router_bias=None, loads=(), loaded=None):
    T, NPAIR, NBUF = NB * P, NB // 2, 4
    R = Region(nc, tag)
    rstd, std = R.sb("rstd", [P, NB]), R.sb("std", [P, NB])
    xn = [R.sb(f"xn{i}", [P, 2 * D]) for i in range(NBUF)]
    psX = [R.ps(f"psX{i}", [P, 512]) for i in range(NBUF)]
    std_ready, rstd_ready = R.sem("std_ready"), R.sem("rstd_ready")
    xn_ready, xt_done, xT_ready = R.sem("xn_ready"), R.sem("xT_done"), R.sem("xT_ready")
    if router is not None:
        rw, rb = R.sb("rw", [P, DC * 8]), R.sb("rb", [1, 8])
        psR = R.ps("psR", [P, 512])
        r_loaded, r_done, r_read = R.sem("router_loaded"), R.sem("router_done"), R.sem("router_read")
    block = R.block()
    NR = 0 if router is None else 16 + (16 if router_bias is not None else 0)

    @block.sync
    def _(sp):
        if router is not None:
            sp.dma_start(rw[:, :], router).then_inc(r_loaded, 16)
            if router_bias is not None:
                sp.dma_start(rb[:, :], router_bias).then_inc(r_loaded, 16)
        for dst, src in loads:
            sp.dma_start(dst, src).then_inc(loaded, 16)
        if router is not None:
            sp.wait_ge(r_loaded, NR)

    @block.vector
    def _(dve):
        dve.wait_ge(std_ready, 1)
        nc.vector.reciprocal(rstd[:, :], std[:, :]).then_inc(rstd_ready, 1)
        dve.wait_ge(rstd_ready, 1)
        for n in range(NPAIR):
            if n >= NBUF:
                dve.wait_ge(xt_done, n - NBUF + 1)
            for i in range(2):
                b = 2 * n + i
                ins = nc.vector.tensor_scalar(xn[n % NBUF][:, i * D:(i + 1) * D], G.x[:, b * D:(b + 1) * D], G.mv[:, 2 * b:2 * b + 1],
                                              rstd[:, b:b + 1], ALU.subtract, ALU.mult)
            ins.then_inc(xn_ready, 1)
        if router is not None:
            dve.wait_ge(r_done, 1)
            nc.vector.tensor_copy(logits[:, :], psR[:, 0:8 * NB]).then_inc(r_read, 1)
            dve.wait_ge(r_read, 1)

    @block.tensor
    def _(pe):
        def route(n):
            pe.wait_ge(xT_ready, n + 1)
            for b in (2 * n, 2 * n + 1):
                for c in range(DC):
                    last = nc.tensor.matmul(psR[:, b * 8:(b + 1) * 8], xT[:, c * T + b * P:c * T + (b + 1) * P], rw[:, c * 8:(c + 1) * 8],
                                            start=(c == 0), stop=(c == DC - 1 and router_bias is None))
                if router_bias is not None:
                    last = nc.tensor.matmul(psR[:, b * 8:(b + 1) * 8], G.ones_row[:, :], rb[:, :], start=False, stop=True)
            return last

        if router is not None:
            pe.wait_ge(r_loaded, NR)
        for n in range(NPAIR):
            pe.wait_ge(xn_ready, n + 1)
            if n >= NBUF:
                pe.wait_ge(xT_ready, n - NBUF + 1)
            for i in range(2):
                for c in range(DC):
                    last = nc.tensor.transpose(psX[n % NBUF][:, (c * 2 + i) * P:(c * 2 + i + 1) * P],
                                               xn[n % NBUF][:, i * D + c * P:i * D + (c + 1) * P], G.ident[:, :])
            last.then_inc(xt_done, 1)
            if router is not None and n >= 1:
                route(n - 1)
        if router is not None:
            route(NPAIR - 1).then_inc(r_done, 1)

    @block.scalar
    def _(act):
        nc.scalar.activation(std[:, :], variances(G), ACT.Sqrt, bias=G.neg1e5[:, 0:1]).then_inc(std_ready, 1)
        for n in range(NPAIR):
            act.wait_ge(xt_done, n + 1)
            nc.scalar.activation(xT[:, :].rearrange("p (c n) -> p c n", c=DC)[:, :, n * 2 * P:(n + 1) * 2 * P],
                                 psX[n % NBUF][:, :].rearrange("p (c t) -> p c t", c=DC), ACT.Copy).then_inc(xT_ready, 1)

    R.close()


def experts(nc, G, A, tag, softmax_router, shared):
    E, F = 8, 512
    FC = F // P
    WE = 2 * DC * F + FC * D
    n_experts = E + (1 if shared else 0)
    R = Region(nc, tag)
    xT = R.sb("xT", [P, DC * NB * P])
    prob, comb = R.sb("prob", [P, NB * E]), R.sb("comb", [P, (E + 1) * NB])
    st6 = R.sb("st6", [P, 6 * NB])
    W = R.sb("W", [P, WE])
    w_loaded = R.sem("weights_loaded")
    normalised_transpose(nc, G, tag + "_n", xT, A[tag + "_router"], prob, A.get(tag + "_rbias"), [(W[:, :], A[tag + "_w"][0])], w_loaded)

    Wh, Wl = ([R.sb(f"W_{n}{i}", [P, WE], F32R) for i in range(2)] for n in ("high", "low"))
    xh, xl = R.sb("x_high", [P, DC * NB * P], F32R), R.sb("x_low", [P, DC * NB * P], F32R)
    t1, t2, oh1, oh2 = (R.sb(n, [P, NB * E]) for n in ("t1", "t2", "oh1", "oh2"))
    m1, m2, key = (R.sb(n, [P, NB]) for n in ("m1", "m2", "key"))
    order = R.sb("order", [P, E])
    sg = [R.sb(f"sg{i}", [P, GT]) for i in range(2)]
    h = [R.sb(f"h{i}", [P, GT]) for i in range(2)]
    hh, hl = R.sb("h_high", [P, FC * GT], F32R), R.sb("h_low", [P, FC * GT], F32R)
    psG = [R.ps(f"psG{i}", [P, GT]) for i in range(2)]
    psU = [R.ps(f"psU{i}", [P, GT]) for i in range(2)]
    psY = [R.ps(f"psY{i}", [P, 512]) for i in range(4)]
    wh_ready, w_split = R.sem("weights_high"), R.sem("weights_split")
    xh_ready, x_split, hh_ready, h_split = R.sem("x_high_ready"), R.sem("x_split"), R.sem("h_high_ready"), R.sem("h_split")
    gu_done, sg_ready, h_ready, y_done, y_used = (R.sem(n) for n in ("gate_up_done", "silu_ready", "h_ready", "y_done", "y_used"))
    order_ready, routed, a_ready = R.sem("order_ready"), R.sem("logits_shifted"), R.sem("prob_ready")
    s_step = R.sem("dve_step")
    block = R.block()

    @block.sync
    def _(sp):
        for e in range(1, n_experts):
            sp.wait_ge(w_split, e)
            sp.dma_start(W[:, :], A[tag + "_w"][e]).then_inc(w_loaded, 16)
        sp.wait_ge(w_loaded, 16 * n_experts)

    @block.gpsimd
    def _(pool):
        for e in range(E):
            nc.gpsimd.memset(order[:, e:e + 1], float(E - e)).then_inc(order_ready, 1)
        for e in range(1, n_experts):
            pool.wait_ge(w_loaded, 16 * (e + 1))
            if e >= 2:
                pool.wait_ge(y_done, NG * (e - 1))
            nc.gpsimd.tensor_copy(Wh[e % 2][:, :], W[:, :]).then_inc(wh_ready, 1)
            pool.wait_ge(wh_ready, e + 1)
            nc.gpsimd.tensor_tensor(Wl[e % 2][:, :], W[:, :], Wh[e % 2][:, :].bitcast(F32), ALU.subtract).then_inc(w_split, 1)

    def tokens(t, g):
        return t[:, :].rearrange("p (c n) -> p c n", c=DC)[:, :, g * GT:(g + 1) * GT]

    def gate(w, c, j):
        return w[:, c * F + j * P:c * F + (j + 1) * P]

    def up(w, c, j):
        return w[:, DC * F + c * F + j * P:DC * F + c * F + (j + 1) * P]

    def down(w, j):
        return w[:, 2 * DC * F + j * D:2 * DC * F + (j + 1) * D]

    @block.tensor
    def _(pe):
        def group(n, g, i):
            for j in range(FC):
                pe.wait_ge(h_ready, n * FC + j + 1)
                for part, ps in ((gate, psG), (up, psU)):
                    for c in range(DC):
                        xs = bass.ds(g * GT + c * NB * P, GT)
                        for w, x in ((Wh, xh), (Wh, xl), (Wl, xh)):
                            last = nc.tensor.matmul(ps[j % 2][:, :], part(w[i], c, j), x[:, xs],
                                                    start=(c == 0 and w is Wh and x is xh), stop=(c == DC - 1 and w is Wl))
                last.then_inc(gu_done, 1)
            pe.wait_ge(y_used, n + 1)
            for j in range(FC):
                pe.wait_ge(h_split, n * FC + j + 1)
                for t in range(GB):
                    ts = slice(j * GT + t * P, j * GT + (t + 1) * P)
                    for a, w in ((hh, Wh), (hh, Wl), (hl, Wh)):
                        last = nc.tensor.matmul(psY[t][:, 0:D], a[:, ts], down(w[i], j),
                                                start=(j == 0 and a is hh and w is Wh), stop=(j == FC - 1 and a is hl))
            last.then_inc(y_done, 1)

        with pe.Fori(0, E // 2) as ep:
            for i in range(2):
                with pe.Fori(0, NG) as g:
                    pe.wait_ge(w_split, ep * 2 + i + 1)
                    pe.wait_ge(x_split, g + 1)
                    group(ep * (2 * NG) + (g + i * NG), g, i)
        if shared:
            pe.wait_ge(w_split, E + 1)
            with pe.Fori(0, NG) as g:
                group(g + E * NG, g, 0)

    @block.scalar
    def _(act):
        for g in range(NG):
            nc.scalar.activation(tokens(xh, g), tokens(xT, g), ACT.Copy).then_inc(xh_ready, 1)
            if g == 0:
                act.wait_ge(w_loaded, 16)
                nc.scalar.activation(Wh[0][:, :], W[:, :], ACT.Copy).then_inc(wh_ready, 1)
        act.wait_ge(routed, 1)
        nc.scalar.activation(prob[:, :], prob[:, :], ACT.Exp if softmax_router else ACT.Sigmoid).then_inc(a_ready, 1)

        def group(n):
            for j in range(FC):
                act.wait_ge(gu_done, n * FC + j + 1)
                act.wait_ge(h_ready, n * FC + j + 1)
                nc.scalar.activation(sg[j % 2][:, :], psG[j % 2][:, :], ACT.Silu).then_inc(sg_ready, 1)

        with act.Fori(0, n_experts * NG) as n:
            group(n)

    @block.vector
    def _(dve):
        step = Step(dve, s_step)
        p3, a3, b3 = (t[:, :].rearrange("p (b e) -> p b e", e=E) for t in (prob, t1, t2))
        o1, o2 = (t[:, :].rearrange("p (b e) -> p b e", e=E) for t in (oh1, oh2))
        order3 = order[:, :].unsqueeze(1).to_broadcast([P, NB, E])

        def wide(t):
            return t[:, :].unsqueeze(2).to_broadcast([P, NB, E])

        for i in range(2):
            nc.vector.memset(G.pad[:, 1 + i:2 + i], 0.0).then_inc(h_ready, 1)
        nc.vector.memset(G.pad[:, 3:4], 0.0).then_inc(y_used, 1)
        for g in range(NG):
            dve.wait_ge(xh_ready, g + 1)
            nc.vector.tensor_tensor(tokens(xl, g), tokens(xT, g), tokens(xh, g).bitcast(F32), ALU.subtract).then_inc(x_split, 1)
            if g == 0:
                dve.wait_ge(wh_ready, 1)
                nc.vector.tensor_tensor(Wl[0][:, :], W[:, :], Wh[0][:, :].bitcast(F32), ALU.subtract).then_inc(w_split, 1)
        if softmax_router:
            step.do(nc.vector.tensor_reduce(m1[:, :], p3, AX.X, ALU.max))
            nc.vector.tensor_tensor(p3, p3, wide(m1), ALU.subtract).then_inc(routed, 1)
        else:
            nc.vector.memset(G.pad[:, 4:5], 0.0).then_inc(routed, 1)
        dve.wait_ge(a_ready, 1)
        if softmax_router:
            step.do(nc.vector.tensor_reduce(m1[:, :], p3, AX.X, ALU.add))
            step.do(nc.vector.reciprocal(m2[:, :], m1[:, :]))
            step.do(nc.vector.tensor_tensor(p3, p3, wide(m2), ALU.mult))
        dve.wait_ge(order_ready, E)

        def best(src, mx, tmp, hot):
            step.do(nc.vector.tensor_reduce(mx[:, :], src, AX.X, ALU.max))
            step.do(nc.vector.tensor_tensor(tmp, src, wide(mx), ALU.is_equal))
            step.do(nc.vector.tensor_tensor(tmp, tmp, order3, ALU.mult))
            step.do(nc.vector.tensor_reduce(key[:, :], tmp, AX.X, ALU.max))
            step.do(nc.vector.tensor_tensor(hot, tmp, wide(key), ALU.is_equal))

        best(p3, m1, a3, o1)
        step.do(nc.vector.scalar_tensor_tensor(t2[:, :], oh1[:, :], -2.0, prob[:, :], ALU.mult, ALU.add))
        best(b3, m2, a3, o2)
        step.do(nc.vector.tensor_tensor(m1[:, :], m1[:, :], m2[:, :], ALU.add))
        step.do(nc.vector.reciprocal(m1[:, :], m1[:, :]))
        step.do(nc.vector.tensor_tensor(o1, o1, o2, ALU.add))
        step.do(nc.vector.tensor_tensor(o1, o1, p3, ALU.mult))
        step.sig(nc.vector.tensor_tensor(comb[:, 0:E * NB].rearrange("p (e b) -> p b e", e=E), o1, wide(m1), ALU.mult))
        step.do(nc.vector.memset(comb[:, E * NB:], 1.0))

        def group(n, g, col):
            for j in range(FC):
                dve.wait_ge(sg_ready, n * FC + j + 1)
                js = slice(j * GT, (j + 1) * GT)
                nc.vector.tensor_tensor(h[j % 2][:, :], sg[j % 2][:, :], psU[j % 2][:, :], ALU.mult).then_inc(h_ready, 1)
                dve.wait_ge(h_ready, n * FC + j + 3)
                nc.vector.tensor_copy(hh[:, js], h[j % 2][:, :]).then_inc(hh_ready, 1)
                dve.wait_ge(hh_ready, n * FC + j + 1)
                nc.vector.tensor_tensor(hl[:, js], h[j % 2][:, :], hh[:, js].bitcast(F32), ALU.subtract).then_inc(h_split, 1)
            dve.wait_ge(y_done, n + 1)
            for t in range(GB):
                xb = G.x[:, bass.ds(g * (GB * D) + t * D, D)]
                last = nc.vector.scalar_tensor_tensor(xb, psY[t][:, 0:D], comb[:, bass.ds(col + t, 1)], xb, ALU.mult, ALU.add)
            last.then_inc(y_used, 1)

        with dve.Fori(0, E // 2) as ep:
            for i in range(2):
                with dve.Fori(0, NG) as g:
                    group(ep * (2 * NG) + (g + i * NG), g, ep * (2 * NB) + (g * GB + i * NB))
        if shared:
            with dve.Fori(0, NG) as g:
                group(g + E * NG, g, g * GB + E * NB)
        dve.wait_ge(y_used, n_experts * NG + 1)
        all_row_stats(nc, dve, step, G, st6)

    R.close()
RMS_EPS = 1.1920929e-07
SC, ST = 64, 16


def rms_factors(nc, G, tag):
    R = Region(nc, tag)
    ms, rt, eps = R.sb("ms", [P, NB]), R.sb("rt", [P, NB]), R.sb("eps", [P, 1])
    s_step, ms_ready, root_ready = R.sem("dve_step"), R.sem("ms_ready"), R.sem("root_ready")
    block = R.block()

    @block.vector
    def _(dve):
        step = Step(dve, s_step)
        step.do(nc.vector.memset(eps[:, :], RMS_EPS))
        step.do(nc.vector.tensor_tensor(ms[:, :], means(G), means(G), ALU.mult))
        nc.vector.tensor_tensor(ms[:, :], ms[:, :], variances(G), ALU.add).then_inc(ms_ready, 1)
        dve.wait_ge(root_ready, 1)
        step.do(nc.vector.reciprocal(G.rrms[:, :], rt[:, :]))

    @block.scalar
    def _(act):
        act.wait_ge(ms_ready, 1)
        nc.scalar.activation(rt[:, :], ms[:, :], ACT.Sqrt, bias=eps[:, 0:1]).then_inc(root_ready, 1)

    R.close()


def normalise_in_place(nc, G, tag, saved):
    R = Region(nc, tag)
    rstd, std = R.sb("rstd", [P, NB]), R.sb("std", [P, NB])
    s_step, std_ready, saved_ready, x_ready = R.sem("dve_step"), R.sem("std_ready"), R.sem("saved"), R.sem("x_ready")
    block = R.block()

    @block.scalar
    def _(act):
        nc.scalar.activation(std[:, :], variances(G), ACT.Sqrt, bias=G.neg1e5[:, 0:1]).then_inc(std_ready, 1)
        for g in range(NG):
            xg = slice(g * GB * D, (g + 1) * GB * D)
            nc.scalar.activation(saved[:, xg], G.x[:, xg], ACT.Copy).then_inc(saved_ready, 1)

    @block.vector
    def _(dve):
        step = Step(dve, s_step)
        dve.wait_ge(std_ready, 1)
        step.do(nc.vector.reciprocal(rstd[:, :], std[:, :]))
        for b in range(NB):
            if b % GB == 0:
                dve.wait_ge(saved_ready, b // GB + 1)
            xb = G.x[:, b * D:(b + 1) * D]
            nc.vector.tensor_scalar(xb, xb, G.mv[:, b * 2:b * 2 + 1], rstd[:, b:b + 1], ALU.subtract, ALU.mult).then_inc(x_ready, 1)
        dve.wait_ge(x_ready, NB)
        step.do(nc.vector.tensor_tensor(variances(G), variances(G), rstd[:, :], ALU.mult))
        step.do(nc.vector.tensor_tensor(variances(G), variances(G), rstd[:, :], ALU.mult))
        step.do(nc.vector.memset(means(G), 0.0))

    R.close()


def selective_scan(nc, G, A, saved):
    NP2 = NB // 2
    R = Region(nc, "scan")
    inw, gatew = R.sb("inw", [P, DC * SC]), R.sb("gatew", [P, DC * SC])
    dtw, dtb, outw = R.sb("dtw", [P, P]), R.sb("dtb", [P, 1]), R.sb("outw", [P, D])
    bp, cp, alog = R.sb("bp", [P, ST]), R.sb("cp", [P, ST]), R.sb("alog", [P, ST])
    nw, Am = R.sb("nw", [P, DC]), R.sb("Am", [P, ST])
    bdB, bdC = R.sb("bdB", [P, ST * P]), R.sb("bdC", [P, ST * P])
    xn, hT = R.sb("xn", [P, 2 * D]), R.sb("hT", [P, 2 * D])
    zg = [R.sb(f"zg{i}", [P, 2 * P]) for i in range(2)]
    gg, dt, dtz = ([R.sb(f"{n}{i}", [P, P]) for i in range(2)] for n in ("gg", "dt", "dtz"))
    v, av, ev, lv = (R.sb(n, [P, P]) for n in ("v", "av", "ev", "lv"))
    eg, rg, y, yT = (R.sb(n, [P, P]) for n in ("eg", "rg", "y", "yT"))
    ab, u, st = R.sb("abar", [P, ST * P]), R.sb("u", [P, ST * P]), R.sb("states", [P, ST * P])
    st6 = R.sb("st6", [P, 6 * NB])
    psX, psZ, psY0, psY1 = (R.ps(n, [P, 512]) for n in ("psX", "psZ", "psY0", "psY1"))
    psY = (psY0, psY1)
    psB = R.ps("psB", [P, ST * P])
    S = Shared()
    S.dt_ready, S.abar_act = R.sem("dt_ready"), R.sem("abar_by_act")
    ones = R.sb("ones", [P, P - 1])
    HS = ST // 2
    S.loaded, S.zeroed, S.dt_loaded, S.aexp_ready = (R.sem(n) for n in ("loaded", "zeroed", "dt_loaded", "aexp_ready",))
    S.consts_ready, S.xn_ready, S.xT_done, S.hT_ready = (R.sem(n) for n in ("consts_ready", "xn_ready", "xT_done", "hT_ready",))
    S.z_done, S.z_ready, S.dt_done, S.b_done = (R.sem(n) for n in ("z_done", "z_ready", "dt_done", "b_done",))
    S.v_ready, S.abs_ready, S.log_ready, S.exp_ready = (R.sem(n) for n in ("v_ready", "abs_ready", "log_ready", "exp_ready",))
    S.abar_ready, S.u_ready, S.c_done = (R.sem(n) for n in ("abar_ready", "u_ready", "c_done",))
    S.yT_ready, S.y_done, S.summed, S.x_ready = (R.sem(n) for n in ("yT_ready", "y_done", "summed", "x_ready",))
    S.state_used, S.gate_exp, S.bias_ready, S.scanned = (R.sem(n) for n in ("state_used", "gate_exp", "bias_ready", "scanned",))
    s_step, a_step, p_step = R.sem("dve_step"), R.sem("act_step"), R.sem("pool_step")
    block = R.block()
    loads = [(inw, A["l1s_in"]), (gatew, A["l1s_gate"]), (dtb, A["l1s_dtb"]), (outw, A["l1s_out"]), (bp, A["l1s_B"]),
             (cp, A["l1s_C"]), (alog, A["l1s_Alog"]), (nw, A["l1s_norm"])]
    NL = 16 * len(loads)

    @block.sync
    def _(sp):
        for dst, src in loads:
            sp.dma_start(dst[:, :], src).then_inc(S.loaded, 16)
        sp.wait_ge(S.zeroed, 3)
        for i in range(2):
            sp.dma_start(dtw[i * SC:(i + 1) * SC, i * SC:(i + 1) * SC], A["l1s_dtw"]).then_inc(S.dt_loaded, 16)
        sp.wait_ge(S.dt_loaded, 32)

    @block.gpsimd
    def _(pool):
        step = Step(pool, p_step)
        for t in (bdB, bdC, dtw):
            nc.gpsimd.memset(t[:, :], 0.0).then_inc(S.zeroed, 1)
        nc.gpsimd.memset(ab[:, :], 0.0).then_inc(S.zeroed, 1)
        nc.gpsimd.memset(ones[:, :], 1.0).then_inc(S.zeroed, 1)
        pool.wait_ge(S.zeroed, 5)

        def body(p, i):
            pool.wait_ge(S.xn_ready, 2 * p + 2)
            xp = G.x[:, bass.ds(p * (2 * D), 2 * D)]
            nc.gpsimd.tensor_tensor(xp, xp, saved[:, bass.ds(p * (2 * D), 2 * D)], ALU.add).then_inc(S.summed, 1)
            pool.wait_ge(S.dt_ready, p + 1)
            past(pool, S.scanned, p)
            ab3 = ab[:, :].rearrange("p (s t) -> p s t", s=ST)[:, HS:, 1:]
            step.do(nc.gpsimd.tensor_tensor(ab3, dt[i][:, 1:].unsqueeze(1).to_broadcast([P, ST - HS, P - 1]),
                                            Am[:, HS:].unsqueeze(2).to_broadcast([P, ST - HS, P - 1]), ALU.mult))
            nc.gpsimd.tensor_tensor(ab3, ab3, ones[:, :].unsqueeze(1).to_broadcast([P, ST - HS, P - 1]), ALU.add).then_inc(S.abar_ready, 1)

        pool.wait_ge(S.consts_ready, 3)
        body(0, 0)
        with pool.Fori(1, NP2 - 2, 2) as p:
            step.enter(p, 1, start=1)
            body(p, 1)
            body(p + 1, 0)
            assert step.n == 2
            step.n = 1
            step.leave(NP2 - 2)
        body(NP2 - 1, 1)

    @block.tensor
    def _(pe):
        pe.wait_ge(S.loaded, NL)
        pe.wait_ge(S.dt_loaded, 32)
        pe.wait_ge(S.consts_ready, 3)

        def transpose_x(p):
            pe.wait_ge(S.xn_ready, 2 * p + 2)
            past(pe, S.hT_ready, p)
            for c in range(DC):
                for i in range(2):
                    last = nc.tensor.transpose(psX[:, (c * 2 + i) * P:(c * 2 + i + 1) * P],
                                               xn[:, i * D + c * P:i * D + (c + 1) * P], G.ident[:, :])
            last.then_inc(S.xT_done, 1)

        def project(p):
            pe.wait_ge(S.hT_ready, p + 1)
            past(pe, S.v_ready, p)
            for k, w in enumerate((inw, gatew)):
                for i in range(2):
                    for c in range(DC):
                        last = nc.tensor.matmul(psZ[i * SC:(i + 1) * SC, k * P:(k + 1) * P], w[:, c * SC:(c + 1) * SC],
                                                hT[:, (c * 2 + i) * P:(c * 2 + i + 1) * P], start=(c == 0), stop=(c == DC - 1))
            last.then_inc(S.z_done, 1)

        def steps(p, i):
            pe.wait_ge(S.z_ready, p + 1)
            nc.tensor.matmul(psZ[:, 2 * P:3 * P], dtw[:, :], zg[i][:, 0:P], start=True, stop=True).then_inc(S.dt_done, 1)

        def inputs(p, i):
            past(pe, S.state_used, p)
            for s in range(ST):
                last = nc.tensor.matmul(psB[:, s * P:(s + 1) * P], bdB[:, s * P:(s + 1) * P], zg[i][:, 0:P], start=True, stop=True)
            last.then_inc(S.b_done, 1)

        def outputs(p, i):
            pe.wait_ge(S.u_ready, p + 1)
            for s in range(ST):
                last = nc.tensor.matmul(psB[:, s * P:(s + 1) * P], bdC[:, s * P:(s + 1) * P], zg[i][:, 0:P], start=True, stop=True)
            last.then_inc(S.c_done, 1)

        def project_out(p):
            pe.wait_ge(S.yT_ready, p + 1)
            past(pe, S.x_ready, 2 * p)
            for i in range(2):
                last = nc.tensor.matmul(psY[i][:, 0:D], yT[i * SC:(i + 1) * SC, :], outw[i * SC:(i + 1) * SC, :],
                                        start=True, stop=True)
            last.then_inc(S.y_done, 1)

        def body(p, i, more=True):
            inputs(p, i)
            if more:
                transpose_x(p + 1)
                project(p + 1)
            outputs(p, i)
            if more:
                steps(p + 1, 1 - i)
            project_out(p)

        transpose_x(0)
        project(0)
        steps(0, 0)
        body(0, 0)
        with pe.Fori(1, NP2 - 2, 2) as p:
            body(p, 1)
            body(p + 1, 0)
        body(NP2 - 1, 1, more=False)

    @block.scalar
    def _(act):
        step = Step(act, a_step)
        act.wait_ge(S.loaded, NL)
        nc.scalar.activation(alog[:, :], alog[:, :], ACT.Exp).then_inc(S.aexp_ready, 1)

        act.wait_ge(S.zeroed, 5)
        act.wait_ge(S.consts_ready, 3)

        def body(p, i):
            act.wait_ge(S.xT_done, p + 1)
            past(act, S.z_done, p)
            for c in range(DC):
                ins = nc.scalar.activation(hT[:, c * D:(c + 1) * D], psX[:, c * D:(c + 1) * D], ACT.Copy, scale=nw[:, c:c + 1])
            ins.then_inc(S.hT_ready, 1)
            act.wait_ge(S.z_done, p + 1)
            past(act, S.yT_ready, p - 1)
            past(act, S.c_done, p - 1)
            nc.scalar.activation(zg[i][:, :], psZ[:, 0:2 * P], ACT.Copy).then_inc(S.z_ready, 1)
            act.wait_ge(S.z_ready, p + 1)
            past(act, S.dt_ready, p)
            nc.scalar.activation(eg[:, :], zg[i][:, P:2 * P], ACT.Exp, scale=-1.0).then_inc(S.gate_exp, 1)
            act.wait_ge(S.dt_done, p + 1)
            nc.scalar.activation(v[:, :], psZ[:, 2 * P:3 * P], ACT.Identity, bias=dtb[:, 0:1]).then_inc(S.v_ready, 1)
            act.wait_ge(S.abs_ready, p + 1)
            nc.scalar.activation(ev[:, :], av[:, :], ACT.Exp, scale=-1.0).then_inc(S.exp_ready, 1)
            act.wait_ge(S.exp_ready, p + 1)
            nc.scalar.activation(lv[:, :], ev[:, :], ACT.Ln, bias=1.0).then_inc(S.log_ready, 1)
            act.wait_ge(S.dt_ready, p + 1)
            past(act, S.scanned, p)
            for s in range(HS):
                ins = nc.scalar.activation(ab[:, s * P + 1:(s + 1) * P], dt[i][:, 1:], ACT.Identity, scale=Am[:, s:s + 1], bias=1.0)
            ins.then_inc(S.abar_act, 1)

        body(0, 0)
        with act.Fori(1, NP2 - 2, 2) as p:
            body(p, 1)
            body(p + 1, 0)
        body(NP2 - 1, 1)

    @block.vector
    def _(dve):
        step = Step(dve, s_step)
        dve.wait_ge(S.loaded, NL)
        dve.wait_ge(S.zeroed, 5)
        dve.wait_ge(S.aexp_ready, 1)
        for big, small in ((bdB, bp), (bdC, cp)):
            for i in range(2):
                ins = nc.vector.tensor_copy(big[:, :].rearrange("p (s r) -> p s r", s=ST)[i * SC:(i + 1) * SC, :, i * SC:(i + 1) * SC],
                                            small[i * SC:(i + 1) * SC, :].unsqueeze(2).to_broadcast([SC, ST, SC]))
            ins.then_inc(S.consts_ready, 1)
        nc.vector.tensor_scalar(Am[:, :], alog[:, :], -1.0, None, ALU.mult).then_inc(S.consts_ready, 1)

        def normalise(p):
            past(dve, S.xT_done, p)
            for i in range(2):
                b = p * 2 + i
                nc.vector.tensor_scalar(xn[:, i * D:(i + 1) * D], G.x[:, bass.ds(b * D, D)], G.rrms[:, bass.ds(b, 1)], None,
                                        ALU.mult).then_inc(S.xn_ready, 1)

        def gates(p, i):
            dve.wait_ge(S.v_ready, p + 1)
            nc.vector.scalar_tensor_tensor(av[:, :], v[:, :], -1.0, v[:, :], ALU.mult, ALU.max).then_inc(S.abs_ready, 1)
            dve.wait_ge(S.gate_exp, p + 1)
            step.do(nc.vector.tensor_scalar(rg[:, :], eg[:, :], 1.0, None, ALU.add))
            step.do(nc.vector.reciprocal(rg[:, :], rg[:, :]))
            step.sig(nc.vector.tensor_tensor(gg[i][:, :], zg[i][:, P:2 * P], rg[:, :], ALU.mult))

        def step_sizes(p, i):
            dve.wait_ge(S.log_ready, p + 1)
            nc.vector.scalar_tensor_tensor(dt[i][:, :], v[:, :], 0.0, lv[:, :], ALU.max, ALU.add).then_inc(S.dt_ready, 1)
            dve.wait_ge(S.dt_ready, p + 1)
            step.sig(nc.vector.tensor_tensor(dtz[i][:, :], dt[i][:, :], zg[i][:, 0:P], ALU.mult))

        def add_y(p):
            dve.wait_ge(S.y_done, p + 1)
            dve.wait_ge(S.summed, p + 1)
            for i in range(2):
                xb = G.x[:, bass.ds(p * (2 * D) + i * D, D)]
                nc.vector.tensor_tensor(xb, xb, psY[i][:, 0:D], ALU.add).then_inc(S.x_ready, 1)

        def body(p, i, more=True, first=False):
            if more:
                normalise(p + 1)
            step.wait()
            dve.wait_ge(S.b_done, p + 1)
            nc.vector.tensor_tensor(u[:, :].rearrange("p (s t) -> p s t", s=ST), psB[:, :].rearrange("p (s t) -> p s t", s=ST),
                                    dtz[i][:, :].unsqueeze(1).to_broadcast([P, ST, P]), ALU.mult).then_inc(S.u_ready, 1)
            if not first:
                add_y(p - 1)
            dve.wait_ge(S.u_ready, p + 1)
            dve.wait_ge(S.abar_ready, p + 1)
            dve.wait_ge(S.abar_act, p + 1)
            nc.vector.tensor_tensor_scan(st[:, :], ab[:, :], u[:, :], 0.0, ALU.mult, ALU.add).then_inc(S.scanned, 1)
            dve.wait_ge(S.scanned, p + 1)
            dve.wait_ge(S.c_done, p + 1)
            nc.vector.tensor_tensor(u[:, :], st[:, :], psB[:, :], ALU.mult).then_inc(S.state_used, 1)
            if more:
                gates(p + 1, 1 - i)
            dve.wait_ge(S.state_used, p + 1)
            step.do(nc.vector.tensor_reduce(y[:, :], u[:, :].rearrange("p (s t) -> p t s", s=ST), AX.X, ALU.add))
            nc.vector.tensor_tensor(yT[:, :], y[:, :], gg[i][:, :], ALU.mult).then_inc(S.yT_ready, 1)
            if more:
                step_sizes(p + 1, 1 - i)

        normalise(0)
        gates(0, 0)
        step_sizes(0, 0)
        body(0, 0, first=True)
        with dve.Fori(1, NP2 - 2, 2) as p:
            step.enter(p, 5, start=1)
            body(p, 1)
            body(p + 1, 0)
            assert step.n == 10
            step.n = 5
            step.leave(NP2 - 2)
        body(NP2 - 1, 1, more=False)
        add_y(NP2 - 1)
        dve.wait_ge(S.x_ready, NB)
        all_row_stats(nc, dve, step, G, st6)

    R.close()


def l1_attention(nc, G, A):
    R = Region(nc, "l1a")
    saved = R.sb("saved", [P, NB * D])
    normalise_in_place(nc, G, "l1a_ln", saved)
    rms_factors(nc, G, "l1a_rms1")
    attention16(nc, G, A, "l1a_att", "causal", "l1a_", normed="rms")
    rms_factors(nc, G, "l1a_rms2")
    selective_scan(nc, G, A, saved)
    R.close()
def wide_attention(nc, G, A):
    W = 64
    IN = H * W
    IC = IN // P
    VW = W + 1
    R = Region(nc, "l2a")
    xT = R.sb("xT", [P, DC * NB * P])
    wq, wk, wv = (R.sb(n, [P, DC * IN]) for n in ("wq", "wk", "wv"))
    wo, bo = R.sb("wo", [P, IC * D]), R.sb("bo", [1, D])
    loaded = R.sem("weights_loaded")
    loads = [(t[:, :], A["l2a_" + n]) for t, n in ((wk, "Wk"), (wq, "Wq"), (wv, "Wv"), (wo, "Wo"), (bo, "bo"))]
    NL = 16 * len(loads)
    normalised_transpose(nc, G, "l2a_n", xT, loads=loads, loaded=loaded)
    st6 = R.sb("st6", [P, 6 * NB])
    xs = R.sb("xs", [P, D])
    qk = R.sb("qk", [P, 2 * IN])
    V = R.sb("V", [P, H * VW])
    Pn, PT = R.sb("Pn", [P, H * P]), R.sb("PT", [P, H * P])
    osb, oT = R.sb("osb", [P, IN]), R.sb("oT", [P, IN])
    mx, rden = R.sb("mx", [P, H]), R.sb("rden", [P, H])
    psS, psB = R.ps("psS", [P, 2048]), R.ps("psB", [P, 2048])
    ones_ready = R.sem("ones_ready")
    xs_ready, q_done, k_done, q_ready, k_ready, s_done, v_done, v_ready = (R.sem(n) for n in (
        "xs_ready", "q_done", "k_done", "q_ready", "k_ready", "scores_done", "v_done", "v_ready"))
    shifted, p_ready, pt_done, pt_half, pt_ready = (R.sem(n) for n in ("shifted", "p_ready", "pT_done", "pT_half", "pT_ready"))
    o_done, osb_ready, ot_done, ot_ready, y_done, x_ready = (R.sem(n) for n in (
        "o_done", "o_ready", "oT_done", "oT_ready", "y_done", "x_ready"))
    s_step = R.sem("dve_step")
    block = R.block()
    last = NB - 1

    def col(h):
        return (h // 8) * 1024 + (h % 2) * 512 + (h % 8 // 2) * P

    @block.gpsimd
    def _(pool):
        def stage(b):
            past(pool, v_done, b)
            nc.gpsimd.tensor_copy(xs[:, :].rearrange("p (c t) -> p c t", c=DC),
                                  xT[:, :].rearrange("p (c n) -> p c n", c=DC)[:, :, bass.ds(b * P, P)]).then_inc(xs_ready, 1)

        stage(0)
        with pool.Fori(1, NB) as b:
            stage(b)

    @block.tensor
    def _(pe):
        pe.wait_ge(loaded, NL)
        pe.wait_ge(ones_ready, 1)

        def project_qk(b):
            past(pe, v_ready, b)
            for i, w, done in ((1, wk, k_done), (0, wq, q_done)):
                if i == 0:
                    past(pe, x_ready, b - 1)
                for j in range(IC):
                    for c in range(DC):
                        ins = nc.tensor.matmul(psB[:, i * IN + j * P:i * IN + (j + 1) * P], w[:, c * IN + j * P:c * IN + (j + 1) * P],
                                               xT[:, bass.ds(b * P + c * NB * P, P)], start=(c == 0), stop=(c == DC - 1))
                ins.then_inc(done, 1)

        def scores(b):
            pe.wait_ge(q_ready, b + 1)
            pe.wait_ge(k_ready, b + 1)
            for u in range(2):
                for g in (2 * u, 2 * u + 1):
                    nc.tensor.matmul(psS[:, g * 512:(g + 1) * 512], G.identb[:, :],
                                     G.neg_upper[:, :].unsqueeze(1).to_broadcast([P, 4, P]), start=True, stop=False)
                for h in range(8 * u, 8 * u + 8):
                    r, j = (h % 2) * W, (h // 2) * P
                    ins = nc.tensor.matmul(psS[:, col(h):col(h) + P], qk[r:r + W, j:j + P], qk[r:r + W, IN + j:IN + j + P],
                                           start=False, stop=(h // 2 % 4 == 3))
                ins.then_inc(s_done, 1)

        def transpose_o(b):
            pe.wait_ge(osb_ready, b + 1)
            for j in range(IC):
                ins = nc.tensor.transpose(psB[:, j * P:(j + 1) * P], osb[:, j * P:(j + 1) * P], G.ident[:, :])
            ins.then_inc(ot_done, 1)

        def project_v(b):
            pe.wait_ge(xs_ready, b + 1)
            for n in range(2):
                for c in range(DC):
                    ins = nc.tensor.matmul(psB[:, IN + n * 512:IN + (n + 1) * 512], xs[:, c * P:(c + 1) * P],
                                           wv[:, c * IN + n * 512:c * IN + (n + 1) * 512], start=(c == 0), stop=(c == DC - 1))
            ins.then_inc(v_done, 1)

        def project_out(b):
            pe.wait_ge(ot_ready, b + 1)
            for j in range(IC):
                nc.tensor.matmul(psB[:, 0:D], oT[:, j * P:(j + 1) * P], wo[:, j * D:(j + 1) * D], start=(j == 0), stop=False)
            nc.tensor.matmul(psB[:, 0:D], G.ones_row[:, :], bo[:, :], start=False, stop=True).then_inc(y_done, 1)

        def transpose_p(b):
            for u in range(2):
                pe.wait_ge(p_ready, 2 * b + u + 1)
                for h in range(8 * u, 8 * u + 8):
                    ins = nc.tensor.transpose(psS[:, col(h):col(h) + P], Pn[:, col(h):col(h) + P], G.ident[:, :])
                ins.then_inc(pt_done, 1)

        def weigh_values(b, more):
            pe.wait_ge(v_ready, b + 1)
            if more:
                pe.wait_ge(q_ready, b + 2)
                pe.wait_ge(k_ready, b + 2)
            else:
                pe.wait_ge(x_ready, b)
            for u in range(2):
                pe.wait_ge((pt_half, pt_ready)[u], b + 1)
                for h in range(8 * u, 8 * u + 8):
                    o = (h // 4) * 512 + (h % 4) * VW
                    ins = nc.tensor.matmul(psB[:, o:o + VW], PT[:, col(h):col(h) + P], V[:, h * VW:(h + 1) * VW], start=True, stop=True)
            ins.then_inc(o_done, 1)

        def body(b, more, first=False):
            scores(b)
            if not first:
                transpose_o(b - 1)
            project_v(b)
            if not first:
                project_out(b - 1)
            if more:
                project_qk(b + 1)
            transpose_p(b)
            weigh_values(b, more)

        project_qk(0)
        body(0, True, first=True)
        with pe.Fori(1, last) as b:
            body(b, True)
        body(last, False)
        transpose_o(last)
        project_out(last)

    @block.scalar
    def _(act):
        def take_q(b):
            act.wait_ge(q_done, b + 1)
            past(act, s_done, 2 * b)
            nc.scalar.activation(qk[:, 0:IN], psB[:, 0:IN], ACT.Copy).then_inc(q_ready, 1)

        def take_oT(b):
            act.wait_ge(ot_done, b + 1)
            past(act, y_done, b)
            nc.scalar.activation(oT[:, :], psB[:, 0:IN], ACT.Copy).then_inc(ot_ready, 1)

        def body(b, more, first=False):
            if not first:
                take_oT(b - 1)
            for u in range(2):
                act.wait_ge(shifted, 2 * b + u + 1)
                half = Pn[:, u * 1024:(u + 1) * 1024]
                nc.scalar.activation(half, half, ACT.Exp, scale=W ** -0.5).then_inc(p_ready, 1)
            act.wait_ge(v_done, b + 1)
            past(act, o_done, b)
            nc.scalar.activation(V[:, :].rearrange("p (h e) -> p h e", h=H)[:, :, 0:W],
                                 psB[:, IN:2 * IN].rearrange("p (h e) -> p h e", h=H), ACT.Copy).then_inc(v_ready, 1)
            if more:
                take_q(b + 1)
            act.wait_ge(pt_done, 2 * b + 1)
            nc.scalar.activation(PT[:, 0:1024], psS[:, 0:1024], ACT.Copy).then_inc(pt_half, 1)

        take_q(0)
        body(0, True, first=True)
        with act.Fori(1, last) as b:
            body(b, True)
        body(last, False)
        take_oT(last)

    @block.vector
    def _(dve):
        step = Step(dve, s_step)
        nc.vector.memset(V[:, :], 1.0).then_inc(ones_ready, 1)
        dve.wait_ge(ones_ready, 1)

        def take_k(b):
            dve.wait_ge(k_done, b + 1)
            past(dve, s_done, 2 * b)
            nc.vector.tensor_copy(qk[:, IN:2 * IN], psB[:, IN:2 * IN]).then_inc(k_ready, 1)

        def add_y(b):
            dve.wait_ge(y_done, b + 1)
            xb = G.x[:, bass.ds(b * D, D)]
            nc.vector.tensor_tensor(xb, xb, psB[:, 0:D], ALU.add).then_inc(x_ready, 1)

        def body(b, more, first=False):
            for u in range(2):
                us, hs = slice(u * 1024, (u + 1) * 1024), slice(u * 8, u * 8 + 8)
                S3 = psS[:, us].rearrange("p (h t) -> p h t", h=8)
                dve.wait_ge(s_done, 2 * b + u + 1)
                step.do(nc.vector.tensor_reduce(mx[:, hs], S3, AX.X, ALU.max))
                past(dve, pt_done, 2 * b)
                nc.vector.tensor_tensor(Pn[:, us].rearrange("p (h t) -> p h t", h=8), S3,
                                        mx[:, hs].unsqueeze(2).to_broadcast([P, 8, P]), ALU.subtract).then_inc(shifted, 1)
            if not first:
                add_y(b - 1)
            if more:
                take_k(b + 1)
            dve.wait_ge(pt_done, 2 * b + 2)
            past(dve, o_done, b)
            nc.vector.tensor_copy(PT[:, 1024:2048], psS[:, 1024:2048]).then_inc(pt_ready, 1)
            dve.wait_ge(o_done, b + 1)
            O4 = psB[:, :].rearrange("p (k n) -> p k n", k=4)[:, :, 0:4 * VW].rearrange("p k (h e) -> p k h e", h=4)
            step.do(nc.vector.reciprocal(rden[:, :].rearrange("p (k h) -> p k h", k=4), O4[:, :, :, W]))
            past(dve, ot_done, b)
            for k in range(4):
                ins = nc.vector.tensor_tensor(osb[:, k * 4 * W:(k + 1) * 4 * W].rearrange("p (h e) -> p h e", h=4), O4[:, k, :, 0:W],
                                              rden[:, 4 * k:4 * k + 4].unsqueeze(2).to_broadcast([P, 4, W]), ALU.mult)
            ins.then_inc(osb_ready, 1)

        take_k(0)
        body(0, True, first=True)
        with dve.Fori(1, last) as b:
            step.enter(b, 3, start=1)
            body(b, True)
            step.leave(last - 1)
        body(last, False)
        add_y(last)
        dve.wait_ge(x_ready, NB)
        all_row_stats(nc, dve, step, G, st6)

    R.close()


def memory_attention(nc, G, A):
    SCALE = 0.4 * 0.6
    R = Region(nc, "l2x")
    xT = R.sb("xT", [P, DC * NB * P])
    ctx = R.sb("ctx", [P, NB * D])
    loaded = R.sem("ctx_loaded")
    normalised_transpose(nc, G, "l2x_n", xT, loaded=loaded, loads=[
        (ctx[:, :].rearrange("p (b d) -> p b d", b=NB), A["ctx"].rearrange("b p d -> p b d"))])
    st6 = R.sb("st6", [P, 6 * NB])
    xs = R.sb("xs", [P, 2 * D])
    Pn, PT = R.sb("Pn", [P, 2 * P]), R.sb("PT", [P, 2 * P])
    mx, nmx, den, rden = (R.sb(n, [P, 2]) for n in ("mx", "nmx", "den", "rden"))
    psS, psT, psO = (R.ps(n, [P, 512]) for n in ("psS", "psT", "psO"))
    xs_ready, s_done, max_ready, p_ready, pt_done, pt_ready, o_done, x_ready = (R.sem(n) for n in (
        "xs_ready", "scores_done", "max_ready", "p_ready", "pT_done", "pT_ready", "o_done", "x_ready"))
    s_step = R.sem("dve_step")
    block = R.block()
    NP2 = NB // 2

    @block.gpsimd
    def _(pool):
        def stage(p):
            past(pool, s_done, p)
            nc.gpsimd.tensor_copy(xs[:, :].rearrange("p (c t) -> p c t", c=DC),
                                  xT[:, :].rearrange("p (c n) -> p c n", c=DC)[:, :, bass.ds(p * 2 * P, 2 * P)])\
                .then_inc(xs_ready, 1)

        stage(0)
        with pool.Fori(1, NP2) as p:
            stage(p)

    @block.tensor
    def _(pe):
        pe.wait_ge(loaded, 16)

        def body(p):
            pe.wait_ge(xs_ready, p + 1)
            past(pe, p_ready, p)
            for i in range(2):
                for c in range(DC):
                    ins = nc.tensor.matmul(psS[:, i * P:(i + 1) * P], xs[:, c * 2 * P + i * P:c * 2 * P + (i + 1) * P],
                                           G.ctxT[:, bass.ds(p * 2 * P + (c * NB + i) * P, P)], start=(c == 0), stop=(c == DC - 1))
            ins.then_inc(s_done, 1)
            pe.wait_ge(p_ready, p + 1)
            for i in range(2):
                ins = nc.tensor.transpose(psT[:, i * P:(i + 1) * P], Pn[:, i * P:(i + 1) * P], G.ident[:, :])
            ins.then_inc(pt_done, 1)
            pe.wait_ge(pt_ready, p + 1)
            past(pe, x_ready, p)
            for i in range(2):
                ins = nc.tensor.matmul(psO[:, i * D:(i + 1) * D], PT[:, i * P:(i + 1) * P], ctx[:, bass.ds(p * 2 * D + i * D, D)],
                                       start=True, stop=True)
            ins.then_inc(o_done, 1)

        body(0)
        with pe.Fori(1, NP2) as p:
            body(p)

    @block.scalar
    def _(act):
        def body(p):
            act.wait_ge(max_ready, p + 1)
            past(act, pt_done, p)
            for i in range(2):
                ins = nc.scalar.activation(Pn[:, i * P:(i + 1) * P], psS[:, i * P:(i + 1) * P], ACT.Exp, scale=SCALE,
                                           bias=nmx[:, i:i + 1], accum_out=den[:, i:i + 1])
            ins.then_inc(p_ready, 1)
            act.wait_ge(pt_done, p + 1)
            past(act, o_done, p)
            nc.scalar.activation(PT[:, :], psT[:, 0:2 * P], ACT.Copy).then_inc(pt_ready, 1)

        body(0)
        with act.Fori(1, NP2) as p:
            body(p)

    @block.vector
    def _(dve):
        step = Step(dve, s_step)
        dve.wait_ge(loaded, 16)

        def body(p):
            dve.wait_ge(s_done, p + 1)
            step.do(nc.vector.tensor_reduce(mx[:, :], psS[:, 0:2 * P].rearrange("p (i t) -> p i t", i=2), AX.X, ALU.max))
            nc.vector.tensor_scalar(nmx[:, :], mx[:, :], -SCALE, None, ALU.mult).then_inc(max_ready, 1)
            dve.wait_ge(p_ready, p + 1)
            step.do(nc.vector.reciprocal(rden[:, :], den[:, :]))
            step.do(nc.vector.tensor_scalar(rden[:, :], rden[:, :], 0.6, None, ALU.mult))
            xp, cp = G.x[:, bass.ds(p * 2 * D, 2 * D)], ctx[:, bass.ds(p * 2 * D, 2 * D)]
            step.do(nc.vector.tensor_tensor(xp, xp, cp, ALU.add))
            dve.wait_ge(o_done, p + 1)
            for i in range(2):
                xb = G.x[:, bass.ds(p * 2 * D + i * D, D)]
                ins = nc.vector.scalar_tensor_tensor(xb, psO[:, i * D:(i + 1) * D], rden[:, i:i + 1], xb, ALU.mult, ALU.add)
            ins.then_inc(x_ready, 1)

        body(0)
        with dve.Fori(1, NP2) as p:
            step.enter(p, 4, start=1)
            body(p)
            step.leave(NP2 - 1)
        dve.wait_ge(x_ready, NP2)
        all_row_stats(nc, dve, step, G, st6)

    R.close()


MAGIC = 1.5 * 2.0 ** 23
TWO_PI = float(2.0 * np.pi)


def phase_ffn(nc, G, A):
    F = 1024
    FC = F // P
    INV = 1.0 / TWO_PI
    R = Region(nc, "l2f")
    xT = R.sb("xT", [P, DC * NB * P])
    w1, w2 = R.sb("w1", [P, DC * F]), R.sb("w2", [P, FC * D])
    b1, theta, wr, wi = (R.sb(n, [P, FC]) for n in ("b1", "theta", "wr", "wi"))
    b2 = R.sb("b2", [1, D])
    loaded = R.sem("weights_loaded")
    loads = [(t[:, :], A["l2f_" + n]) for t, n in ((w1, "W1"), (b1, "b1"), (theta, "theta"), (wr, "wr"), (wi, "wi"), (b2, "b2"), (w2, "W2"))]
    NL = 16 * len(loads)
    normalised_transpose(nc, G, "l2f_n", xT, loads=loads, loaded=loaded)
    turn, tb, ang, rnd, sc, coef = R.sb("turn", [P, FC]), R.sb("tb", [P, FC]), R.sb("ang", [P, 2 * FC]), R.sb("rnd", [P, 2 * FC]), \
        R.sb("sc", [P, 2 * FC]), R.sb("coef", [P, FC])
    hb, yt, kt, ft, sn, q = ([R.sb(f"{n}{i}", [P, GT]) for i in range(2)] for n in ("hb", "yt", "kt", "ft", "sn", "q"))
    aT = R.sb("aT", [P, FC * GT])
    st6 = R.sb("st6", [P, 6 * NB])
    psH = [R.ps(f"psH{i}", [P, GT]) for i in range(4)]
    psY = [R.ps(f"psY{i}", [P, 512]) for i in range(4)]
    ang_ready, sc_ready, coef_ready = (R.sem(n) for n in (
        "angles_ready", "sin_cos_ready", "coef_ready"))
    up_done, y_ready, k_ready, f_ready, sin_ready, q_ready, a_ready, y_done, y_used = (R.sem(n) for n in (
        "up_done", "turns_ready", "rounded", "f_ready", "sin_ready", "q_ready", "act_ready", "y_done", "y_used"))
    s_step = R.sem("dve_step")
    block = R.block()

    @block.tensor
    def _(pe):
        pe.wait_ge(loaded, NL)

        def group(g):
            for j in range(FC):
                pe.wait_ge(y_ready, g * FC + j + 1)
                for c in range(DC):
                    ins = nc.tensor.matmul(psH[j % 4][:, :], w1[:, c * F + j * P:c * F + (j + 1) * P],
                                           xT[:, bass.ds(g * GT + c * NB * P, GT)], start=(c == 0), stop=(c == DC - 1))
                ins.then_inc(up_done, 1)
            pe.wait_ge(y_used, g + 1)
            for j in range(FC):
                pe.wait_ge(a_ready, g * FC + j + 1)
                for t in range(GB):
                    nc.tensor.matmul(psY[t][:, 0:D], aT[:, j * GT + t * P:j * GT + (t + 1) * P], w2[:, j * D:(j + 1) * D],
                                     start=(j == 0), stop=False)
            for t in range(GB):
                ins = nc.tensor.matmul(psY[t][:, 0:D], G.ones_row[:, :], b2[:, :], start=False, stop=True)
            ins.then_inc(y_done, 1)

        with pe.Fori(0, NG) as g:
            group(g)

    @block.scalar
    def _(act):
        act.wait_ge(ang_ready, 1)
        nc.scalar.activation(sc[:, :], ang[:, :], ACT.Sin, scale=TWO_PI).then_inc(sc_ready, 1)
        act.wait_ge(coef_ready, 1)

        def sine(n, j):
            act.wait_ge(f_ready, n + j + 1)
            nc.scalar.activation(sn[j % 2][:, :], ft[j % 2][:, :], ACT.Sin, scale=TWO_PI).then_inc(sin_ready, 1)

        with act.Fori(0, NG) as g:
            n = g * FC
            for j in range(FC):
                act.wait_ge(up_done, n + j + 1)
                act.wait_ge(q_ready, n + j + 1)
                nc.scalar.activation(hb[j % 2][:, :], psH[j % 4][:, :], ACT.Identity, bias=b1[:, j:j + 1])
                nc.scalar.activation(yt[j % 2][:, :], psH[j % 4][:, :], ACT.Identity, scale=0.1 * INV, bias=tb[:, j:j + 1])\
                    .then_inc(y_ready, 1)
                if j:
                    sine(n, j - 1)
            sine(n, FC - 1)

    @block.gpsimd
    def _(pool):
        with pool.Fori(0, NG) as g:
            for j in range(FC):
                pool.wait_ge(k_ready, g * FC + j + 1)
                nc.gpsimd.tensor_tensor(ft[j % 2][:, :], yt[j % 2][:, :], kt[j % 2][:, :], ALU.subtract).then_inc(f_ready, 1)

    @block.vector
    def _(dve):
        step = Step(dve, s_step)
        for i in range(4):
            nc.vector.memset(G.pad[:, 1 + i:2 + i], 0.0).then_inc(y_ready, 1)
        for i in range(2):
            nc.vector.memset(G.pad[:, 5 + 2 * i:6 + 2 * i], 0.0).then_inc(q_ready, 1)
        nc.vector.memset(G.pad[:, 9:10], 0.0).then_inc(y_used, 1)
        dve.wait_ge(loaded, NL)
        step.do(nc.vector.tensor_scalar(ang[:, 0:FC], theta[:, :], INV, None, ALU.mult))
        step.sig(nc.vector.tensor_scalar(ang[:, FC:], ang[:, 0:FC], 0.25, None, ALU.add))
        step.do(nc.vector.tensor_scalar(tb[:, :], b1[:, :], 0.1 * INV, None, ALU.mult))
        step.sig(nc.vector.tensor_tensor(tb[:, :], tb[:, :], ang[:, 0:FC], ALU.add))
        step.do(nc.vector.tensor_scalar(rnd[:, :], ang[:, :], MAGIC, MAGIC, ALU.add, ALU.subtract))
        nc.vector.tensor_tensor(ang[:, :], ang[:, :], rnd[:, :], ALU.subtract).then_inc(ang_ready, 1)
        dve.wait_ge(sc_ready, 1)
        step.do(nc.vector.tensor_tensor(sc[:, 0:FC], sc[:, 0:FC], wi[:, :], ALU.mult))
        step.do(nc.vector.tensor_tensor(sc[:, FC:], sc[:, FC:], wr[:, :], ALU.mult))
        step.do(nc.vector.tensor_tensor(coef[:, :], sc[:, 0:FC], sc[:, FC:], ALU.add))
        step.do(nc.vector.tensor_tensor(coef[:, :], coef[:, :], wi[:, :], ALU.mult))
        nc.vector.tensor_scalar(coef[:, :], coef[:, :], 0.1, None, ALU.mult).then_inc(coef_ready, 1)
        dve.wait_ge(coef_ready, 1)

        def combine(n, j):
            dve.wait_ge(sin_ready, n + j + 1)
            nc.vector.scalar_tensor_tensor(q[j % 2][:, :], sn[j % 2][:, :], coef[:, j:j + 1], hb[j % 2][:, :], ALU.mult, ALU.add)\
                .then_inc(q_ready, 1)
            dve.wait_ge(q_ready, n + j + 3)
            nc.vector.tensor_scalar(aT[:, j * GT:(j + 1) * GT], q[j % 2][:, :], 0.0, None, ALU.max).then_inc(a_ready, 1)

        with dve.Fori(0, NG) as g:
            n = g * FC
            for j in range(FC):
                dve.wait_ge(y_ready, n + j + 5)
                nc.vector.tensor_scalar(kt[j % 2][:, :], yt[j % 2][:, :], MAGIC, MAGIC, ALU.add, ALU.subtract).then_inc(k_ready, 1)
                if j:
                    combine(n, j - 1)
            combine(n, FC - 1)
            dve.wait_ge(y_done, g + 1)
            for t in range(GB):
                xb = G.x[:, bass.ds(g * (GB * D) + t * D, D)]
                ins = nc.vector.tensor_tensor(xb, xb, psY[t][:, 0:D], ALU.add)
            ins.then_inc(y_used, 1)
        dve.wait_ge(y_used, NG + 1)
        all_row_stats(nc, dve, step, G, st6)

    R.close()
def kernel_attention(nc, G, A):
    FQ = 3 * D
    FV = 2 * D
    NH3 = 3 * H
    STATE_SCALE = 1.0 / P ** 2
    R = Region(nc, "l3a")
    w, bias = R.sb("w", [P, DC * 5 * D]), R.sb("bias", [1, 5 * D])
    xT = R.sb("xT", [P, DC * NB * P])
    wo, bo, g, bt = R.sb("wo", [P, DC * D]), R.sb("bo", [1, D]), R.sb("ln_g", [P, DC]), R.sb("ln_b", [P, DC])
    loaded = R.sem("weights_loaded")
    loads = [(t[:, :], A["l3a_" + n]) for t, n in ((w, "w"), (bias, "bias"), (wo, "Wo"), (bo, "bo"), (g, "g"), (bt, "b"))]
    NL = 16 * len(loads)
    normalised_transpose(nc, G, "l3a_n", xT, loads=loads, loaded=loaded)
    F, VV = R.sb("F", [P, NB * FQ]), R.sb("VV", [P, NB * FV])
    ss = R.sb("ss", [P, NB * NH3])
    st6 = R.sb("st6", [P, 6 * NB])
    std, rstd = R.sb("std", [P, NB]), R.sb("rstd", [P, NB])
    diag = R.sb("diag", [P, P])
    OUT = xT

    B = Region(nc, "l3a_f")
    xs = [B.sb(f"xs{i}", [P, D]) for i in range(2)]
    sq = B.sb("sq", [P, FQ])
    ps = [B.ps(f"ps{i}", [P, 3 * 512]) for i in range(2)]
    w_ready, xs_ready, done, silu_ready, v_taken, half_ready, sq_ready, ss_ready = (B.sem(n) for n in (
        "w_ready", "xs_ready", "proj_done", "silu_ready", "v_taken", "half_ready", "sq_ready", "ss_ready"))
    block = B.block()
    @block.gpsimd
    def _(pool):
        def stage(b, i):
            past(pool, done, b - 1)
            nc.gpsimd.tensor_copy(xs[i][:, :].rearrange("p (c t) -> p c t", c=DC),
                                  xT[:, :].rearrange("p (c n) -> p c n", c=DC)[:, :, bass.ds(b * P, P)]).then_inc(xs_ready, 1)

        stage(0, 0)
        stage(1, 1)
        with pool.Fori(2, NB - 1, 2) as b:
            stage(b, 0)
            stage(b + 1, 1)

    @block.tensor
    def _(pe):
        pe.wait_ge(loaded, NL)
        pe.wait_ge(w_ready, 5 * DC)

        def project(b, i):
            pe.wait_ge(xs_ready, b + 1)
            past(pe, v_taken, b - 1)
            past(pe, silu_ready, b - 1)
            for o, n, col in ((0, D, 0), (512, 2 * D, D), (1024, 2 * D, 3 * D)):
                for c in range(DC):
                    nc.tensor.matmul(ps[i][:, o:o + n], xs[i][:, c * P:(c + 1) * P], w[:, c * 5 * D + col:c * 5 * D + col + n],
                                     start=(c == 0), stop=False)
                ins = nc.tensor.matmul(ps[i][:, o:o + n], G.ones_row[:, :], bias[:, col:col + n], start=False, stop=True)
            ins.then_inc(done, 1)

        project(0, 0)
        project(1, 1)
        with pe.Fori(2, NB - 1, 2) as b:
            project(b, 0)
            project(b + 1, 1)

    @block.scalar
    def _(act):
        def take(b, i):
            act.wait_ge(done, b + 1)
            nc.scalar.activation(F[:, bass.ds(b * FQ, D)], ps[i][:, 0:D], ACT.Silu)
            nc.scalar.activation(F[:, bass.ds(b * FQ + D, 2 * D)], ps[i][:, 512:1024], ACT.Silu).then_inc(silu_ready, 1)
            nc.scalar.activation(VV[:, bass.ds(b * FV, FV)], ps[i][:, 1024:1536], ACT.Copy).then_inc(v_taken, 1)

        with act.Fori(0, NB - 1, 2) as b:
            take(b, 0)
            take(b + 1, 1)

    @block.vector
    def _(dve):
        dve.wait_ge(loaded, NL)
        for c in range(DC):
            for k in range(5):
                wd = w[:, c * 5 * D + k * D + c * P:c * 5 * D + k * D + (c + 1) * P]
                nc.vector.tensor_tensor(wd, wd, G.ident[:, :], ALU.add).then_inc(w_ready, 1)
        nc.vector.tensor_copy(diag[:, :].rearrange("p (h e) -> p h e", h=HC), G.headmask[:, :].unsqueeze(2).to_broadcast([P, HC, HD]))
        with dve.Fori(0, NB) as b:
            dve.wait_ge(silu_ready, b + 1)
            Fb = F[:, bass.ds(b * FQ, FQ)]
            nc.vector.tensor_scalar(Fb, Fb, 0.5, None, ALU.add).then_inc(half_ready, 1)
            dve.wait_ge(half_ready, b + 1)
            nc.vector.tensor_tensor(sq[:, :], Fb, Fb, ALU.mult).then_inc(sq_ready, 1)
            dve.wait_ge(sq_ready, b + 1)
            nc.vector.tensor_reduce(ss[:, bass.ds(b * NH3, NH3)], sq[:, :].rearrange("p (h e) -> p h e", h=NH3), AX.X, ALU.add)\
                .then_inc(ss_ready, 1)
        dve.wait_ge(ss_ready, NB)

    B.close()

    B = Region(nc, "l3a_s")
    fn = B.sb("fn", [P, FQ])
    qT = B.sb("qT", [P, D])
    s0, s1 = B.sb("s0", [P, D]), B.sb("s1", [P, D])
    psQ, psS, psO = (B.ps(n, [P, 512]) for n in ("psQ", "psS", "psO"))
    root_ready, fn_ready, qt_done, qt_ready, s_done, s_ready, o_done, out_ready = (B.sem(n) for n in (
        "root_ready", "fn_ready", "qT_done", "qT_ready", "states_done", "states_ready", "o_done", "out_ready"))
    s_step = B.sem("dve_step")
    block = B.block()

    @block.tensor
    def _(pe):
        def body(b):
            pe.wait_ge(fn_ready, b + 1)
            past(pe, qt_ready, b)
            for c in range(DC):
                ins = nc.tensor.transpose(psQ[:, c * P:(c + 1) * P], fn[:, c * P:(c + 1) * P], G.ident[:, :])
            ins.then_inc(qt_done, 1)
            past(pe, s_ready, b)
            for k in range(2):
                for c in range(DC):
                    o = k * D + c * P
                    ins = nc.tensor.matmul(psS[:, o:o + P], fn[:, D + o:D + o + P], VV[:, bass.ds(b * FV + o, P)], start=True, stop=True)
            ins.then_inc(s_done, 1)
            pe.wait_ge(qt_ready, b + 1)
            pe.wait_ge(s_ready, b + 1)
            past(pe, out_ready, b)
            for c in range(DC):
                ins = nc.tensor.matmul(psO[:, c * P:(c + 1) * P], qT[:, c * P:(c + 1) * P], s1[:, c * P:(c + 1) * P], start=True, stop=True)
            ins.then_inc(o_done, 1)

        body(0)
        with pe.Fori(1, NB) as b:
            body(b)

    @block.scalar
    def _(act):
        nc.scalar.activation(ss[:, :], ss[:, :], ACT.Sqrt).then_inc(root_ready, 1)

        def body(b):
            act.wait_ge(qt_done, b + 1)
            past(act, o_done, b)
            nc.scalar.activation(qT[:, :], psQ[:, 0:D], ACT.Copy).then_inc(qt_ready, 1)
            act.wait_ge(o_done, b + 1)
            nc.scalar.activation(OUT[:, bass.ds(b * D, D)], psO[:, 0:D], ACT.Copy).then_inc(out_ready, 1)

        body(0)
        with act.Fori(1, NB) as b:
            body(b)

    @block.vector
    def _(dve):
        step = Step(dve, s_step)
        dve.wait_ge(root_ready, 1)
        step.do(nc.vector.tensor_scalar(ss[:, :], ss[:, :], 1e-6, None, ALU.add))
        step.do(nc.vector.reciprocal(ss[:, :], ss[:, :]))

        def features(b):
            past(dve, s_done, b)
            past(dve, qt_done, b)
            nc.vector.tensor_tensor(fn[:, :].rearrange("p (h e) -> p h e", h=NH3),
                                    F[:, bass.ds(b * FQ, FQ)].rearrange("p (h e) -> p h e", h=NH3),
                                    ss[:, bass.ds(b * NH3, NH3)].unsqueeze(2).to_broadcast([P, NH3, HD]), ALU.mult).then_inc(fn_ready, 1)

        def states(b):
            dve.wait_ge(s_done, b + 1)
            step.do(nc.vector.scalar_tensor_tensor(s0[:, :].rearrange("p (c n) -> p c n", c=DC),
                                                   psS[:, 0:D].rearrange("p (c n) -> p c n", c=DC), STATE_SCALE,
                                                   diag[:, :].unsqueeze(1).to_broadcast([P, DC, P]), ALU.mult, ALU.mult))
            past(dve, o_done, b)
            nc.vector.tensor_tensor(s1[:, :], s0[:, :], psS[:, D:2 * D], ALU.mult).then_inc(s_ready, 1)

        features(0)
        states(0)
        features(1)
        with dve.Fori(1, NB - 1) as b:
            step.enter(b, 1, start=1)
            states(b)
            features(b + 1)
            step.leave(NB - 2)
        states(NB - 1)
        dve.wait_ge(out_ready, NB)
        all_row_stats(nc, dve, step, G, st6, rows=OUT)

    B.close()

    B = Region(nc, "l3a_o")
    on, oT = B.sb("on", [P, D]), B.sb("oT", [P, D])
    psX, psY = B.ps("psX", [P, 512]), B.ps("psY", [P, 512])
    std_ready, on_ready, t_done, oT_ready, y_done, x_ready = (B.sem(n) for n in (
        "std_ready", "on_ready", "t_done", "oT_ready", "y_done", "x_ready"))
    s_step = B.sem("dve_step")
    block = B.block()

    @block.tensor
    def _(pe):
        def body(b):
            pe.wait_ge(on_ready, b + 1)
            past(pe, oT_ready, b)
            for c in range(DC):
                ins = nc.tensor.transpose(psX[:, c * P:(c + 1) * P], on[:, c * P:(c + 1) * P], G.ident[:, :])
            ins.then_inc(t_done, 1)
            pe.wait_ge(oT_ready, b + 1)
            past(pe, x_ready, b)
            for c in range(DC):
                nc.tensor.matmul(psY[:, 0:D], oT[:, c * P:(c + 1) * P], wo[:, c * D:(c + 1) * D], start=(c == 0), stop=False)
            nc.tensor.matmul(psY[:, 0:D], G.ones_row[:, :], bo[:, :], start=False, stop=True).then_inc(y_done, 1)

        body(0)
        with pe.Fori(1, NB) as b:
            body(b)

    @block.scalar
    def _(act):
        nc.scalar.activation(std[:, :], variances(G), ACT.Sqrt, bias=G.neg1e5[:, 0:1]).then_inc(std_ready, 1)

        def body(b):
            act.wait_ge(t_done, b + 1)
            past(act, y_done, b)
            for c in range(DC):
                ins = nc.scalar.activation(oT[:, c * P:(c + 1) * P], psX[:, c * P:(c + 1) * P], ACT.Identity,
                                           scale=g[:, c:c + 1], bias=bt[:, c:c + 1])
            ins.then_inc(oT_ready, 1)

        body(0)
        with act.Fori(1, NB) as b:
            body(b)

    @block.vector
    def _(dve):
        step = Step(dve, s_step)
        dve.wait_ge(std_ready, 1)
        step.do(nc.vector.reciprocal(rstd[:, :], std[:, :]))

        def normalise(b):
            past(dve, t_done, b)
            nc.vector.tensor_scalar(on[:, :], OUT[:, bass.ds(b * D, D)], G.mv[:, bass.ds(b * 2, 1)], rstd[:, bass.ds(b, 1)],
                                    ALU.subtract, ALU.mult).then_inc(on_ready, 1)

        def add(b):
            dve.wait_ge(y_done, b + 1)
            xb = G.x[:, bass.ds(b * D, D)]
            nc.vector.tensor_tensor(xb, xb, psY[:, 0:D], ALU.add).then_inc(x_ready, 1)

        normalise(0)
        normalise(1)
        add(0)
        with dve.Fori(1, NB - 1) as b:
            normalise(b + 1)
            add(b)
        add(NB - 1)
        dve.wait_ge(x_ready, NB)
        all_row_stats(nc, dve, step, G, st6)

    B.close()
    R.close()


def quantised_ffn(nc, G, A):
    F = 1024
    FC = F // P
    T = NB * P
    RMAX = bass.bass_isa.ReduceOp.max
    R = Region(nc, "l3f")
    xT = R.sb("xT", [P, DC * T])
    w1, w2 = R.sb("w1", [P, DC * F]), R.sb("w2", [P, FC * D])
    b1, b2 = R.sb("b1", [P, FC]), R.sb("b2", [P, D])
    loaded = R.sem("weights_loaded")
    loads = [(t[:, :], A["l3f_" + n]) for t, n in ((w1, "W1"), (w2, "W2"), (b1, "b1"), (b2, "b2"))]
    NL = 16 * len(loads)
    normalised_transpose(nc, G, "l3f_n", xT, loads=loads, loaded=loaded)
    w1q, w2q = R.sb("w1q", [P, DC * F], BF16), R.sb("w2q", [P, FC * D], BF16)
    xq = R.sb("xq", [P, DC * T], BF16)
    tmp = R.sb("tmp", [P, DC * F])
    ext, top = R.sb("ext", [P, 4]), R.sb("top", [P, 4])
    hext, htop = R.sb("hext", [P, 2]), R.sb("htop", [P, 2])
    part = R.sb("part", [P, 2 * NG * FC])
    sc = R.sb("sc", [P, 24])
    hT = R.sb("hT", [P, NG * FC * GT])
    ra, rb = ([R.sb(f"{n}{i}", [P, GT]) for i in range(2)] for n in ("ra", "rb"))
    hq = R.sb("hq", [P, FC * GT], BF16)
    yb = R.sb("yb", [P, D])
    psH = [R.ps(f"psH{i}", [P, GT]) for i in range(4)]
    psY = [R.ps(f"psY{i}", [P, 512]) for i in range(4)]
    ext_ready, top_ready, q_ready, h_done, h_ready, h_taken, hext_ready, htop_ready, s2_ready = (R.sem(n) for n in (
        "ext_ready", "top_ready", "quantised", "up_done", "gelu_ready", "range_taken", "hext_ready",
        "htop_ready", "scales_ready"))
    ra_ready, rb_ready, hq_ready, y_done, y_used = (R.sem(n) for n in ("scaled", "clipped", "hq_ready", "y_done", "y_used"))
    s_step = R.sem("dve_step")
    block = R.block()
    def s(i):
        return sc[:, i:i + 1]

    SX, ISX, LO, HI, SW1, SW2, ISW1, ISW2, S1, T0, SH, ISH, HLO, HHI, S2 = range(15)

    @block.gpsimd
    def _(pool):
        pool.wait_ge(ext_ready, 4)
        nc.gpsimd.partition_all_reduce(top[:, :], ext[:, :], P, RMAX).then_inc(top_ready, 1)
        pool.wait_ge(hext_ready, 2)
        nc.gpsimd.partition_all_reduce(htop[:, :], hext[:, :], P, RMAX).then_inc(htop_ready, 1)

    @block.tensor
    def _(pe):
        pe.wait_ge(q_ready, 3)
        with pe.Fori(0, NG) as g:
            for j in range(FC):
                pe.wait_ge(h_ready, g * FC + j + 1)
                for c in range(DC):
                    ins = nc.tensor.matmul(psH[j % 4][:, :], w1q[:, c * F + j * P:c * F + (j + 1) * P],
                                           xq[:, bass.ds(g * GT + c * T, GT)], start=(c == 0), stop=(c == DC - 1))
                ins.then_inc(h_done, 1)
        with pe.Fori(0, NG) as g:
            pe.wait_ge(y_used, g + 1)
            for j in range(FC):
                pe.wait_ge(hq_ready, g * FC + j + 1)
                for t in range(GB):
                    ins = nc.tensor.matmul(psY[t][:, 0:D], hq[:, j * GT + t * P:j * GT + (t + 1) * P], w2q[:, j * D:(j + 1) * D],
                                           start=(j == 0), stop=(j == FC - 1))
            ins.then_inc(y_done, 1)

    @block.scalar
    def _(act):
        act.wait_ge(q_ready, 3)
        with act.Fori(0, NG) as g:
            for j in range(FC):
                act.wait_ge(h_done, g * FC + j + 1)
                nc.scalar.activation(hT[:, bass.ds(g * (FC * GT) + j * GT, GT)], psH[j % 4][:, :], ACT.Gelu,
                                     scale=s(S1), bias=b1[:, j:j + 1]).then_inc(h_ready, 1)
        act.wait_ge(s2_ready, 1)

        def to_bf16(n, j):
            act.wait_ge(rb_ready, n + j + 1)
            nc.scalar.activation(hq[:, j * GT:(j + 1) * GT], rb[j % 2][:, :], ACT.Copy, bias=-MAGIC).then_inc(hq_ready, 1)

        with act.Fori(0, NG) as g:
            n = g * FC
            for j in range(FC):
                nc.scalar.activation(ra[j % 2][:, :], hT[:, bass.ds(g * (FC * GT) + j * GT, GT)], ACT.Identity,
                                     scale=s(ISH), bias=s(S2 + 1)).then_inc(ra_ready, 1)
                if j == 1:
                    act.wait_ge(y_done, g + 1)
                if j:
                    to_bf16(n, j - 1)
            to_bf16(n, FC - 1)

    @block.vector
    def _(dve):
        step = Step(dve, s_step)
        for i in range(4):
            nc.vector.memset(G.pad[:, 1 + i:2 + i], 0.0).then_inc(h_ready, 1)
        nc.vector.memset(G.pad[:, 5:6], 0.0).then_inc(y_used, 1)
        nc.vector.memset(G.pad[:, 6:7], 0.0).then_inc(y_done, 1)
        step.sig(nc.vector.memset(s(S2 + 1), MAGIC))
        nc.vector.tensor_reduce(ext[:, 0:1], xT[:, :], AX.X, ALU.max).then_inc(ext_ready, 1)
        nc.vector.tensor_reduce(ext[:, 1:2], xT[:, :], AX.X, ALU.min, negate=True).then_inc(ext_ready, 1)
        dve.wait_ge(loaded, NL)
        for k, w in enumerate((w1, w2)):
            nc.vector.tensor_reduce(ext[:, 2 + k:3 + k], w[:, :], AX.X, ALU.max, apply_absolute_value=True).then_inc(ext_ready, 1)
        dve.wait_ge(top_ready, 1)

        def affine(up, down, sx, isx, lo, hi):
            step.do(nc.vector.tensor_tensor(s(T0), up, down, ALU.add))
            step.do(nc.vector.tensor_scalar(s(sx), s(T0), 1.0 / 255.0, 1e-8, ALU.mult, ALU.max))
            step.do(nc.vector.reciprocal(s(isx), s(sx)))
            step.do(nc.vector.tensor_tensor(s(T0), down, s(isx), ALU.mult))
            step.do(nc.vector.tensor_scalar(s(T0), s(T0), MAGIC, MAGIC, ALU.add, ALU.subtract))
            step.do(nc.vector.tensor_scalar(s(T0), s(T0), -128.0, -128.0, ALU.add, ALU.max))
            step.do(nc.vector.tensor_scalar(s(T0), s(T0), 127.0, None, ALU.min))
            step.do(nc.vector.tensor_scalar(s(lo), s(T0), -1.0, -128.0, ALU.mult, ALU.add))
            step.do(nc.vector.tensor_scalar(s(hi), s(lo), MAGIC + 255.0, None, ALU.add))
            step.do(nc.vector.tensor_scalar(s(lo), s(lo), MAGIC, None, ALU.add))

        affine(top[:, 0:1], top[:, 1:2], SX, ISX, LO, HI)
        step.do(nc.vector.tensor_scalar(sc[:, SW1:SW1 + 2], top[:, 2:4], 1.0 / 127.0, 1e-8, ALU.mult, ALU.max))
        step.do(nc.vector.reciprocal(sc[:, ISW1:ISW1 + 2], sc[:, SW1:SW1 + 2]))
        step.do(nc.vector.tensor_tensor(s(S1), s(SX), s(SW1), ALU.mult))
        for w, wq_, isw in ((w1, w1q, ISW1), (w2, w2q, ISW2)):
            step.do(nc.vector.tensor_scalar(tmp[:, :], w[:, :], s(isw), MAGIC, ALU.mult, ALU.add))
            step.do(nc.vector.tensor_scalar(tmp[:, :], tmp[:, :], MAGIC + 127.0, MAGIC - 127.0, ALU.min, ALU.max))
            nc.vector.tensor_scalar(wq_[:, :], tmp[:, :], MAGIC, None, ALU.subtract).then_inc(q_ready, 1)
            dve.wait_ge(q_ready, 1)
        step.do(nc.vector.tensor_scalar(xT[:, :], xT[:, :], s(ISX), MAGIC, ALU.mult, ALU.add))
        step.do(nc.vector.tensor_scalar(xT[:, :], xT[:, :], s(LO), s(HI), ALU.max, ALU.min))
        nc.vector.tensor_scalar(xq[:, :], xT[:, :], MAGIC, None, ALU.subtract).then_inc(q_ready, 1)
        with dve.Fori(0, NG) as g:
            for j in range(FC):
                dve.wait_ge(h_ready, g * FC + j + 5)
                hc = hT[:, bass.ds(g * (FC * GT) + j * GT, GT)]
                nc.vector.tensor_reduce(part[:, bass.ds(g * FC + j, 1)], hc, AX.X, ALU.max)
                nc.vector.tensor_reduce(part[:, bass.ds(g * FC + (NG * FC + j), 1)], hc, AX.X, ALU.min).then_inc(h_taken, 1)
        dve.wait_ge(h_taken, NG * FC)
        nc.vector.tensor_reduce(hext[:, 0:1], part[:, 0:NG * FC], AX.X, ALU.max).then_inc(hext_ready, 1)
        nc.vector.tensor_reduce(hext[:, 1:2], part[:, NG * FC:], AX.X, ALU.min, negate=True).then_inc(hext_ready, 1)
        dve.wait_ge(htop_ready, 1)
        affine(htop[:, 0:1], htop[:, 1:2], SH, ISH, HLO, HHI)
        nc.vector.tensor_tensor(s(S2), s(SH), s(SW2), ALU.mult).then_inc(s2_ready, 1)
        dve.wait_ge(s2_ready, 1)

        with dve.Fori(0, NG) as g:
            n = g * FC
            for j in range(FC):
                dve.wait_ge(ra_ready, n + j + 1)
                nc.vector.tensor_scalar(rb[j % 2][:, :], ra[j % 2][:, :], s(HLO), s(HHI), ALU.max, ALU.min).then_inc(rb_ready, 1)
            dve.wait_ge(y_done, g + 2)
            step.enter(g, 2 * GB)
            for t in range(GB):
                xb = G.x[:, bass.ds(g * (GB * D) + t * D, D)]
                step.do(nc.vector.scalar_tensor_tensor(yb[:, :], psY[t][:, 0:D], s(S2), b2[:, :], ALU.mult, ALU.add))
                step.do(nc.vector.tensor_tensor(xb, xb, yb[:, :], ALU.add))
            step.leave(NG)
            nc.vector.memset(G.pad[:, 7:8], 0.0).then_inc(y_used, 1)

    R.close()
SEG = (77, 16, 35)
SEG0 = (0, 77, 93)
MAXREL = 16
NREL = SEG[0] - 1 + MAXREL


def stream_keys(nc, G, A, KD, VD, loads, att_loaded):
    IN, T = 1024, NB * P
    IC = IN // P
    seg_rows = [sum(SEG[:s]) * NB for s in range(3)]

    R = Region(nc, "l3x_kv")
    ck = R.sb("ck", [P, DC * T])
    wk = [R.sb(f"wk{s}", [P, DC * IN]) for s in range(3)]
    wv = [R.sb(f"wv{s}", [P, DC * IN]) for s in range(3)]
    KT = [R.sb(f"KT{i}", [P, GB * IN]) for i in range(2)]
    Vs = [R.sb(f"Vs{i}", [P, IN]) for i in range(2)]
    k_loaded, v_loaded = R.sem("k_weights_loaded"), R.sem("v_weights_loaded")
    suffixes = ("", "_ip", "_ap")
    normalised_transpose(nc, G, "l3x_n", G.ctxT, loaded=k_loaded, loads=[(ck[:, :], A["ctx_packed"])]
                         + [(wk[s][:, :], A["l3x_Wk" + n]) for s, n in enumerate(suffixes)])
    psK = [R.ps(f"psK{i}", [P, 512]) for i in range(4)]
    psV = [R.ps(f"psV{i}", [P, 512]) for i in range(4)]
    k_done, ka_taken, kd_taken, v_done, va_taken, vd_taken = (R.sem(n) for n in (
        "k_done", "k_taken_act", "k_taken_dve", "v_done", "v_taken_act", "v_taken_dve"))
    k_stored, v_stored = [R.sem(f"k{i}_stored") for i in range(2)], [R.sem(f"v{i}_stored") for i in range(2)]
    block = R.block()
    units = [(s, j) for s in range(3) for j in range(IC)]
    tiles = [(s, r0, min(P, NB * SEG[s] - r0)) for s in range(3) for r0 in range(0, NB * SEG[s], P)]

    def kt_view(g, s):
        return KT[g % 2][:, :].rearrange("p (b j k) -> p j b k", b=GB, j=IC)[:, :, :, SEG0[s]:SEG0[s] + SEG[s]]

    @block.sync
    def _(sp):
        for s, n in enumerate(suffixes):
            sp.dma_start(wv[s][:, :], A["l3x_Wv" + n]).then_inc(v_loaded, 16)
        for dst, src in loads:
            sp.dma_start(dst, src).then_inc(att_loaded, 16)
        for g in range(NG):
            sp.wait_ge(ka_taken, (g + 1) * len(units) // 2)
            sp.wait_ge(kd_taken, (g + 1) * len(units) // 2)
            sp.dma_start(KD[g], KT[g % 2][:, :]).then_inc(k_stored[g % 2], 16)
        for n, (s, r0, m) in enumerate(tiles):
            sp.wait_ge(va_taken, n + 1)
            sp.wait_ge(vd_taken, n + 1)
            sp.dma_start(VD[seg_rows[s] + r0:seg_rows[s] + r0 + m, :], Vs[n % 2][0:m, :]).then_inc(v_stored[n % 2], 16)
        for i in range(2):
            sp.wait_ge(k_stored[i], 16 * (NG // 2))
            sp.wait_ge(v_stored[i], 16 * ((len(tiles) + 1 - i) // 2))

    @block.tensor
    def _(pe):
        pe.wait_ge(k_loaded, 16 * 4)
        for g in range(NG):
            for n, (s, j) in enumerate(units):
                taken = ka_taken if n % 2 == 0 else kd_taken
                past(pe, taken, g * len(units) // 2 + n // 2 - 1)
                for c in range(DC):
                    o = c * T + seg_rows[s] + g * GB * SEG[s]
                    ins = nc.tensor.matmul(psK[n % 4][:, 0:GB * SEG[s]], wk[s][:, c * IN + j * P:c * IN + (j + 1) * P],
                                           ck[:, o:o + GB * SEG[s]], start=(c == 0), stop=(c == DC - 1))
                ins.then_inc(k_done, 1)
        pe.wait_ge(v_loaded, 16 * 3)
        for n, (s, r0, m) in enumerate(tiles):
            past(pe, va_taken, n - 1)
            past(pe, vd_taken, n - 1)
            for q in range(2):
                for c in range(DC):
                    o = c * T + seg_rows[s] + r0
                    ins = nc.tensor.matmul(psV[2 * (n % 2) + q][0:m, :], ck[:, o:o + m], wv[s][:, c * IN + q * 512:c * IN + (q + 1) * 512],
                                           start=(c == 0), stop=(c == DC - 1))
            ins.then_inc(v_done, 1)

    def take_keys(eng, copy, odd, taken):
        for g in range(NG):
            if g >= 2:
                eng.wait_ge(k_stored[g % 2], 16 * (g // 2))
            for n, (s, j) in enumerate(units):
                if n % 2 == odd:
                    eng.wait_ge(k_done, g * len(units) + n + 1)
                    copy(kt_view(g, s)[:, j], psK[n % 4][:, 0:GB * SEG[s]].rearrange("p (b k) -> p b k", b=GB)).then_inc(taken, 1)

    def take_values(eng, copy, q, taken):
        for n, (s, r0, m) in enumerate(tiles):
            if n >= 2:
                eng.wait_ge(v_stored[n % 2], 16 * (n // 2))
            eng.wait_ge(v_done, n + 1)
            copy(Vs[n % 2][0:m, q * 512:(q + 1) * 512], psV[2 * (n % 2) + q][0:m, :]).then_inc(taken, 1)

    @block.scalar
    def _(act):
        def copy(dst, src):
            return nc.scalar.activation(dst, src, ACT.Copy)
        take_keys(act, copy, 0, ka_taken)
        take_values(act, copy, 0, va_taken)

    @block.vector
    def _(dve):
        take_keys(dve, nc.vector.tensor_copy, 1, kd_taken)
        take_values(dve, nc.vector.tensor_copy, 1, vd_taken)

    R.close()


def stream_attention(nc, G, A):
    W, IN, T = 64, 1024, NB * P
    IC, HH = IN // P, H // 2
    GB, NG, GT = 8, NB // 8, 8 * P
    KD = nc.dram_tensor("keys", (4, P, 4 * IN), F32, kind="Internal").ap()
    VD = nc.dram_tensor("values", (T, IN), F32, kind="Internal").ap()
    seg_rows = [sum(SEG[:s]) * NB for s in range(3)]
    xT = G.ctxT
    R = Region(nc, "l3x")
    wq, wo, bo = R.sb("wq", [P, DC * IN]), R.sb("wo", [P, IC * D]), R.sb("bo", [1, D])
    rk, rv = R.sb("rel_k", [P, P - 1 + SEG[0]]), R.sb("rel_v", [SEG[0], (NREL + 1) * W])
    gates = R.sb("gates", [P, 2])
    loaded = R.sem("weights_loaded")
    loads = [(t[:, :], A["l3x_" + n]) for t, n in ((wq, "Wq"), (wo, "Wo"), (bo, "bo"), (rk, "relk"), (rv, "relv"), (gates, "gates"))]
    NL = 16 * len(loads)
    stream_keys(nc, G, A, KD, VD, loads, loaded)
    gate3 = R.sb("gate3", [P, 3])
    K, V = [R.sb(f"K{i}", [P, IN]) for i in range(2)], [R.sb(f"V{i}", [P, IN]) for i in range(2)]
    qT = R.sb("qT", [P, IC * GT])
    RP = R.sb("rel_or_weights", [P, GB * H * P])
    Pn = [R.sb(f"Pn{i}", [P, HH * P]) for i in range(3)]
    mx = [R.sb(f"mx{i}", [P, 3 * HH]) for i in range(2)]
    den = [R.sb(f"den{i}", [P, 3 * HH]) for i in range(2)]
    fac = [R.sb(f"fac{i}", [P, 3 * HH]) for i in range(3)]
    st6 = R.sb("st6", [P, 6 * NB])
    psS, psB = R.ps("psS", [P, 2048]), R.ps("psB", [P, 2048])
    gate_ready = R.sem("gates_ready")
    kv_loaded = [R.sem(f"kv{i}_loaded") for i in range(2)]
    q_done, q_taken, r_done, r0_taken, r1_taken, s_done, shifted, e_ready, f_ready, p_ready = (R.sem(n) for n in (
        "q_done", "q_taken", "rel_done", "rel0_taken", "rel1_taken", "scores_done", "shifted", "exp_ready", "factors_ready", "p_ready"))
    t_done, pt_taken, pv_done, ot_taken, w_done, w_taken, y_done, x_ready = (R.sem(n) for n in (
        "pT_done", "pT_taken", "pv_done", "o_taken", "relv_done", "relv_taken", "y_done", "x_ready"))
    s_step = R.sem("dve_step")
    block = R.block()
    RPv = RP[:, :].rearrange("p (b h i) -> p b h i", b=GB, h=H)
    qTv = qT[:, :].rearrange("p (j b i) -> p b j i", j=IC, b=GB)
    OTv = qTv
    QN = 512 // (GB * HH)
    runs = [(i0, min(QN, NREL - i0)) for i0 in range(0, NREL, QN)]
    NU = len(runs) + GB
    UN = 2 * GB
    TAIL = P - NREL

    def bank(i, n=512):
        return psB[:, i * 512:i * 512 + n]

    @block.sync
    def _(sp):
        with sp.Fori(0, NG) as g:
            for b in range(GB):
                i = b % 2
                sp.wait_ge(pv_done, g * UN + 2 * b + 2)
                sp.dma_start(K[i][:, :], KD[bass.ds(g * 2 + b // 4, 1), :, (b % 4) * IN:(b % 4 + 1) * IN].rearrange("g p n -> (g p) n"))\
                    .then_inc(kv_loaded[i], 16)
                for s in range(3):
                    sp.dma_start(V[i][SEG0[s]:SEG0[s] + SEG[s], :],
                                 VD[bass.ds(g * (GB * SEG[s]) + (seg_rows[s] + b * SEG[s]), SEG[s]), :]).then_inc(kv_loaded[i], 16)

    @block.tensor
    def _(pe):
        pe.wait_ge(loaded, NL)

        def rows(half):
            return slice(half * W, (half + 1) * W)

        def scores(g, u):
            b, half = u // 2, u % 2
            if half == 0:
                pe.wait_ge(kv_loaded[b % 2], g * (32 * GB) + 64 * (b // 2 + 1))
            if u >= 2:
                pe.wait_ge(shifted, g * (3 * UN) + 3 * (u - 1))
            for j in range(HH):
                o = half * 1024 + j * P
                nc.tensor.matmul(psS[:, o:o + P], qTv[rows(half), b, j, :], K[b % 2][rows(half), j * P:(j + 1) * P],
                                 start=True, stop=False)
                ins = nc.tensor.matmul(psS[:, o:o + SEG[0]], RPv[0:SEG[0], b, half * HH + j, :], G.ident[0:SEG[0], 0:SEG[0]],
                                       start=False, stop=True)
            ins.then_inc(s_done, 1)

        def weigh(g, u):
            b, half = u // 2, u % 2
            if u >= 1:
                pe.wait_ge(pt_taken, g * UN + u)
            pe.wait_ge(p_ready, g * (3 * UN) + 3 * (u + 1))
            for j in range(HH):
                ins = nc.tensor.transpose(psB[:, 1024 + j * P:1024 + (j + 1) * P], Pn[u % 3][:, j * P:(j + 1) * P], G.ident[:, :])
            ins.then_inc(t_done, 1)
            pe.wait_ge(pt_taken, g * UN + u + 1)
            if u >= 2:
                pe.wait_ge(ot_taken, g * UN + u - 1)
            for j in range(HH):
                h = 2 * j + half
                ins = nc.tensor.matmul(psB[rows(half), j * P:(j + 1) * P], V[b % 2][:, h * W:(h + 1) * W], RPv[:, b, half * HH + j, :],
                                       start=True, stop=True)
            ins.then_inc(pv_done, 1)

        with pe.Fori(0, NG) as g:
            for n in range(2 * IC):
                j, t = n // 2, n % 2
                if n >= 4:
                    pe.wait_ge(q_taken, g * (2 * IC) + n - 3)
                for c in range(DC):
                    ins = nc.tensor.matmul(bank(n % 4), wq[:, c * IN + j * P:c * IN + (j + 1) * P],
                                           xT[:, bass.ds(g * GT + (c * T + t * 512), 512)], start=(c == 0), stop=(c == DC - 1))
                ins.then_inc(q_done, 1)
            pe.wait_ge(q_taken, g * (2 * IC) + 2 * IC)
            for u in range(NU):
                if u >= 2:
                    pe.wait_ge(r0_taken, g * NU + u - 1)
                    pe.wait_ge(r1_taken, g * NU + u - 1)
                if u < len(runs):
                    i0, n = runs[u]
                    for i in range(i0, i0 + n):
                        for half in range(2):
                            ins = nc.tensor.matmul(bank(2 * (u % 2) + half)[0:SEG[0], (i - i0) * (GB * HH):(i - i0 + 1) * (GB * HH)],
                                                   rk[rows(half), P - 1 - i:P - 1 - i + SEG[0]], qTv[rows(half), :, :, i],
                                                   start=True, stop=True)
                else:
                    for half in range(2):
                        ins = nc.tensor.matmul(bank(2 * (u % 2) + half)[0:SEG[0], 0:HH * TAIL], rk[rows(half), 0:SEG[0]],
                                               qTv[rows(half), u - len(runs), :, NREL:], start=True, stop=True)
                ins.then_inc(r_done, 1)
            pe.wait_ge(r0_taken, g * NU + NU)
            pe.wait_ge(r1_taken, g * NU + NU)
            scores(g, 0)
            scores(g, 1)
            for u in range(UN):
                if u + 2 < UN:
                    scores(g, u + 2)
                weigh(g, u)
            pe.wait_ge(ot_taken, g * UN + UN)
            for u in range(NU):
                if u >= 4:
                    pe.wait_ge(w_taken, g * NU + u - 3)
                for i in (range(runs[u][0], sum(runs[u])) if u < len(runs) else (NREL,)):
                    for half in range(2):
                        if u < len(runs):
                            dst = bank(u % 4)[rows(half), (i - runs[u][0]) * (GB * HH):(i - runs[u][0] + 1) * (GB * HH)]
                            src = RPv[0:SEG[0], :, half * HH:(half + 1) * HH, i]
                        else:
                            dst = bank(u % 4)[rows(half), 0:HH * TAIL]
                            src = RPv[0:SEG[0], u - len(runs), half * HH:(half + 1) * HH, NREL:]
                        ins = nc.tensor.matmul(dst, rv[:, i * W:(i + 1) * W], src, start=True, stop=True)
                ins.then_inc(w_done, 1)
            pe.wait_ge(w_taken, g * NU + NU)
            for b in range(GB):
                if b >= 4:
                    pe.wait_ge(x_ready, g * GB + b - 3)
                for j in range(IC):
                    nc.tensor.matmul(bank(b % 4, D), OTv[:, b, j, :], wo[:, j * D:(j + 1) * D], start=(j == 0), stop=False)
                nc.tensor.matmul(bank(b % 4, D), G.ones_row[:, :], bo[:, :], start=False, stop=True).then_inc(y_done, 1)
            pe.wait_ge(x_ready, g * GB + GB)

    def take_rel(eng, copy, g, half, taken):
        for u in range(NU):
            eng.wait_ge(r_done, g * NU + u + 1)
            ps = bank(2 * (u % 2) + half)
            if u < len(runs):
                i0, n = runs[u]
                copy(RPv[0:SEG[0], :, half * HH:(half + 1) * HH, i0:i0 + n],
                     ps[0:SEG[0], 0:n * GB * HH].rearrange("p (i b j) -> p b j i", b=GB, j=HH)).then_inc(taken, 1)
            else:
                copy(RPv[0:SEG[0], u - len(runs), half * HH:(half + 1) * HH, NREL:],
                     ps[0:SEG[0], 0:HH * TAIL].rearrange("p (j i) -> p j i", j=HH)).then_inc(taken, 1)

    @block.scalar
    def _(act):
        act.wait_ge(loaded, NL)
        nc.scalar.activation(gates[:, :], gates[:, :], ACT.Tanh).then_inc(gate_ready, 1)

        def exps(g, u):
            act.wait_ge(shifted, g * (3 * UN) + 3 * (u + 1))
            nc.scalar.activation(Pn[u % 3][:, :], Pn[u % 3][:, :], ACT.Exp, scale=W ** -0.5).then_inc(e_ready, 1)

        def take(g, u):
            b, half = u // 2, u % 2
            act.wait_ge(t_done, g * UN + u + 1)
            nc.scalar.activation(RP[:, (b * H + half * HH) * P:(b * H + (half + 1) * HH) * P], psB[:, 1024:2048],
                                 ACT.Copy).then_inc(pt_taken, 1)
            act.wait_ge(pv_done, g * UN + u + 1 + 4)
            nc.scalar.activation(OTv[half * W:(half + 1) * W, b], psB[half * W:(half + 1) * W, 0:1024].rearrange("p (j i) -> p j i", j=IC),
                                 ACT.Copy).then_inc(ot_taken, 1)

        with act.Fori(0, NG) as g:
            for n in range(2 * IC):
                act.wait_ge(q_done, g * (2 * IC) + n + 1)
                nc.scalar.activation(qT[:, n * 512:(n + 1) * 512], bank(n % 4), ACT.Copy).then_inc(q_taken, 1)
            take_rel(act, lambda o, i: nc.scalar.activation(o, i, ACT.Copy), g, 0, r0_taken)
            exps(g, 0)
            for u in range(UN):
                if u + 1 < UN:
                    exps(g, u + 1)
                take(g, u)

    @block.gpsimd
    def _(pool):
        with pool.Fori(0, NG) as g:
            for u in range(UN):
                pool.wait_ge(f_ready, g * UN + u + 1)
                for s in range(3):
                    v = Pn[u % 3][:, :].rearrange("p (h k) -> p h k", h=HH)[:, :, SEG0[s]:SEG0[s] + SEG[s]]
                    nc.gpsimd.tensor_tensor(v, v, fac[u % 3][:, s * HH:(s + 1) * HH].unsqueeze(2).to_broadcast([P, HH, SEG[s]]), ALU.mult)\
                        .then_inc(p_ready, 1)

    @block.vector
    def _(dve):
        step = Step(dve, s_step)
        for i in range(4):
            nc.vector.memset(G.pad[:, 1 + i:2 + i], 0.0).then_inc(pv_done, 1)
        step.sig(nc.vector.memset(gate3[:, 0:1], 1.0))
        dve.wait_ge(gate_ready, 1)
        step.do(nc.vector.tensor_scalar(gate3[:, 1:3], gates[:, :], 1.0, None, ALU.add))

        def shift(g, u):
            half = u % 2
            dve.wait_ge(s_done, g * UN + u + 1)
            S3 = psS[:, half * 1024:(half + 1) * 1024].rearrange("p (h k) -> p h k", h=HH)
            P3 = Pn[u % 3][:, :].rearrange("p (h k) -> p h k", h=HH)
            for s in range(3):
                step.sig(nc.vector.tensor_reduce(mx[half][:, s * HH:(s + 1) * HH], S3[:, :, SEG0[s]:SEG0[s] + SEG[s]], AX.X, ALU.max))
            step.wait()
            for s in range(3):
                nc.vector.tensor_tensor(P3[:, :, SEG0[s]:SEG0[s] + SEG[s]], S3[:, :, SEG0[s]:SEG0[s] + SEG[s]],
                                        mx[half][:, s * HH:(s + 1) * HH].unsqueeze(2).to_broadcast([P, HH, SEG[s]]), ALU.subtract)\
                    .then_inc(shifted, 1)

        def factors(g, u):
            half = u % 2
            dve.wait_ge(e_ready, g * UN + u + 1)
            P3 = Pn[u % 3][:, :].rearrange("p (h k) -> p h k", h=HH)
            for s in range(3):
                step.sig(nc.vector.tensor_reduce(den[half][:, s * HH:(s + 1) * HH], P3[:, :, SEG0[s]:SEG0[s] + SEG[s]], AX.X, ALU.add))
            step.wait()
            step.do(nc.vector.reciprocal(den[half][:, :], den[half][:, :]))
            nc.vector.tensor_tensor(fac[u % 3][:, :].rearrange("p (s h) -> p s h", s=3), den[half][:, :].rearrange("p (s h) -> p s h", s=3),
                                    gate3[:, :].unsqueeze(2).to_broadcast([P, 3, HH]), ALU.mult).then_inc(f_ready, 1)

        with dve.Fori(0, NG) as g:
            step.enter(g, 7 * UN)
            take_rel(dve, nc.vector.tensor_copy, g, 1, r1_taken)
            shift(g, 0)
            for u in range(UN):
                if u + 1 < UN:
                    if u >= 2:
                        dve.wait_ge(t_done, g * UN + u - 1)
                    shift(g, u + 1)
                factors(g, u)
            dve.wait_ge(ot_taken, g * UN + UN)
            for u in range(NU):
                dve.wait_ge(w_done, g * NU + u + 1)
                if u < len(runs):
                    i0, n = runs[u]
                    o = OTv[:, :, :, i0:i0 + n]
                    i = bank(u % 4)[:, 0:n * GB * HH].rearrange("p (i b j) -> p b j i", b=GB, j=HH)
                else:
                    o = OTv[:, u - len(runs), :, NREL:]
                    i = bank(u % 4)[:, 0:HH * TAIL].rearrange("p (j i) -> p j i", j=HH)
                nc.vector.tensor_tensor(o, o, i, ALU.add).then_inc(w_taken, 1)
            for b in range(GB):
                dve.wait_ge(y_done, g * GB + b + 1)
                xb = G.x[:, bass.ds(g * (GB * D) + b * D, D)]
                nc.vector.tensor_tensor(xb, xb, bank(b % 4, D), ALU.add).then_inc(x_ready, 1)
            step.leave(NG)
        dve.wait_ge(x_ready, NB)
        all_row_stats(nc, dve, step, G, st6)

    R.close()
STAGES = ("l0a", "l0x", "l0f", "l1a", "l1x", "l1f", "l2a", "l2x", "l2f", "l3a", "l3x", "l3f")
SUBLAYERS = {
    "l0a": lambda nc, G, A: attention16(nc, G, A, "l0a", "linear", "l0a_", out_bias=True),
    "l0x": lambda nc, G, A: attention16(nc, G, A, "l0x", "softmax", "l0x_", cross=True, biased=True, out_bias=True),
    "l0f": lambda nc, G, A: experts(nc, G, A, "l0f", True, False),
    "l1a": l1_attention,
    "l1x": lambda nc, G, A: attention16(nc, G, A, "l1x", "relu2", "l1x_", cross=True),
    "l1f": lambda nc, G, A: experts(nc, G, A, "l1f", False, True),
}


SUBLAYERS["l2a"], SUBLAYERS["l2x"], SUBLAYERS["l2f"] = wide_attention, memory_attention, phase_ffn


SUBLAYERS["l3a"], SUBLAYERS["l3f"] = kernel_attention, quantised_ffn


SUBLAYERS["l3x"] = stream_attention


def expert(gate, up, down):
    return np.concatenate([chunks(gate), chunks(up), chunks(down)], axis=1)


def more_layout(I, A):
    I = {n: np.asarray(a) for n, a in I.items()}
    A["l0f_router"] = chunks(I["L0_ffn_router_w"].T)
    A["l0f_w"] = np.stack([expert(I["L0_ffn_w_gate"][e].T, I["L0_ffn_w_up"][e].T, I["L0_ffn_w_down"][e].T) for e in range(8)])
    twice = lambda a: np.concatenate([a, a], axis=0)
    A["l1s_in"], A["l1s_gate"] = chunks(I["L1_attn_in_w"].T), chunks(I["L1_attn_gate_w"].T)
    A["l1s_dtw"], A["l1s_dtb"] = np.ascontiguousarray(I["L1_attn_dt_w"].T), twice(I["L1_attn_dt_b"].reshape(-1, 1))
    A["l1s_out"], A["l1s_Alog"] = twice(I["L1_attn_out_w"].T), twice(I["L1_attn_A_log"])
    A["l1s_B"], A["l1s_C"] = twice(I["L1_attn_Bp_w"].T), twice(I["L1_attn_Cp_w"].T)
    A["l1s_norm"] = cols(I["L1_attn_norm2_w"])
    for n in ("Wq", "Wk", "Wv", "Wo"):
        A["l2a_" + n] = chunks(I["L2_attn_" + n])
    A["l2a_bo"] = row(I["L2_attn_bo"])
    A["ctx"] = np.ascontiguousarray(I["ctx_1024"])
    A["l2f_W1"], A["l2f_W2"] = chunks(I["L2_ffn_W1"]), chunks(I["L2_ffn_W2"])
    A["l2f_b1"], A["l2f_b2"], A["l2f_theta"] = cols(I["L2_ffn_b1"]), row(I["L2_ffn_b2"]), cols(I["L2_ffn_quantum_phases"])
    A["l2f_wr"], A["l2f_wi"] = cols(I["L2_ffn_quantum_weights_real"]), cols(I["L2_ffn_quantum_weights_imag"])
    A["l3a_w"] = chunks(np.concatenate([I["L3_attn_Wq"].T, I["L3_attn_Wk"][0].T, I["L3_attn_Wk"][1].T,
                                       I["L3_attn_Wv"][0].T, I["L3_attn_Wv"][1].T], axis=1))
    A["l3a_bias"] = row(np.concatenate([I["L3_attn_bq"], I["L3_attn_bk"].reshape(-1), I["L3_attn_bv"].reshape(-1)]))
    A["l3a_Wo"], A["l3a_bo"] = chunks(I["L3_attn_Wo"].T), row(I["L3_attn_bo"])
    A["l3a_g"], A["l3a_b"] = cols(I["L3_attn_ln_g"]), cols(I["L3_attn_ln_b"])
    A["l3f_W1"], A["l3f_W2"], A["l3f_b1"] = chunks(I["L3_ffn_W1"].T), chunks(I["L3_ffn_W2"].T), cols(I["L3_ffn_b1"])
    A["l3f_b2"] = np.ascontiguousarray(np.broadcast_to(I["L3_ffn_b2"].reshape(1, D), (P, D)))
    for n in ("Wq", "Wk", "Wv", "Wk_ip", "Wv_ip", "Wk_ap", "Wv_ap", "Wo"):
        A["l3x_" + n] = chunks(I["L3_xattn_" + n])
    A["l3x_bo"] = row(I["L3_xattn_bo"])
    ctx = I["ctx_1024"]
    A["ctx_packed"] = chunks(np.concatenate([ctx[:, a:a + n].reshape(-1, D) for a, n in zip(SEG0, SEG)]).T)
    at = np.clip(np.arange(P - 1 + SEG[0]) - (P - 1), -MAXREL, MAXREL) + MAXREL
    A["l3x_relk"] = twice(np.ascontiguousarray(I["L3_xattn_rel_k"][at].T))
    at = np.clip(np.arange(SEG[0])[:, None] - np.arange(NREL + 1)[None, :], -MAXREL, MAXREL) + MAXREL
    A["l3x_relv"] = np.ascontiguousarray(I["L3_xattn_rel_v"][at].reshape(SEG[0], -1))
    both = np.stack([I["L3_xattn_alpha"], I["L3_xattn_beta"]]).reshape(1, 2)
    A["l3x_gates"] = np.ascontiguousarray(np.broadcast_to(both, (P, 2)))
    A["l1f_router"] = chunks(I["L1_ffn_router_w"].T)
    A["l1f_rbias"] = row(I["L1_ffn_routing_bias"])
    A["l1f_w"] = np.stack([expert(I["L1_ffn_gate_w"][e], I["L1_ffn_up_w"][e], I["L1_ffn_down_w"][e]) for e in range(8)]
                          + [expert(I["L1_ffn_shared_gate"].T, I["L1_ffn_shared_up"].T, I["L1_ffn_shared_down"].T)])


def used_inputs():
    t = set(STAGES)
    names = {"x", "ctxT"}
    names |= {f"{k}_{w}" for k in t for w in ("Wq", "Wk", "Wv", "Wo", "bq", "bk", "bv", "bo", "norm", "router", "rbias", "w", "W1", "W2", "b1", "b2",
                                          "theta", "wr", "wi", "bias", "g", "b")}
    if "l0x" in t:
        names |= {"mask_bc"}
    if "l1a" in t:
        names |= {"l1s_" + n for n in ("in", "gate", "dtw", "dtb", "out", "Alog", "B", "C", "norm")}
    if "l2x" in t:
        names |= {"ctx"}
    if "l3x" in t:
        names |= {"ctx_packed"} | {"l3x_" + n for n in ("Wk_ip", "Wk_ap", "Wv_ip", "Wv_ap", "relk", "relv", "gates")}
    if "l1x" in t:
        names |= {"maskT", "nbias_bc"}
    return names
def chunks(a):
    a = np.asarray(a)
    return np.ascontiguousarray(a.reshape(-1, P, a.shape[-1]).transpose(1, 0, 2).reshape(P, -1))


def cols(a):
    return np.ascontiguousarray(np.asarray(a).reshape(-1, P).T)


def row(a):
    return np.ascontiguousarray(np.asarray(a).reshape(1, -1))


def layout(I):
    A = {"x": np.ascontiguousarray(I["x"])}
    ctx = np.asarray(I["ctx_1024"])
    A["ctxT"] = chunks(ctx.reshape(NB * P, D).T)
    m = np.ascontiguousarray(I["mask_BxS2_bf1"]).view(np.uint8).reshape(1, NB * P)
    A["mask_bc"] = np.ascontiguousarray(np.broadcast_to(m, (P, NB * P))).view(np.uint32)
    m = np.ascontiguousarray(I["mask_BxSxS2_bk0"]).view(np.uint8)
    A["maskT"] = np.ascontiguousarray(m.transpose(2, 0, 1).reshape(P, NB * P)).view(np.uint32)
    A["nbias_bc"] = np.ascontiguousarray(np.broadcast_to(np.asarray(I["L1_xattn_nbias"]).reshape(1, 1), (P, 1)))
    for n, o in (("Wq", "Wq"), ("Wk", "Wk"), ("Wv", "Wv"), ("Wp", "Wo")):
        A["l0a_" + o] = chunks(np.asarray(I["L0_attn_" + n]).T)
    A["l0a_bo"] = row(I["L0_attn_bp"])
    for n in ("Wq", "Wk", "Wv", "Wo"):
        A["l0x_" + n] = chunks(np.asarray(I["L0_xattn_" + n]).T)
    A["l0x_bq"], A["l0x_bk"] = cols(I["L0_xattn_bq"]), cols(I["L0_xattn_bk"])
    A["l0x_bv"], A["l0x_bo"] = row(I["L0_xattn_bv"]), row(I["L0_xattn_bo"])
    qkv = np.asarray(I["L1_attn_qkv_w"])
    for i, n in enumerate(("Wq", "Wk", "Wv")):
        A["l1a_" + n] = chunks(qkv[i * D:(i + 1) * D].T)
    A["l1a_Wo"] = chunks(np.asarray(I["L1_attn_o_w"]).T)
    A["l1a_norm"] = cols(I["L1_attn_norm1_w"])
    A["l1x_Wq"] = chunks(np.asarray(I["L1_xattn_Wq"]).T)
    kv = np.asarray(I["L1_xattn_Wkv"])
    A["l1x_Wk"], A["l1x_Wv"] = chunks(kv[:D].T), chunks(kv[D:].T)
    A["l1x_Wo"] = chunks(np.asarray(I["L1_xattn_Wo"]).T)
    more_layout(I, A)
    return {n: a for n, a in A.items() if n in used_inputs()}


def program(nc, A):
    G = Shared()
    with ExitStack() as ctx:
        def sb(name, shape, dt=F32):
            return ctx.enter_context(nc.sbuf_tensor(name, shape, dt))
        G.x = sb("x", [P, NB * D])
        G.mv, G.rrms = sb("mean_var", [P, 2 * NB]), sb("rrms", [P, NB])
        G.ctxT = sb("ctxT", [P, DC * NB * P])
        G.ident, G.identb = sb("ident", [P, P]), sb("identb", [P, P], BF16)
        G.triu, G.neg_upper = sb("triu", [P, P]), sb("neg_upper", [P, P], BF16)
        G.headmask = sb("headmask", [P, HC])
        G.neg1e5 = sb("ln_eps", [P, 1])
        G.pad = sb("pad", [1, 16])
        G.ones_row = sb("ones_row", [1, P])
        setup(nc, G, A)
        for sublayer in STAGES:
            SUBLAYERS[sublayer](nc, G, A)
        finish(nc, G, A)


def kernel(**inputs):
    import concourse.bacc as bacc
    from concourse.bass_utils import run_bass_kernel_spmd

    nc = bacc.Bacc("TRN2", target_bir_lowering=False, num_devices=1)
    arrays = layout(inputs)
    A = {n: nc.dram_tensor(f"in_{n}", a.shape, mybir.dt.from_np(a.dtype), kind="ExternalInput").ap()
         for n, a in arrays.items()}
    A["out"] = nc.dram_tensor("out_x", (NB, P, D), F32, kind="ExternalOutput").ap()
    program(nc, A)
    r = run_bass_kernel_spmd(nc, [{f"in_{n}": a for n, a in arrays.items()}], core_ids=[0])
    return r.results[0]["out_x"]
```
